# Optimizing a Trainium2 kernel written in Bass

```python
import numpy as np
import jax
import jax.numpy as jnp

def _softmax(x, axis=-1):
    return jax.nn.softmax(x, axis=axis)

def _gelu(x):
    return jax.nn.gelu(x, approximate=True)

def _silu(x):
    return jax.nn.silu(x)

def _sigmoid(x):
    return jax.nn.sigmoid(x)

def _layernorm(x, axis=-1, eps=1e-05):
    m = jnp.mean(x, axis=axis, keepdims=True)
    v = jnp.var(x, axis=axis, keepdims=True)
    return (x - m) / jnp.sqrt(v + eps)

def _scatter_add(tgt, idx, src, axis=0):
    return tgt.at[idx].add(src)

def _segment_sum(src, seg, n):
    return jax.ops.segment_sum(src, seg, n)
kernel_name = 'mk_gnn_resnorm_d1_gnn_r32_0cc6e7'

def setup_inputs(seed: int=0):
    np.random.seed(seed)
    _w = jnp.asarray

    def _rec_inputs():
        import jax
        import jax.numpy as jnp
        _gk = jax.random.key(seed)
        x = -0.000202 + 1 * jax.random.normal(jax.random.fold_in(_gk, 1), (50000, 128), jnp.float32)
        src = jax.random.randint(jax.random.fold_in(_gk, 2), (50000,), 0, 50000, jnp.int32)
        dst = jnp.minimum((50000 * jax.random.uniform(jax.random.fold_in(_gk, 3), (50000,)) ** 2.0).astype(jnp.int32), 49999)
        _o = jnp.argsort(dst, stable=True)
        src = src[_o]
        dst = dst[_o]
        return (x, src, dst)
    x, src, dst = _rec_inputs()

    def _L0_gnn_setup():
        import jax, jax.numpy as jnp
        import numpy as np
        N = 50000
        E = 18750
        C = 128
        M = 128
        D = 4
        EPS = 1e-05
        SLOPE = 0.2

        def _lrelu(x):
            return jnp.where(x >= 0, x, SLOPE * x)

        def _layernorm(x, g, b):
            mu = jnp.mean(x, axis=-1, keepdims=True)
            var = jnp.var(x, axis=-1, keepdims=True)
            return (x - mu) * jax.lax.rsqrt(var + EPS) * g + b
        key = jax.random.key(seed)
        ks = jax.random.split(key, 18)
        s = 0.02
        inp = {'x': jax.random.normal(ks[0], (N, C), jnp.float32), 'edge_index': jax.random.randint(ks[1], (2, E), 0, N, dtype=jnp.int32), 'eW1': jax.random.normal(ks[2], (D, 2 * C, M), jnp.float32) * s, 'eb1': jnp.zeros((D, M), jnp.float32), 'eW2': jax.random.normal(ks[3], (D, M, M), jnp.float32) * s, 'eb2': jnp.zeros((D, M), jnp.float32), 'eW3': jax.random.normal(ks[4], (D, M, M), jnp.float32) * s, 'eg': jnp.ones((D, M), jnp.float32), 'ebt': jnp.zeros((D, M), jnp.float32), 'nW1': jax.random.normal(ks[5], (D, C + M, C), jnp.float32) * s, 'nb1': jnp.zeros((D, C), jnp.float32), 'nW2': jax.random.normal(ks[6], (D, C, C), jnp.float32) * s, 'nb2': jnp.zeros((D, C), jnp.float32), 'nW3': jax.random.normal(ks[7], (D, C, C), jnp.float32) * s, 'ng': jnp.ones((D, C), jnp.float32), 'nbt': jnp.zeros((D, C), jnp.float32)}
        return inp
    _L0_gnn_all = _L0_gnn_setup()
    _L0_gnn_in = {k: v for k, v in _L0_gnn_all.items() if k in ('eW1', 'eb1', 'eW2', 'eb2', 'eW3', 'eg', 'ebt', 'nW1', 'nb1', 'nW2', 'nb2', 'nW3', 'ng', 'nbt')}
    del _L0_gnn_all
    return {'x': x, 'src': src, 'dst': dst, 'L0_gnn_eW1': _L0_gnn_in['eW1'], 'L0_gnn_eb1': _L0_gnn_in['eb1'], 'L0_gnn_eW2': _L0_gnn_in['eW2'], 'L0_gnn_eb2': _L0_gnn_in['eb2'], 'L0_gnn_eW3': _L0_gnn_in['eW3'], 'L0_gnn_eg': _L0_gnn_in['eg'], 'L0_gnn_ebt': _L0_gnn_in['ebt'], 'L0_gnn_nW1': _L0_gnn_in['nW1'], 'L0_gnn_nb1': _L0_gnn_in['nb1'], 'L0_gnn_nW2': _L0_gnn_in['nW2'], 'L0_gnn_nb2': _L0_gnn_in['nb2'], 'L0_gnn_nW3': _L0_gnn_in['nW3'], 'L0_gnn_ng': _L0_gnn_in['ng'], 'L0_gnn_nbt': _L0_gnn_in['nbt']}

def reference(x, src, dst, L0_gnn_eW1, L0_gnn_eb1, L0_gnn_eW2, L0_gnn_eb2, L0_gnn_eW3, L0_gnn_eg, L0_gnn_ebt, L0_gnn_nW1, L0_gnn_nb1, L0_gnn_nW2, L0_gnn_nb2, L0_gnn_nW3, L0_gnn_ng, L0_gnn_nbt):
    import jax
    import jax.numpy as jnp

    def _L0_gnn_ref(x, edge_index, eW1, eb1, eW2, eb2, eW3, eg, ebt, nW1, nb1, nW2, nb2, nW3, ng, nbt):
        import jax, jax.numpy as jnp
        import numpy as np
        N = 50000
        E = 18750
        C = 128
        M = 128
        D = 4
        EPS = 1e-05
        SLOPE = 0.2

        def _lrelu(x):
            return jnp.where(x >= 0, x, SLOPE * x)

        def _layernorm(x, g, b):
            mu = jnp.mean(x, axis=-1, keepdims=True)
            var = jnp.var(x, axis=-1, keepdims=True)
            return (x - mu) * jax.lax.rsqrt(var + EPS) * g + b
        src, dest = (edge_index[0], edge_index[1])
        depth = eW1.shape[0]
        n = x.shape[0]
        for i in range(depth):
            msg = jnp.concatenate((x[dest], x[src]), axis=-1)
            msg = _lrelu(msg @ eW1[i] + eb1[i])
            msg = _lrelu(msg @ eW2[i] + eb2[i])
            msg = _layernorm(msg @ eW3[i], eg[i], ebt[i])
            aggr = jax.ops.segment_sum(msg, dest, num_segments=n)
            h = jnp.concatenate((x, aggr), axis=-1)
            h = _lrelu(h @ nW1[i] + nb1[i])
            h = _lrelu(h @ nW2[i] + nb2[i])
            x = _layernorm(h @ nW3[i], ng[i], nbt[i])
        return x
    edge_index = jnp.stack([src, dst])
    x = _layernorm(x + _L0_gnn_ref(x, edge_index, L0_gnn_eW1, L0_gnn_eb1, L0_gnn_eW2, L0_gnn_eb2, L0_gnn_eW3, L0_gnn_eg, L0_gnn_ebt, L0_gnn_nW1, L0_gnn_nb1, L0_gnn_nW2, L0_gnn_nb2, L0_gnn_nW3, L0_gnn_ng, L0_gnn_nbt), axis=-1)
    return x

_drawn_inputs = setup_inputs


def setup_inputs(seed=0):
    import zlib

    import numpy as np

    out = dict(_drawn_inputs(seed))
    spreads = {'L0_gnn_eb1': (0.0, 0.1),
     'L0_gnn_eb2': (0.0, 0.1),
     'L0_gnn_eg': (1.0, 0.2),
     'L0_gnn_ebt': (0.0, 0.29),
     'L0_gnn_nb1': (0.0, 0.1),
     'L0_gnn_nb2': (0.0, 0.1),
     'L0_gnn_ng': (1.0, 0.2),
     'L0_gnn_nbt': (0.0, 0.1)}
    factors = {}
    for name, (base, spread) in spreads.items():
        noise = np.random.default_rng([zlib.crc32(name.encode()), seed]).standard_normal(out[name].shape)
        drawn = base * np.exp(spread * noise) if base else spread * noise
        out[name] = jnp.asarray(drawn.astype(out[name].dtype))
    for name, factor in factors.items():
        out[name] = (out[name] * factor).astype(out[name].dtype)
    return out
```

```python
from contextlib import ExitStack

import concourse.bass as bass
from concourse import mybir
from concourse.alu_op_type import AluOpType as ALU

ACT = mybir.ActivationFunctionType
F32 = mybir.dt.float32
BF16 = mybir.dt.bfloat16
I32 = mybir.dt.int32
AX = mybir.AxisListType

P = 128
TILES = 4
GROUP = P * TILES
SLOTS = 2
EPS = 1e-5
SLOPE = 0.2
SKIP = 1 << 20
DMA = 16
EB1, EB2, EG, EBT, NB1, NB2, XG, XB = range(8)
VECS = 8
EW1_DST, EW1_SRC, EW2, EW3, NW1_X, NW1_AGG, NW2, NW3 = range(8)


def done(k):
    return k + 1 + SLOTS


def free(k):
    return k + 1


def gnn_kernel(nc, x, src, dst, eW1, eb1, eW2, eb2, eW3, eg, ebt, nW1, nb1, nW2, nb2, nW3, ng, nbt, out):
    N, C = x.shape
    E = src.shape[0]
    L = eW2.shape[0]
    assert C == P
    GE = -(-E // (SLOTS * GROUP)) * SLOTS
    GN = -(-N // (SLOTS * GROUP)) * SLOTS
    EP, NP = GE * GROUP, GN * GROUP
    PAIRS_E, PAIRS_N = GE // SLOTS, GN // SLOTS
    NT = EP // P
    assert GE <= P and EP < SKIP and NP < SKIP and NP > N
    LAST_ROWS = N - (GN - 1) * GROUP
    assert 0 < LAST_ROWS and LAST_ROWS % TILES == 0
    CHUNKS = next(c for c in range(6, NT + 1) if NT % c == 0)
    CW = EP // CHUNKS
    CT = NT // CHUNKS

    x_state = nc.dram_tensor("x_state", [NP, C], F32, kind="Internal").ap()
    agg = nc.dram_tensor("agg", [NP, C], F32, kind="Internal").ap()
    dst_sorted = nc.dram_tensor("dst_sorted", [EP + 2, 1], I32, kind="Internal").ap()
    src_sorted = nc.dram_tensor("src_sorted", [EP + 2, 1], I32, kind="Internal").ap()
    cont_dram = nc.dram_tensor("cont_dram", [GE, GROUP], BF16, kind="Internal").ap()

    x_groups = x_state.rearrange("(g p t) c -> g p (t c)", p=P, t=TILES)
    agg_groups = agg.rearrange("(g p t) c -> g p (t c)", p=P, t=TILES)
    x_in_groups = x[0:(GN - 1) * GROUP, :].rearrange("(g p t) c -> g p (t c)", p=P, t=TILES)
    out_groups = out[0:(GN - 1) * GROUP, :].rearrange("(g p t) c -> g p (t c)", p=P, t=TILES)
    LAST_P = LAST_ROWS // TILES
    x_in_last = x[(GN - 1) * GROUP:N, :].rearrange("(p t) c -> p (t c)", t=TILES)
    out_last = out[(GN - 1) * GROUP:N, :].rearrange("(p t) c -> p (t c)", t=TILES)

    with ExitStack() as ctx:
        def sb(name, shape, dt=F32):
            return ctx.enter_context(nc.sbuf_tensor(name, shape, dt))

        def sem(name):
            return ctx.enter_context(nc.semaphore(name))

        ident = sb("ident", [P, P])
        mean_w = sb("mean_w", [P, P])
        below = sb("below", [P, P])
        eps_col = sb("eps_col", [P, 1])
        ones_col = sb("ones_col", [P, 1])
        zeros = sb("zeros", [P, C])
        pad_vals = sb("pad_vals", [1, GROUP], I32)
        pad_ends = sb("pad_ends", [1, 1], I32)
        vec_rows = sb("vec_rows", [L * VECS, C])
        vecs_all = sb("vecs_all", [P, L * VECS])
        vecs = sb("vecs", [P, VECS])
        W = sb("W", [P, 8, C])
        W3c = sb("W3c", [P, 2, C])
        w3_mean = sb("w3_mean", [P, 2])
        gain_all = sb("gain_all", [P, C])
        shift_all = sb("shift_all", [P, C])
        e_now = sb("e_now", [P, GROUP], I32)
        e_prev = sb("e_prev", [P, GROUP], I32)
        e_next = sb("e_next", [P, GROUP], I32)
        e_src = sb("e_src", [P, GROUP], I32)
        e_tab = sb("e_tab", [P, 3, GROUP])
        e_cont = sb("e_cont", [P, GROUP], BF16)
        disorder = sb("disorder", [P, 1])
        unsorted = sb("unsorted", [1, 1], I32)
        idx_all = sb("idx_all", [P, GE, 3 * TILES], I32)
        cont_all = sb("cont_all", [P, EP], BF16)
        src_rows = sb("src_rows", [P, SLOTS, TILES, C])
        dst_rows = sb("dst_rows", [P, SLOTS, TILES, C])
        gather_idx = sb("gather_idx", [P, SLOTS, 2 * TILES], I32)
        scatter_idx = sb("scatter_idx", [P, SLOTS, TILES], I32)
        srcT = sb("srcT", [P, SLOTS, GROUP])
        dstT = sb("dstT", [P, SLOTS, GROUP])
        eh1 = sb("eh1", [P, SLOTS, GROUP])
        eh2 = sb("eh2", [P, SLOTS, GROUP])
        esq = sb("esq", [P, SLOTS, GROUP])
        ersd = sb("ersd", [P, SLOTS, GROUP])
        msg = sb("msg", [P, SLOTS, GROUP])
        seg = sb("seg", [P, SLOTS, GROUP])
        seg_rows = sb("seg_rows", [P, SLOTS, TILES, C])
        x_rows = sb("x_rows", [P, SLOTS, TILES, C])
        a_rows = sb("a_rows", [P, SLOTS, TILES, C])
        xT = sb("xT", [P, SLOTS, GROUP])
        aT = sb("aT", [P, SLOTS, GROUP])
        nh1 = sb("nh1", [P, SLOTS, GROUP])
        nh2 = sb("nh2", [P, SLOTS, GROUP])
        nsq = sb("nsq", [P, SLOTS, TILES, C])
        new_rows = sb("new_rows", [P, SLOTS, TILES, C])
        nss = sb("nss", [P, SLOTS, TILES])
        nrs = sb("nrs", [P, SLOTS, TILES])
        fmean = sb("fmean", [P, SLOTS, TILES])

        banks = [[ctx.enter_context(nc.psum_tensor(f"bank{u}{b}", [P, GROUP], F32)) for b in range(4)]
                 for u in range(SLOTS)]

        s_const = sem("const_made")
        s_cst2 = sem("columns_made")
        passed = {e: sem(f"{e}_passed") for e in ("sp", "pool", "pe", "act", "dve")}
        s_pads = sem("pads_made")
        s_raw = sem("edges_copied")
        s_check = sem("check_loaded")
        s_dis = sem("disorder_counted")
        s_dsum = sem("disorder_summed")
        s_flag = sem("flag_made")
        s_edges = sem("edges_loaded")
        s_tab = sem("tables_made")
        s_cont = sem("cont_made")
        s_cdram = sem("cont_in_dram")
        s_call = sem("cont_spread")
        s_tabT = sem("tables_turned")
        s_idx = sem("idx_made")
        s_vrow = sem("vec_rows_set")
        s_vload = sem("vec_rows_loaded")
        s_vT = sem("vecs_turned")
        s_vall = sem("vecs_all_made")
        s_xinit = sem("x_state_filled")
        s_azero = sem("agg_zeroed")
        s_gb = sem("gain_shift_loaded")
        q_cols = sem("sort_columns_loaded")
        q_chunk = sem("sort_chunk_loaded")
        q_conv = sem("sort_chunk_converted")
        q_used = sem("sort_chunk_used")
        q_step = sem("sort_step")
        q_count = sem("sort_tiles_counted")
        q_rank = sem("sort_ranks_made")
        q_copy = sem("sort_staged")
        q_put = sem("sort_scattered")
        s_wload = sem("weights_loaded")
        s_wmean = sem("w3_means")
        s_wts = sem("weights_ready")
        s_gidx = sem("gather_idx_staged")
        s_sidx = sem("scatter_idx_staged")
        s_src = [sem(f"src_rows_gathered{u}") for u in range(SLOTS)]
        s_dst = [sem(f"dst_rows_gathered{u}") for u in range(SLOTS)]
        s_scat = [sem(f"seg_rows_scattered{u}") for u in range(SLOTS)]
        e_srcP = sem("src_turned")
        e_dstP = sem("dst_turned")
        e_srcT = sem("src_scaled")
        e_dstT = sem("dst_scaled")
        e_h1P = sem("e_h1_product")
        e_h1b = sem("e_h1_biased")
        e_h1 = sem("e_h1_ready")
        e_h2P = sem("e_h2_product")
        e_h2b = sem("e_h2_biased")
        e_h2 = sem("e_h2_ready")
        e_h3P = sem("e_h3_product")
        e_sq = sem("e_squares")
        e_varP = sem("e_variance")
        e_sd = sem("e_deviation")
        e_rsd = sem("e_rsd")
        e_nrm = sem("e_normed")
        e_msg = sem("e_message")
        e_seg = sem("e_running_sum")
        e_segP = sem("e_sum_turned")
        e_out = sem("e_sum_rows")
        s_x = [sem(f"x_rows_loaded{u}") for u in range(SLOTS)]
        s_a = [sem(f"a_rows_loaded{u}") for u in range(SLOTS)]
        s_st = [sem(f"new_rows_stored{u}") for u in range(SLOTS)]
        n_xP = sem("x_turned")
        n_aP = sem("a_turned")
        n_xT = sem("x_scaled")
        n_aT = sem("a_copied")
        n_h1P = sem("n_h1_product")
        n_h1b = sem("n_h1_biased")
        n_h1 = sem("n_h1_ready")
        n_h2P = sem("n_h2_product")
        n_h2b = sem("n_h2_biased")
        n_h2 = sem("n_h2_ready")
        n_h3P = sem("n_h3_product")
        n_sq = sem("n_squares")
        n_ss = sem("n_square_sums")
        n_sd = sem("n_deviation")
        n_rs = sem("n_rsd")
        n_new = sem("n_new_rows")
        f_x = [sem(f"f_x_loaded{u}") for u in range(SLOTS)]
        f_r = [sem(f"f_residual_loaded{u}") for u in range(SLOTS)]
        f_st = [sem(f"f_out_stored{u}") for u in range(SLOTS)]
        f_sh = sem("f_shifted")
        f_ga = sem("f_gained")
        f_y = sem("f_summed")
        f_mean = sem("f_mean")
        f_c = sem("f_centred")
        f_sq = sem("f_squares")
        f_ss = sem("f_square_sums")
        f_sd = sem("f_deviation")
        f_rs = sem("f_rsd")
        f_new = sem("f_rows")

        block = ctx.enter_context(nc.Block())

        sort_room = cont_all[:, :].bitcast(F32)
        chunk_f = sort_room[:, 0:CW]
        chunk_i = sort_room[:, CW:2 * CW].bitcast(I32)
        chunk_junk = sort_room[:, 2 * CW:3 * CW]
        flat = [b[:, :, :].rearrange("p s f -> p (s f)") for b in (srcT, dstT, eh1, eh2, esq, ersd)]
        assert NT <= SLOTS * GROUP and CHUNKS <= 8
        dcol_f, dcol_i, scol_i = flat[0][:, 0:NT], flat[1][:, 0:NT].bitcast(I32), flat[2][:, 0:NT].bitcast(I32)
        tie, rank_f, rank_i = flat[3][:, 0:NT], flat[4][:, 0:NT], flat[5][:, 0:NT].bitcast(I32)
        equal, equal_junk = msg[:, 0, 0:P], msg[:, 1, 0:P]
        cnt_lo = x_rows[:, :, :, :].rearrange("p s t c -> p (s t c)")
        cnt_hi = a_rows[:, :, :, :].rearrange("p s t c -> p (s t c)")
        PER = SLOTS * GROUP // NT

        def less(c):
            room = [cnt_lo, cnt_hi, xT[:, :, :].rearrange("p s f -> p (s f)"), aT[:, :, :].rearrange("p s f -> p (s f)"),
                    nh1[:, :, :].rearrange("p s f -> p (s f)")]
            return room[c // PER][:, (c % PER) * NT:(c % PER + 1) * NT]

        st_rank, st_dst, st_src = scatter_idx[:, 0, 0:1], scatter_idx[:, 0, 1:2], scatter_idx[:, 0, 2:3]

        def edge_rows(a, shift):
            return a[shift:shift + EP, :].rearrange("(g f) o -> g (f o)", f=GROUP)

        @block.sync
        def _(sp):
            sp.wait_ge(s_pads, 2)
            sp.dma_start(dst_sorted[1:1 + E, :].rearrange("(a e) o -> a (e o)", a=16), dst.rearrange("(a e) -> a e", a=16)).then_inc(s_raw, DMA)
            sp.dma_start(src_sorted[1:1 + E, :].rearrange("(a e) o -> a (e o)", a=16), src.rearrange("(a e) -> a e", a=16)).then_inc(s_raw, DMA)
            raw = 2
            for a in (dst_sorted, src_sorted):
                for at in range(1 + E, 1 + EP, GROUP):
                    n = min(GROUP, 1 + EP - at)
                    sp.dma_start(a[at:at + n, :].rearrange("(a n) o -> a (n o)", a=1), pad_vals[0:1, 0:n]).then_inc(s_raw, DMA)
                    raw += 1
                for at in (0, EP + 1):
                    sp.dma_start(a[at:at + 1, :], pad_ends[0:1, 0:1]).then_inc(s_raw, DMA)
                    raw += 1
            sp.dma_start(gain_all[:, :], ng[L - 1:L, :].to_broadcast([P, C])).then_inc(s_gb, DMA)
            sp.dma_start(shift_all[:, :], nbt[L - 1:L, :].to_broadcast([P, C])).then_inc(s_gb, DMA)
            sp.wait_ge(s_vrow, 1)
            sp.wait_ge(s_const, 5)
            nv = 0
            for k, v in ((EB1, eb1), (EB2, eb2), (EG, eg), (EBT, ebt), (NB1, nb1), (NB2, nb2)):
                sp.dma_start(vec_rows[k:L * VECS:VECS, :], v).then_inc(s_vload, DMA)
                nv += 1
            for k, v in ((XG, ng), (XB, nbt)):
                if L > 1:
                    sp.dma_start(vec_rows[VECS + k:L * VECS:VECS, :], v[0:L - 1, :]).then_inc(s_vload, DMA)
                    nv += 1
            sp.dma_start(vec_rows[XB:XB + 1, :], zeros[0:1, :]).then_inc(s_vload, DMA)
            sp.wait_ge(s_raw, DMA * raw)
            sp.dma_start(e_now[0:GE, :], edge_rows(dst_sorted, 1)).then_inc(s_check, DMA)
            sp.dma_start(e_prev[0:GE, :], edge_rows(dst_sorted, 0)).then_inc(s_check, DMA)
            sp.dma_start(x_state[0:N, :], x).then_inc(s_xinit, DMA)
            pad_rows = NP - N
            sp.dma_start(x_state[N:NP, :].rearrange("(p r) c -> p r c", p=16), zeros[0:16, None, :].to_broadcast([16, pad_rows // 16, C])).then_inc(s_xinit, DMA)
            sp.wait_ge(s_flag, 1)
            is_unsorted = sp.value_load(unsorted[0:1, 0:1], min_val=0, max_val=1)
            with sp.If(is_unsorted != 0):
                with nc.allow_non_contiguous_dma("the sort's columns; a path seldom taken"):
                    sp.dma_start(dcol_i, dst_sorted[1:1 + EP, :].rearrange("(j p) o -> p (j o)", p=P)).then_inc(q_cols, DMA)
                    sp.dma_start(scol_i, src_sorted[1:1 + EP, :].rearrange("(j p) o -> p (j o)", p=P)).then_inc(q_cols, DMA)
                for c in range(CHUNKS):
                    if c:
                        sp.wait_ge(q_conv, c)
                    row = dst_sorted[1 + c * CW:1 + (c + 1) * CW, :].rearrange("(a n) o -> a (n o)", a=1)
                    sp.dma_start(chunk_i, row.to_broadcast([P, CW])).then_inc(q_chunk, DMA)
                sp.wait_ge(q_put, 2 * DMA * NT)
            with sp.Else():
                sp.nop()
            sp.wait_ge(s_dis, 2)
            sp.dma_start(e_now[0:GE, :], edge_rows(dst_sorted, 1)).then_inc(s_edges, DMA)
            sp.dma_start(e_prev[0:GE, :], edge_rows(dst_sorted, 0)).then_inc(s_edges, DMA)
            sp.dma_start(e_next[0:GE, :], edge_rows(dst_sorted, 2)).then_inc(s_edges, DMA)
            sp.dma_start(e_src[0:GE, :], edge_rows(src_sorted, 1)).then_inc(s_edges, DMA)
            sp.wait_ge(s_cont, 1)
            sp.dma_start(cont_dram, e_cont[0:GE, :]).then_inc(s_cdram, DMA)
            sp.wait_ge(s_cdram, DMA)
            sp.dma_start(cont_all[:, :], cont_dram.rearrange("(a g) f -> a (g f)", a=1).to_broadcast([P, EP])).then_inc(s_call, DMA)

            with sp.Fori(0, L) as l:
                sp.wait_ge(n_h3P, l * GN + SLOTS)
                sp.wait_ge(s_const, 1)
                for k, w in ((EW2, eW2), (EW3, eW3), (NW2, nW2), (NW3, nW3)):
                    sp.dma_start(W[:, k, :], w[bass.ds(l, 1), :, :].rearrange("a p c -> p (a c)")).then_inc(s_wload, DMA)
                for k, w in ((EW1_DST, eW1), (NW1_X, nW1)):
                    sp.dma_start(W[:, k:k + 2, :], w[bass.ds(l, 1), :, :].rearrange("a (h p) c -> p (a h) c", p=P)).then_inc(s_wload, DMA)
                for u in range(SLOTS):
                    sp.wait_ge(s_scat[u], (l + 1) * (PAIRS_E * TILES * DMA))
                sp.sem_inc(passed["sp"], 1)

                def load(i):
                    for u in range(SLOTS):
                        k = l * GN + i * SLOTS + u
                        g = i * SLOTS + u
                        sp.wait_ge(n_xP, free(k))
                        sp.dma_start(x_rows[:, u, :, :].rearrange("p t c -> p (t c)"), x_groups[bass.ds(g, 1), :, :].rearrange("a p f -> p (a f)")).then_inc(s_x[u], DMA)
                        sp.wait_ge(n_aP, free(k))
                        sp.dma_start(a_rows[:, u, :, :].rearrange("p t c -> p (t c)"), agg_groups[bass.ds(g, 1), :, :].rearrange("a p f -> p (a f)")).then_inc(s_a[u], DMA)

                def store(i):
                    for u in range(SLOTS):
                        k = l * GN + i * SLOTS + u
                        g = i * SLOTS + u
                        sp.wait_ge(n_new, done(k))
                        sp.dma_start(x_groups[bass.ds(g, 1), :, :].rearrange("a p f -> p (a f)"), new_rows[:, u, :, :].rearrange("p t c -> p (t c)")).then_inc(s_st[u], DMA)

                load(0)
                with sp.Fori(1, PAIRS_N) as i:
                    load(i)
                    store(i - 1)
                store(PAIRS_N - 1)

            for u in range(SLOTS):
                sp.wait_ge(s_st[u], L * PAIRS_N * DMA)

            def f_load(i, last=False):
                for u in range(SLOTS):
                    g = i * SLOTS + u
                    sp.wait_ge(f_new, free(g))
                    part = last and u == SLOTS - 1
                    sp.dma_start(x_rows[:, u, :, :].rearrange("p t c -> p (t c)"), x_groups[bass.ds(g, 1), :, :].rearrange("a p f -> p (a f)")).then_inc(f_x[u], DMA)
                    if part:
                        sp.dma_start(a_rows[0:LAST_P, u, :, :].rearrange("p t c -> p (t c)"), x_in_last).then_inc(f_r[u], DMA)
                    else:
                        sp.dma_start(a_rows[:, u, :, :].rearrange("p t c -> p (t c)"), x_in_groups[bass.ds(g, 1), :, :].rearrange("a p f -> p (a f)")).then_inc(f_r[u], DMA)

            def f_store(i, last=False):
                for u in range(SLOTS):
                    g = i * SLOTS + u
                    sp.wait_ge(f_new, done(g))
                    if last and u == SLOTS - 1:
                        sp.dma_start(out_last, new_rows[0:LAST_P, u, :, :].rearrange("p t c -> p (t c)")).then_inc(f_st[u], DMA)
                    else:
                        sp.dma_start(out_groups[bass.ds(g, 1), :, :].rearrange("a p f -> p (a f)"), new_rows[:, u, :, :].rearrange("p t c -> p (t c)")).then_inc(f_st[u], DMA)

            f_load(0)
            with sp.Fori(1, PAIRS_N - 1) as i:
                f_load(i)
                f_store(i - 1)
            f_load(PAIRS_N - 1, last=True)
            f_store(PAIRS_N - 2)
            f_store(PAIRS_N - 1, last=True)
            for u in range(SLOTS):
                sp.wait_ge(f_st[u], PAIRS_N * DMA)

        @block.gpsimd
        def _(pool):
            pool.sem_inc(f_sh, SLOTS)
            nc.gpsimd.memset(pad_vals[:, :], NP - 1).then_inc(s_pads, 1)
            nc.gpsimd.memset(pad_ends[:, :], -1).then_inc(s_pads, 1)
            nc.gpsimd.memset(ident[:, :], 0.0).then_inc(s_const, 1)
            nc.gpsimd.memset(below[:, :], 1.0).then_inc(s_const, 1)
            pool.wait_ge(s_const, 2)
            nc.gpsimd.affine_select(out=ident[:, :], in_=ident[:, :], compare_op=ALU.not_equal, fill=1.0, base=0,
                                    pattern=[[-1, P]], channel_multiplier=1).then_inc(s_const, 1)
            nc.gpsimd.affine_select(out=below[:, :], in_=below[:, :], compare_op=ALU.is_gt, fill=0.0, base=0,
                                    pattern=[[-1, P]], channel_multiplier=1).then_inc(s_const, 1)
            nc.gpsimd.memset(zeros[:, :], 0.0).then_inc(s_const, 1)
            pool.wait_ge(s_flag, 1)
            is_unsorted = pool.value_load(unsorted[0:1, 0:1], min_val=0, max_val=1)
            with pool.If(is_unsorted != 0):
                pool.wait_ge(q_rank, 1)
                with pool.Fori(0, NT) as j:
                    pool.wait_ge(q_put, j * (2 * DMA))
                    pool.sem_inc(passed["pool"], 1)
                    nc.gpsimd.tensor_copy(st_rank, rank_i[:, bass.ds(j, 1)]).then_inc(q_copy, 1)
                    nc.gpsimd.tensor_copy(st_dst, dcol_i[:, bass.ds(j, 1)]).then_inc(q_copy, 1)
                    nc.gpsimd.tensor_copy(st_src, scol_i[:, bass.ds(j, 1)]).then_inc(q_copy, 1)
                    pool.wait_ge(q_copy, j * 3 + 3)
                    pool.sem_inc(passed["pool"], 1)
                    nc.gpsimd.indirect_dma_start(dst_sorted, bass.IndirectOffsetOnAxis(st_rank, 0), st_dst, None).then_inc(q_put, DMA)
                    nc.gpsimd.indirect_dma_start(src_sorted, bass.IndirectOffsetOnAxis(st_rank, 0), st_src, None).then_inc(q_put, DMA)
            with pool.Else():
                pool.nop()

            pool.wait_ge(s_idx, 3)
            pool.wait_ge(s_xinit, 2 * DMA)
            pool.wait_ge(s_azero, DMA)
            with pool.Fori(0, L) as l:
                for u in range(SLOTS):
                    pool.wait_ge(s_st[u], l * (PAIRS_N * DMA))
                pool.sem_inc(passed["pool"], 1)

                def gather(i):
                    pair = l * PAIRS_E + i
                    for u in range(SLOTS):
                        k = pair * SLOTS + u
                        pool.wait_ge(s_src[u], pair * (TILES * DMA))
                        pool.wait_ge(s_dst[u], pair * (TILES * DMA))
                        pool.sem_inc(passed["pool"], 1)
                        nc.gpsimd.tensor_copy(gather_idx[:, u, :], idx_all[:, bass.ds(i * SLOTS + u, 1), 0:2 * TILES].rearrange("p a f -> p (a f)")).then_inc(s_gidx, 1)
                    for u in range(SLOTS):
                        k = pair * SLOTS + u
                        pool.wait_ge(s_gidx, k + 1)
                        for kind, rows, ready, used in ((0, src_rows, s_src, e_srcP), (1, dst_rows, s_dst, e_dstP)):
                            pool.wait_ge(used, free(k))
                            pool.sem_inc(passed["pool"], 1)
                            for t in range(TILES):
                                nc.gpsimd.indirect_dma_start(rows[:, u, t, :], None, x_state, bass.IndirectOffsetOnAxis(gather_idx[:, u, kind * TILES + t:kind * TILES + t + 1], 0)).then_inc(ready[u], DMA)

                def scatter(i):
                    pair = l * PAIRS_E + i
                    for u in range(SLOTS):
                        pool.wait_ge(s_scat[u], pair * (TILES * DMA))
                        pool.sem_inc(passed["pool"], 1)
                        nc.gpsimd.tensor_copy(scatter_idx[:, u, :], idx_all[:, bass.ds(i * SLOTS + u, 1), 2 * TILES:3 * TILES].rearrange("p a f -> p (a f)")).then_inc(s_sidx, 1)
                    for u in range(SLOTS):
                        k = pair * SLOTS + u
                        pool.wait_ge(s_sidx, k + 1)
                        pool.wait_ge(e_out, done(k))
                        pool.sem_inc(passed["pool"], 1)
                        for t in range(TILES):
                            nc.gpsimd.indirect_dma_start(agg, bass.IndirectOffsetOnAxis(scatter_idx[:, u, t:t + 1], 0), seg_rows[:, u, t, :], None,
                                                         bounds_check=NP - 1, oob_is_err=False).then_inc(s_scat[u], DMA)

                gather(0)
                with pool.Fori(1, PAIRS_E) as i:
                    gather(i)
                    scatter(i - 1)
                scatter(PAIRS_E - 1)

            pool.wait_ge(s_gb, 2 * DMA)

            def f_pair(i):
                for u in range(SLOTS):
                    g = i * SLOTS + u
                    pool.wait_ge(f_r[u], (i + 1) * DMA)
                    nc.gpsimd.tensor_tensor(a_rows[:, u, :, :], a_rows[:, u, :, :], shift_all[:, None, :].to_broadcast([P, TILES, C]), ALU.add).then_inc(f_sh, 1)
            with pool.Fori(0, PAIRS_N) as i:
                f_pair(i)

        @block.tensor
        def _(pe):
            for s in (e_srcP, e_dstP, e_h1P, e_h2P, e_h3P, e_varP, e_segP, n_xP, n_aP, n_h1P, n_h2P, n_h3P):
                pe.sem_inc(s, SLOTS)
            pe.wait_ge(s_const, 5)
            pe.wait_ge(s_vload, DMA * (9 if L > 1 else 7))
            nc.tensor.transpose(banks[0][0][:, 0:L * VECS], vec_rows[:, :], ident[0:L * VECS, 0:L * VECS]).then_inc(s_vT, 1)
            pe.wait_ge(s_dis, 2)
            pe.wait_ge(s_cst2, 3)
            nc.tensor.matmul(banks[0][1][0:1, 0:1], disorder[0:GE, :], ones_col[0:GE, :], start=True, stop=True).then_inc(s_dsum, 1)
            pe.wait_ge(s_tab, 3)
            for kind in range(3):
                for t in range(TILES):
                    mm = nc.tensor.transpose(banks[1][kind][:, t * GE:(t + 1) * GE], e_tab[0:GE, kind, t * P:(t + 1) * P], ident[0:GE, 0:GE])
                mm.then_inc(s_tabT, 1)
            pe.wait_ge(s_vall, 1)
            pe.wait_ge(s_idx, 3)

            def turn(bank, rows, u, signal):
                for t in range(TILES):
                    mm = nc.tensor.transpose(bank[:, t * P:(t + 1) * P], rows[:, u, t, :], ident[:, :])
                mm.then_inc(signal, 1)

            with pe.Fori(0, L) as l:
                pe.wait_ge(s_wts, l + 1)
                pe.sem_inc(passed["pe"], 1)
                with pe.Fori(0, PAIRS_E) as i:
                    pair = l * PAIRS_E + i
                    ks = [pair * SLOTS + u for u in range(SLOTS)]
                    for u, k in enumerate(ks):
                        b = banks[u]
                        pe.wait_ge(s_src[u], (pair + 1) * (TILES * DMA))
                        pe.wait_ge(e_sq, free(k))
                        pe.wait_ge(e_nrm, free(k))
                        turn(b[0], src_rows, u, e_srcP)
                        pe.wait_ge(s_dst[u], (pair + 1) * (TILES * DMA))
                        pe.wait_ge(e_sd, free(k))
                        turn(b[1], dst_rows, u, e_dstP)
                    for u, k in enumerate(ks):
                        b = banks[u]
                        pe.wait_ge(e_dstT, done(k))
                        pe.wait_ge(e_out, free(k))
                        nc.tensor.matmul(b[2][:, :], W[:, EW1_DST, :], dstT[:, u, :], start=True, stop=False)
                        pe.wait_ge(e_srcT, done(k))
                        nc.tensor.matmul(b[2][:, :], W[:, EW1_SRC, :], srcT[:, u, :], start=False, stop=True).then_inc(e_h1P, 1)
                    for u, k in enumerate(ks):
                        pe.wait_ge(e_h1, done(k))
                        pe.wait_ge(e_h2b, free(k))
                        nc.tensor.matmul(banks[u][3][:, :], W[:, EW2, :], eh1[:, u, :], start=True, stop=True).then_inc(e_h2P, 1)
                    for u, k in enumerate(ks):
                        pe.wait_ge(e_h2, done(k))
                        nc.tensor.matmul(banks[u][0][:, :], W3c[:, 0, :], eh2[:, u, :], start=True, stop=True).then_inc(e_h3P, 1)
                    for u, k in enumerate(ks):
                        pe.wait_ge(e_sq, done(k))
                        nc.tensor.matmul(banks[u][1][:, :], mean_w[:, :], esq[:, u, :], start=True, stop=True).then_inc(e_varP, 1)
                    for u, k in enumerate(ks):
                        pe.wait_ge(e_seg, done(k))
                        for t in range(TILES):
                            mm = nc.tensor.transpose(banks[u][2][:, t * P:(t + 1) * P], seg[:, u, t * P:(t + 1) * P], ident[:, :])
                        mm.then_inc(e_segP, 1)
                pe.wait_ge(e_out, (l + 1) * GE + SLOTS)
                pe.sem_inc(passed["pe"], 1)
                with pe.Fori(0, PAIRS_N) as i:
                    pair = l * PAIRS_N + i
                    ks = [pair * SLOTS + u for u in range(SLOTS)]
                    for u, k in enumerate(ks):
                        b = banks[u]
                        pe.wait_ge(s_x[u], (pair + 1) * DMA)
                        pe.wait_ge(n_sq, free(k))
                        pe.wait_ge(n_new, free(k))
                        turn(b[0], x_rows, u, n_xP)
                        pe.wait_ge(s_a[u], (pair + 1) * DMA)
                        pe.wait_ge(n_aT, free(k))
                        turn(b[1], a_rows, u, n_aP)
                    for u, k in enumerate(ks):
                        b = banks[u]
                        pe.wait_ge(n_xT, done(k))
                        pe.wait_ge(n_h1b, free(k))
                        nc.tensor.matmul(b[2][:, :], W[:, NW1_X, :], xT[:, u, :], start=True, stop=False)
                        pe.wait_ge(n_aT, done(k))
                        nc.tensor.matmul(b[2][:, :], W[:, NW1_AGG, :], aT[:, u, :], start=False, stop=True).then_inc(n_h1P, 1)
                    for u, k in enumerate(ks):
                        pe.wait_ge(n_h1, done(k))
                        pe.wait_ge(n_h2b, free(k))
                        nc.tensor.matmul(banks[u][3][:, :], W[:, NW2, :], nh1[:, u, :], start=True, stop=True).then_inc(n_h2P, 1)
                    for u, k in enumerate(ks):
                        pe.wait_ge(n_h2, done(k))
                        for t in range(TILES):
                            mm = nc.tensor.matmul(banks[u][0][:, t * P:(t + 1) * P], nh2[:, u, t * P:(t + 1) * P], W3c[:, 1, :], start=True, stop=True)
                        mm.then_inc(n_h3P, 1)

        @block.scalar
        def _(act):
            for s in (e_srcT, e_h1b, e_h2b, e_sq, e_sd, e_msg, n_xT, n_aT, n_h1b, n_h2b, n_sq, n_sd, f_sq, f_sd):
                act.sem_inc(s, SLOTS)
            act.wait_ge(s_const, 5)
            nc.scalar.dma_start(agg.rearrange("(p r) c -> p r c", p=P), zeros[:, None, :].to_broadcast([P, NP // P, C])).then_inc(s_azero, DMA)
            act.wait_ge(s_cst2, 3)
            with act.Fori(0, L) as l:
                act.wait_ge(s_wts, l + 1)
                act.sem_inc(passed["act"], 1)
                with act.Fori(0, PAIRS_E) as i:
                    pair = l * PAIRS_E + i
                    ks = [pair * SLOTS + u for u in range(SLOTS)]
                    for u, k in enumerate(ks):
                        act.wait_ge(e_srcP, done(k))
                        act.wait_ge(e_h1P, free(k))
                        nc.scalar.activation(srcT[:, u, :], banks[u][0][:, :], ACT.Identity, bias=vecs[:, XB:XB + 1], scale=vecs[:, XG:XG + 1]).then_inc(e_srcT, 1)
                    for u, k in enumerate(ks):
                        act.wait_ge(e_h1P, done(k))
                        act.wait_ge(e_h2P, free(k))
                        nc.scalar.activation(eh1[:, u, :], banks[u][2][:, :], ACT.Identity, bias=vecs[:, EB1:EB1 + 1]).then_inc(e_h1b, 1)
                    for u, k in enumerate(ks):
                        act.wait_ge(e_h2P, done(k))
                        act.wait_ge(e_h3P, free(k))
                        nc.scalar.activation(eh2[:, u, :], banks[u][3][:, :], ACT.Identity, bias=vecs[:, EB2:EB2 + 1]).then_inc(e_h2b, 1)
                    for u, k in enumerate(ks):
                        act.wait_ge(e_h3P, done(k))
                        act.wait_ge(e_varP, free(k))
                        nc.scalar.activation(esq[:, u, :], banks[u][0][:, :], ACT.Square).then_inc(e_sq, 1)
                    for u, k in enumerate(ks):
                        act.wait_ge(e_varP, done(k))
                        act.wait_ge(e_nrm, free(k))
                        nc.scalar.activation(ersd[:, u, :], banks[u][1][:, :], ACT.Sqrt, bias=eps_col[:, :]).then_inc(e_sd, 1)
                    for u, k in enumerate(ks):
                        act.wait_ge(e_nrm, done(k))
                        nc.scalar.activation(msg[:, u, :], msg[:, u, :], ACT.Identity, bias=vecs[:, EBT:EBT + 1], scale=vecs[:, EG:EG + 1]).then_inc(e_msg, 1)
                with act.Fori(0, PAIRS_N) as i:
                    pair = l * PAIRS_N + i
                    ks = [pair * SLOTS + u for u in range(SLOTS)]
                    for u, k in enumerate(ks):
                        act.wait_ge(n_xP, done(k))
                        act.wait_ge(n_h1P, free(k))
                        nc.scalar.activation(xT[:, u, :], banks[u][0][:, :], ACT.Identity, bias=vecs[:, XB:XB + 1], scale=vecs[:, XG:XG + 1]).then_inc(n_xT, 1)
                        act.wait_ge(n_aP, done(k))
                        nc.scalar.activation(aT[:, u, :], banks[u][1][:, :], ACT.Identity).then_inc(n_aT, 1)
                    for u, k in enumerate(ks):
                        act.wait_ge(n_h1P, done(k))
                        act.wait_ge(n_h2P, free(k))
                        nc.scalar.activation(nh1[:, u, :], banks[u][2][:, :], ACT.Identity, bias=vecs[:, NB1:NB1 + 1]).then_inc(n_h1b, 1)
                    for u, k in enumerate(ks):
                        act.wait_ge(n_h2P, done(k))
                        act.wait_ge(n_h3P, free(k))
                        nc.scalar.activation(nh2[:, u, :], banks[u][3][:, :], ACT.Identity, bias=vecs[:, NB2:NB2 + 1]).then_inc(n_h2b, 1)
                    for u, k in enumerate(ks):
                        act.wait_ge(n_h3P, done(k))
                        act.wait_ge(n_ss, free(k))
                        nc.scalar.activation(nsq[:, u, :, :].rearrange("p t c -> p (t c)"), banks[u][0][:, :], ACT.Square).then_inc(n_sq, 1)
                    for u, k in enumerate(ks):
                        act.wait_ge(n_ss, done(k))
                        act.wait_ge(n_new, free(k))
                        nc.scalar.activation(nrs[:, u, :], nss[:, u, :], ACT.Sqrt, bias=eps_col[:, :], scale=1.0 / C).then_inc(n_sd, 1)
            with act.Fori(0, PAIRS_N) as i:
                for u in range(SLOTS):
                    g = i * SLOTS + u
                    act.wait_ge(f_c, done(g))
                    act.wait_ge(f_ss, free(g))
                    nc.scalar.activation(nsq[:, u, :, :], x_rows[:, u, :, :], ACT.Square).then_inc(f_sq, 1)
                for u in range(SLOTS):
                    g = i * SLOTS + u
                    act.wait_ge(f_ss, done(g))
                    act.wait_ge(f_new, free(g))
                    nc.scalar.activation(nrs[:, u, :], nss[:, u, :], ACT.Sqrt, bias=eps_col[:, :], scale=1.0 / C).then_inc(f_sd, 1)

        def rank_edges(dve):
            dve.wait_ge(q_cols, 2 * DMA)
            nc.vector.tensor_copy(dcol_f, dcol_i).then_inc(q_step, 1)
            dve.wait_ge(q_step, 1)
            steps = 1

            def count(c, j):
                dve.wait_ge(q_count, j + c * NT)
                nc.vector.tensor_scalar(chunk_junk, chunk_f, dcol_f[:, bass.ds(j, 1)], None, ALU.is_lt, ALU.add,
                                        accum_out=less(c)[:, bass.ds(j, 1)]).then_inc(q_count, 1)

            for c in range(CHUNKS):
                lo, hi = c * CT, (c + 1) * CT
                dve.wait_ge(q_chunk, (c + 1) * DMA)
                dve.wait_ge(q_used, c)
                nc.vector.tensor_copy(chunk_f, chunk_i).then_inc(q_conv, 1)
                dve.wait_ge(q_conv, c + 1)
                if c:
                    with dve.Fori(0, lo) as j:
                        count(c, j)
                with dve.Fori(lo, hi) as j:
                    at = bass.ds((j - lo) * P, P)
                    count(c, j)
                    nc.vector.tensor_scalar(equal, chunk_f[:, at], dcol_f[:, bass.ds(j, 1)], None, ALU.is_equal).then_inc(q_step, 1)
                    dve.wait_ge(q_step, (j - lo) * 3 + (steps + 1))
                    nc.vector.tensor_tensor(equal_junk, equal, below[:, :], ALU.mult).then_inc(q_step, 1)
                    dve.wait_ge(q_step, (j - lo) * 3 + (steps + 2))
                    nc.vector.reduce_sum(tie[:, bass.ds(j, 1)], equal_junk, AX.X)
                    nc.vector.tensor_scalar(chunk_f[:, at], chunk_f[:, at], -0.5, None, ALU.add).then_inc(q_step, 1)
                    dve.wait_ge(q_step, (j - lo) * 3 + (steps + 3))
                    dve.sem_inc(passed["dve"], 1)
                steps += 3 * CT
                if hi < NT:
                    with dve.Fori(hi, NT) as j:
                        count(c, j)
                dve.wait_ge(q_count, (c + 1) * NT)
                nc.vector.memset(equal, 0.0).then_inc(q_used, 1)
            dve.wait_ge(q_used, CHUNKS)
            nc.vector.tensor_scalar(rank_f, tie, 1.0, None, ALU.add).then_inc(q_step, 1)
            for c in range(CHUNKS):
                dve.wait_ge(q_step, steps + 1 + c)
                nc.vector.tensor_tensor(rank_f, rank_f, less(c), ALU.add).then_inc(q_step, 1)
            dve.wait_ge(q_step, steps + 1 + CHUNKS)
            nc.vector.tensor_copy(rank_i, rank_f).then_inc(q_rank, 1)

        @block.vector
        def _(dve):
            for s in (e_dstT, e_h1, e_h2, e_rsd, e_nrm, e_seg, e_out, n_h1, n_h2, n_ss, n_rs, n_new, f_ga, f_y, f_mean, f_c, f_ss, f_rs, f_new):
                dve.sem_inc(s, SLOTS)
            nc.vector.memset(vec_rows[:, :], 1.0).then_inc(s_vrow, 1)
            nc.vector.memset(mean_w[:, :], 1.0 / C).then_inc(s_cst2, 1)
            nc.vector.memset(eps_col[:, :], EPS).then_inc(s_cst2, 1)
            nc.vector.memset(ones_col[:, :], 1.0).then_inc(s_cst2, 1)
            dve.wait_ge(s_check, 2 * DMA)
            nc.vector.tensor_tensor(e_tab[0:GE, 0, :], e_now[0:GE, :], e_prev[0:GE, :], ALU.is_lt).then_inc(s_dis, 1)
            dve.wait_ge(s_dis, 1)
            nc.vector.reduce_max(disorder[0:GE, :], e_tab[0:GE, 0, :], AX.X).then_inc(s_dis, 1)
            dve.wait_ge(s_dsum, 1)
            nc.vector.tensor_scalar(unsorted[0:1, 0:1], banks[0][1][0:1, 0:1], 1.0, None, ALU.min).then_inc(s_flag, 1)
            dve.wait_ge(s_flag, 1)
            is_unsorted = dve.value_load(unsorted[0:1, 0:1], min_val=0, max_val=1)
            with dve.If(is_unsorted != 0):
                rank_edges(dve)
            with dve.Else():
                dve.nop()

            dve.wait_ge(s_edges, 4 * DMA)
            nc.vector.tensor_tensor(e_cont[0:GE, :], e_now[0:GE, :], e_prev[0:GE, :], ALU.is_equal).then_inc(s_cont, 1)
            nc.vector.tensor_copy(e_tab[0:GE, 0, :], e_src[0:GE, :]).then_inc(s_tab, 1)
            nc.vector.tensor_copy(e_tab[0:GE, 1, :], e_now[0:GE, :]).then_inc(s_tab, 1)
            nc.vector.tensor_tensor(e_tab[0:GE, 2, :], e_now[0:GE, :], e_next[0:GE, :], ALU.is_equal).then_inc(s_cont, 1)
            dve.wait_ge(s_cont, 2)
            nc.vector.scalar_tensor_tensor(e_tab[0:GE, 2, :], e_tab[0:GE, 2, :], float(SKIP), e_now[0:GE, :], ALU.mult, ALU.add).then_inc(s_tab, 1)
            for kind in range(3):
                dve.wait_ge(s_tabT, kind + 1)
                nc.vector.tensor_copy(idx_all[:, :, kind * TILES:(kind + 1) * TILES].rearrange("p g t -> p t g"),
                                      banks[1][kind][:, 0:TILES * GE].rearrange("p (t g) -> p t g", t=TILES)).then_inc(s_idx, 1)
            dve.wait_ge(s_vT, 1)
            nc.vector.tensor_copy(vecs_all[:, :], banks[0][0][:, 0:L * VECS]).then_inc(s_vall, 1)
            nc.vector.memset(seg[:, :, :], 0.0).then_inc(s_vall, 1)
            dve.wait_ge(s_vall, 2)
            dve.wait_ge(s_call, DMA)

            with dve.Fori(0, L) as l:
                dve.wait_ge(s_wload, (l + 1) * (6 * DMA))
                dve.wait_ge(s_call, DMA)
                nc.vector.tensor_copy(vecs[:, :], vecs_all[:, bass.ds(l * VECS, VECS)]).then_inc(s_wmean, 1)
                for n, k in enumerate((EW3, NW3)):
                    nc.vector.reduce_sum(w3_mean[:, n:n + 1], W[:, k, :], AX.X).then_inc(s_wmean, 1)
                dve.wait_ge(s_wmean, l * 4 + 3)
                nc.vector.tensor_scalar(w3_mean[:, :], w3_mean[:, :], 1.0 / C, None, ALU.mult).then_inc(s_wmean, 1)
                dve.wait_ge(s_wmean, l * 4 + 4)
                nc.vector.tensor_scalar(W3c[:, 0, :], W[:, EW3, :], w3_mean[:, 0:1], None, ALU.subtract)
                nc.vector.tensor_scalar(W3c[:, 1, :], W[:, NW3, :], w3_mean[:, 1:2], None, ALU.subtract).then_inc(s_wts, 1)

                dve.wait_ge(s_wts, l + 1)
                dve.sem_inc(passed["dve"], 1)
                with dve.Fori(0, PAIRS_E) as i:
                    pair = l * PAIRS_E + i
                    ks = [pair * SLOTS + u for u in range(SLOTS)]
                    for u, k in enumerate(ks):
                        dve.wait_ge(e_dstP, done(k))
                        dve.wait_ge(e_h1P, free(k))
                        nc.vector.tensor_scalar(dstT[:, u, :], banks[u][1][:, :], vecs[:, XG:XG + 1], vecs[:, XB:XB + 1], ALU.mult, ALU.add).then_inc(e_dstT, 1)
                    for u, k in enumerate(ks):
                        dve.wait_ge(e_h1b, done(k))
                        nc.vector.scalar_tensor_tensor(eh1[:, u, :], eh1[:, u, :], SLOPE, eh1[:, u, :], ALU.mult, ALU.max).then_inc(e_h1, 1)
                    for u, k in enumerate(ks):
                        dve.wait_ge(e_h2b, done(k))
                        nc.vector.scalar_tensor_tensor(eh2[:, u, :], eh2[:, u, :], SLOPE, eh2[:, u, :], ALU.mult, ALU.max).then_inc(e_h2, 1)
                    for u, k in enumerate(ks):
                        dve.wait_ge(e_sd, done(k))
                        nc.vector.reciprocal(ersd[:, u, :], ersd[:, u, :]).then_inc(e_rsd, 1)
                    for u, k in enumerate(ks):
                        dve.wait_ge(e_rsd, done(k))
                        dve.wait_ge(e_seg, free(k))
                        nc.vector.tensor_tensor(msg[:, u, :], banks[u][0][:, :], ersd[:, u, :], ALU.mult).then_inc(e_nrm, 1)
                    for u, k in enumerate(ks):
                        dve.wait_ge(e_msg, done(k))
                        dve.wait_ge(e_segP, free(k))
                        dve.wait_ge(e_seg, k + SLOTS)
                        nc.vector.tensor_tensor_scan(seg[:, u, :], cont_all[:, bass.ds((i * SLOTS + u) * GROUP, GROUP)], msg[:, u, :],
                                                     seg[:, 1 - u, GROUP - 1:GROUP], ALU.mult, ALU.add).then_inc(e_seg, 1)
                    for u, k in enumerate(ks):
                        dve.wait_ge(e_segP, done(k))
                        dve.wait_ge(s_scat[u], pair * (TILES * DMA))
                        nc.vector.tensor_copy(seg_rows[:, u, :, :].rearrange("p t c -> p (t c)"), banks[u][2][:, :]).then_inc(e_out, 1)
                with dve.Fori(0, PAIRS_N) as i:
                    pair = l * PAIRS_N + i
                    ks = [pair * SLOTS + u for u in range(SLOTS)]
                    for u, k in enumerate(ks):
                        dve.wait_ge(n_h1b, done(k))
                        nc.vector.scalar_tensor_tensor(nh1[:, u, :], nh1[:, u, :], SLOPE, nh1[:, u, :], ALU.mult, ALU.max).then_inc(n_h1, 1)
                    for u, k in enumerate(ks):
                        dve.wait_ge(n_h2b, done(k))
                        nc.vector.scalar_tensor_tensor(nh2[:, u, :], nh2[:, u, :], SLOPE, nh2[:, u, :], ALU.mult, ALU.max).then_inc(n_h2, 1)
                    for u, k in enumerate(ks):
                        dve.wait_ge(n_sq, done(k))
                        dve.wait_ge(n_sd, free(k))
                        nc.vector.reduce_sum(nss[:, u, :], nsq[:, u, :, :], AX.X).then_inc(n_ss, 1)
                    for u, k in enumerate(ks):
                        dve.wait_ge(n_sd, done(k))
                        nc.vector.reciprocal(nrs[:, u, :], nrs[:, u, :]).then_inc(n_rs, 1)
                    for u, k in enumerate(ks):
                        dve.wait_ge(n_rs, done(k))
                        dve.wait_ge(s_st[u], pair * DMA)
                        nc.vector.tensor_tensor(new_rows[:, u, :, :], banks[u][0][:, :].rearrange("p (t c) -> p t c", t=TILES),
                                                nrs[:, u, :, None].to_broadcast([P, TILES, C]), ALU.mult).then_inc(n_new, 1)

            dve.wait_ge(s_gb, 2 * DMA)
            with dve.Fori(0, PAIRS_N) as i:
                us = range(SLOTS)
                for u in us:
                    g = i * SLOTS + u
                    dve.wait_ge(f_x[u], (i + 1) * DMA)
                    nc.vector.tensor_tensor(x_rows[:, u, :, :], x_rows[:, u, :, :], gain_all[:, None, :].to_broadcast([P, TILES, C]), ALU.mult).then_inc(f_ga, 1)
                for u in us:
                    g = i * SLOTS + u
                    dve.wait_ge(f_ga, done(g))
                    dve.wait_ge(f_sh, done(g))
                    nc.vector.tensor_tensor(x_rows[:, u, :, :], x_rows[:, u, :, :], a_rows[:, u, :, :], ALU.add).then_inc(f_y, 1)
                for u in us:
                    g = i * SLOTS + u
                    dve.wait_ge(f_y, done(g))
                    nc.vector.reduce_sum(fmean[:, u, :], x_rows[:, u, :, :], AX.X).then_inc(f_mean, 1)
                for u in us:
                    g = i * SLOTS + u
                    dve.wait_ge(f_mean, done(g))
                    nc.vector.scalar_tensor_tensor(x_rows[:, u, :, :], fmean[:, u, :, None].to_broadcast([P, TILES, C]), -1.0 / C, x_rows[:, u, :, :], ALU.mult, ALU.add).then_inc(f_c, 1)
                for u in us:
                    g = i * SLOTS + u
                    dve.wait_ge(f_sq, done(g))
                    dve.wait_ge(f_sd, free(g))
                    nc.vector.reduce_sum(nss[:, u, :], nsq[:, u, :, :], AX.X).then_inc(f_ss, 1)
                for u in us:
                    g = i * SLOTS + u
                    dve.wait_ge(f_sd, done(g))
                    nc.vector.reciprocal(nrs[:, u, :], nrs[:, u, :]).then_inc(f_rs, 1)
                for u in us:
                    g = i * SLOTS + u
                    dve.wait_ge(f_rs, done(g))
                    dve.wait_ge(f_st[u], i * DMA)
                    nc.vector.tensor_tensor(new_rows[:, u, :, :], x_rows[:, u, :, :], nrs[:, u, :, None].to_broadcast([P, TILES, C]), ALU.mult).then_inc(f_new, 1)


_INS = ["x", "src", "dst"] + [f"L0_gnn_{n}" for n in ("eW1", "eb1", "eW2", "eb2", "eW3", "eg", "ebt", "nW1", "nb1", "nW2", "nb2", "nW3", "ng", "nbt")]


def kernel(**inputs):
    import numpy as np
    import concourse.bacc as bacc
    from concourse.bass_utils import run_bass_kernel_spmd

    nc = bacc.Bacc("TRN2", target_bir_lowering=False, num_devices=1)
    arrays, args = {}, []
    for name in _INS:
        a = np.ascontiguousarray(inputs[name])
        arrays[f"in_{name}"] = a
        args.append(nc.dram_tensor(f"in_{name}", a.shape, mybir.dt.from_np(a.dtype), kind="ExternalInput").ap())
    out = nc.dram_tensor("out_0", inputs["x"].shape, F32, kind="ExternalOutput").ap()
    gnn_kernel(nc, *args, out)
    r = run_bass_kernel_spmd(nc, [arrays], core_ids=[0])
    return r.results[0]["out_0"]
```

```python
from contextlib import ExitStack

import concourse.bass as bass
from concourse import mybir
from concourse.alu_op_type import AluOpType as ALU

ACT = mybir.ActivationFunctionType
F32 = mybir.dt.float32
BF16 = mybir.dt.bfloat16
F16 = mybir.dt.float16
I32 = mybir.dt.int32
AX = mybir.AxisListType

P = 128
TILES = 4
GROUP = P * TILES
GROUP_BITS = 9
SLOTS = 2
EPS = 1e-5
SLOPE = 0.2
DMA = 16
EB1, EB2, NB1, NB2, XG, XB = range(6)
VECS = 8
POOL_CONSTS, DVE_CONSTS = 10, 8
EW1_DST, EW1_SRC, EW2, EW3, NW1_X, NW1_AGG, NW2, NW3 = range(8)


def done(k):
    return k + 1 + SLOTS


def prev(k):
    return k + SLOTS


def free(k):
    return k + 1


def skewed(eng, groups, stages, last_apart=False):
    deepest = max(lag for lag, _ in stages)
    pairs = groups // SLOTS

    def steps(i, always):
        for u in range(SLOTS):
            for lag, fn in stages:
                if always or 0 <= i * SLOTS + u - lag < groups:
                    fn(i + (u - lag) // SLOTS, (u - lag) % SLOTS)

    first = -(-deepest // SLOTS)
    end = pairs - 1 if last_apart else pairs
    assert first < end
    for i in range(first):
        steps(i, False)
    with eng.Fori(first, end) as i:
        steps(i, True)
    for i in range(end, pairs + first):
        steps(i, False)


def gnn_kernel(nc, x, src, dst, eW1, eb1, eW2, eb2, eW3, eg, ebt, nW1, nb1, nW2, nb2, nW3, ng, nbt, out):
    N, C = x.shape
    E = src.shape[0]
    L = eW2.shape[0]
    assert C == P and GROUP == 1 << GROUP_BITS
    GE = -(-E // (SLOTS * GROUP)) * SLOTS
    GN = -(-N // (SLOTS * GROUP)) * SLOTS
    EP, NP = GE * GROUP, GN * GROUP
    PAIRS_E, PAIRS_N = GE // SLOTS, GN // SLOTS
    NT = GE * TILES
    assert GE <= P and GN <= P and EP <= NP and NP > N
    LAST_ROWS = N - (GN - 1) * GROUP
    assert 0 < LAST_ROWS and LAST_ROWS % TILES == 0
    LAST_P = LAST_ROWS // TILES
    CHUNKS = next(c for c in range(6, NT + 1) if NT % c == 0)
    CW, CT = EP // CHUNKS, NT // CHUNKS

    def scratch(name, shape, dt):
        return nc.dram_tensor(name, shape, dt, kind="Internal").ap()

    x_state = scratch("x_state", [NP, C], F32)
    aggT = scratch("aggT", [P, NP], F32)
    dst_sorted = scratch("dst_sorted", [EP + 2, 1], I32)
    src_sorted = scratch("src_sorted", [EP + 2, 1], I32)
    rel_dram = scratch("rel_dram", [GE, GROUP], BF16)
    base_dram = scratch("base_dram", [GE, TILES], I32)
    number_dram = scratch("number_dram", [NP, 1], I32)

    x_groups = x_state.rearrange("(g p t) c -> g p (t c)", p=P, t=TILES)
    x_in_groups = x[0:(GN - 1) * GROUP, :].rearrange("(g p t) c -> g p (t c)", p=P, t=TILES)
    out_groups = out[0:(GN - 1) * GROUP, :].rearrange("(g p t) c -> g p (t c)", p=P, t=TILES)
    x_in_last = x[(GN - 1) * GROUP:N, :].rearrange("(p t) c -> p (t c)", t=TILES)
    out_last = out[(GN - 1) * GROUP:N, :].rearrange("(p t) c -> p (t c)", t=TILES)

    with ExitStack() as ctx:
        def sb(name, shape, dt=F32):
            return ctx.enter_context(nc.sbuf_tensor(name, shape, dt))

        def sem(name):
            return ctx.enter_context(nc.semaphore(name))

        def sems(name):
            return [sem(f"{name}{u}") for u in range(SLOTS)]

        ident = sb("ident", [P, P])
        below = sb("below", [P, P])
        after = sb("after", [P, P])
        ones = sb("ones", [P, P])
        group_col = sb("group_col", [P, 1])
        zeros = sb("zeros", [P, C])
        zeros_b = sb("zeros_b", [P, GROUP], BF16)
        eps_col = sb("eps_col", [P, 1])
        part_col = sb("part_col", [P, 1])
        part_i = sb("part_i", [P, 1], I32)
        count_i = sb("count_i", [P, GROUP], I32)
        count_h = sb("count_h", [P, GROUP], F16)
        count_f = sb("count_f", [P, P])
        pad_vals = sb("pad_vals", [1, GROUP], I32)
        pad_ends = sb("pad_ends", [1, 1], I32)
        vec_rows = sb("vec_rows", [L * VECS, C])
        vecs_all = sb("vecs_all", [P, L * VECS])
        vecs = sb("vecs", [P, VECS])
        W = sb("W", [P, 8, C])
        W3c = sb("W3c", [P, 2, C])
        w3_mean = sb("w3_mean", [P, 2])
        msg_gain = sb("msg_gain", [P, C])
        msg_shift = sb("msg_shift", [P, C])
        out_gain = sb("out_gain", [P, C])
        out_shift = sb("out_shift", [P, C])
        e_now = sb("e_now", [P, GROUP], I32)
        e_prev = sb("e_prev", [P, GROUP], I32)
        e_src = sb("e_src", [P, GROUP], I32)
        disorder = sb("disorder", [P, 1])
        unsorted = sb("unsorted", [1, 1], I32)
        row_sum = sb("row_sum", [P, 2])
        base_i = sb("base_i", [P, TILES], I32)
        base_row = sb("base_row", [1, NT], I32)
        off_row = sb("off_row", [1, NT], I32)
        step_row = sb("step_row", [1, GE], I32)
        src_idx = sb("src_idx", [P, GE, TILES], I32)
        num_idx = sb("num_idx", [P, GN, TILES], I32)
        rel_cols = sb("rel_cols", [P, NT])
        rel_all = sb("rel_all", [P, EP], BF16)
        gather_idx = sb("gather_idx", [P, SLOTS, TILES], I32)
        new_idx = sb("new_idx", [P, SLOTS, TILES], I32)
        src_rows = sb("src_rows", [P, SLOTS, TILES, C])
        win_rows = sb("win_rows", [P, SLOTS, TILES, C])
        spread = sb("spread", [P, SLOTS, GROUP])
        collect = sb("collect", [P, SLOTS, TILES, P])
        srcT = sb("srcT", [P, SLOTS, GROUP])
        dstT = sb("dstT", [P, SLOTS, GROUP])
        eh1 = sb("eh1", [P, SLOTS, GROUP])
        eh2 = sb("eh2", [P, SLOTS, GROUP])
        esq = sb("esq", [P, SLOTS, TILES, C])
        msg = sb("msg", [P, SLOTS, TILES, C])
        ess = sb("ess", [P, SLOTS, TILES])
        ers = sb("ers", [P, SLOTS, TILES])
        sums = sb("sums", [P, SLOTS, GROUP + 1])
        x_rows = sb("x_rows", [P, SLOTS, TILES, C])
        aT = sb("aT", [P, SLOTS, GROUP])
        xT = sb("xT", [P, SLOTS, GROUP])
        nh1 = sb("nh1", [P, SLOTS, GROUP])
        nh2 = sb("nh2", [P, SLOTS, GROUP])
        nsq = sb("nsq", [P, SLOTS, TILES, C])
        new_rows = sb("new_rows", [P, SLOTS, TILES, C])
        nss = sb("nss", [P, SLOTS, TILES])
        nrs = sb("nrs", [P, SLOTS, TILES])
        fstat = sb("fstat", [P, SLOTS, TILES, 6])
        fmv = sb("fmv", [P, SLOTS, TILES, 2])
        fshift = sb("fshift", [P, SLOTS, TILES])

        bank = [ctx.enter_context(nc.psum_tensor(f"bank{b}", [P, GROUP], F32)) for b in range(8)]
        B_SRC, B_DST, B_H1, B_H2, B_H3, B_SUM = 0, 1, 2, 3, 4, 6

        s_const = sem("pool_constants")
        s_cst2 = sem("dve_constants")
        passed = {e: sem(f"{e}_passed") for e in ("sp", "pool", "pe", "act", "dve")}
        s_pads = sem("pads_made")
        s_raw = sem("edges_copied")
        s_check = sem("check_loaded")
        s_dis = sem("disorder_counted")
        s_dsum = sem("disorder_summed")
        s_flag = sem("flag_made")
        s_edges = sem("edges_loaded")
        s_colr = sem("columns_rows_ready")
        s_colP = sem("columns_turned")
        s_col = sem("columns_made")
        s_run = sem("edge_scan")
        s_tmp = sem("numbering_step")
        s_offP = sem("edge_offsets")
        s_rel = sem("edge_numbers")
        s_reld = sem("rel_in_dram")
        s_rela = sem("rel_spread")
        s_based = sem("base_in_dram")
        s_baser = sem("base_row_loaded")
        s_rows = sem("row_tables")
        s_relP = sem("rel_turned")
        s_relc = sem("rel_columns")
        h_lo = sem("histogram_masks")
        h_P = sem("histogram_tiles")
        h_all = sem("histogram_over")
        s_node = sem("node_scan")
        s_noffP = sem("node_offsets")
        s_num = sem("node_numbers")
        s_numd = sem("numbers_in_dram")
        s_numP = sem("numbers_turned")
        s_numi = sem("number_table")
        s_vrow = sem("vec_rows_set")
        s_vload = sem("vec_rows_loaded")
        s_vT = sem("vecs_turned")
        s_vall = sem("vecs_all_made")
        s_azero = sem("aggT_zeroed")
        s_gb = sem("out_gain_shift_loaded")
        m_stage = sem("remap_staged")
        m_got = sems("remap_gathered")
        m_put = sem("remap_kept")
        p_x = sems("perm_x_loaded")
        p_clear = sem("perm_pads_cleared")
        p_stage = sem("perm_staged")
        p_put = sems("perm_scattered")
        q_cols = sem("sort_columns_loaded")
        q_chunk = sem("sort_chunk_loaded")
        q_conv = sem("sort_chunk_converted")
        q_used = sem("sort_chunk_used")
        q_step = sem("sort_step")
        q_count = sem("sort_tiles_counted")
        q_rank = sem("sort_ranks_made")
        q_copy = sem("sort_staged")
        q_put = sem("sort_scattered")
        s_wload = sem("weights_loaded")
        s_wmean = sem("w3_means")
        s_wts = sem("weights_ready")
        s_gidx = sem("gather_idx_staged")
        s_src = sems("src_rows_gathered")
        s_win = sems("win_rows_loaded")
        s_agg = sem("sums_stored")
        e_srcP, e_srcT = sem("e_src_turned"), sem("e_src_scaled")
        e_spread, e_dstP, e_dstT = sem("e_spread"), sem("e_dst_spread"), sem("e_dst_scaled")
        e_h1P, e_h1b, e_h1 = sem("e_h1_product"), sem("e_h1_biased"), sem("e_h1_ready")
        e_h2P, e_h2b, e_h2 = sem("e_h2_product"), sem("e_h2_biased"), sem("e_h2_ready")
        e_h3P, e_sq, e_ss, e_sd = sem("e_h3_product"), sem("e_squares"), sem("e_square_sums"), sem("e_deviation")
        e_rs, e_gain, e_msg, e_coll = sem("e_rsd"), sem("e_gained"), sem("e_message"), sem("e_collect")
        e_sumP, e_sumc, e_sum = sem("e_sum_product"), sem("e_sum_copied"), sem("e_sum_carried")
        s_x, s_a, s_st = sems("x_rows_loaded"), sems("aT_loaded"), sems("new_rows_stored")
        n_xP, n_xT = sem("n_x_turned"), sem("n_x_scaled")
        n_h1P, n_h1b, n_h1 = sem("n_h1_product"), sem("n_h1_biased"), sem("n_h1_ready")
        n_h2P, n_h2b, n_h2 = sem("n_h2_product"), sem("n_h2_biased"), sem("n_h2_ready")
        n_h3P, n_sq, n_ss, n_sd = sem("n_h3_product"), sem("n_squares"), sem("n_square_sums"), sem("n_deviation")
        n_rs, n_new = sem("n_rsd"), sem("n_new_rows")
        f_idx, f_x, f_r, f_st = sem("f_idx_staged"), sems("f_x_gathered"), sems("f_residual_loaded"), sems("f_out_stored")
        f_ga, f_sh, f_y, f_bn, f_mv = sem("f_gained"), sem("f_shifted"), sem("f_summed"), sem("f_stats"), sem("f_mean_var")
        f_sd, f_rs, f_ms, f_new = sem("f_deviation"), sem("f_rsd"), sem("f_mean_shift"), sem("f_rows")

        block = ctx.enter_context(nc.Block())

        def whole(b):
            return b[:, :, :].rearrange("p s f -> p (s f)") if len(b.shape) == 3 else b[:, :, :, :].rearrange("p s t c -> p (s t c)")

        sort_room = rel_all[:, :].bitcast(F32)
        chunk_f = sort_room[:, 0:CW]
        chunk_i = sort_room[:, CW:2 * CW].bitcast(I32)
        chunk_junk = sort_room[:, 2 * CW:3 * CW]
        dcol_f, dcol_i, scol_i = whole(srcT)[:, 0:NT], whole(dstT)[:, 0:NT].bitcast(I32), whole(eh1)[:, 0:NT].bitcast(I32)
        tie, rank_f, rank_i = whole(eh2)[:, 0:NT], whole(esq)[:, 0:NT], whole(spread)[:, 0:NT].bitcast(I32)
        equal, equal_junk = whole(msg)[:, 0:P], whole(msg)[:, P:2 * P]
        PER = SLOTS * GROUP // NT
        sort_counts = [whole(x_rows), whole(aT), whole(xT), whole(nh1), whole(nh2)]
        assert CHUNKS <= PER * len(sort_counts)

        def less(c):
            return sort_counts[c // PER][:, (c % PER) * NT:(c % PER + 1) * NT]

        st_rank, st_dst, st_src = gather_idx[:, 0, 0:1], gather_idx[:, 0, 1:2], gather_idx[:, 0, 2:3]

        rows = [whole(b)[:, s * GROUP:(s + 1) * GROUP] for b in (nh1, nh2, nsq, new_rows, aT, xT) for s in range(SLOTS)]
        g_start, g_run, g_num, g_rel, g_hi, g_lo, g_src, n_has, n_run, n_a, n_b, n_number = rows
        g_hi_i, g_lo_i = whole(collect)[:, 0:GROUP].bitcast(I32), whole(collect)[:, GROUP:2 * GROUP].bitcast(I32)
        number_i = whole(spread)[:, 0:GROUP].bitcast(I32)
        rel_b = whole(spread)[:, GROUP:GROUP + GROUP // 2].bitcast(BF16)
        base_f = whole(sums)[0:1, 0:NT]
        row_f = whole(sums)[0:1, NT:2 * NT]
        hi_cols, lo_cols, src_cols = whole(srcT)[:, 0:NT], whole(dstT)[:, 0:NT], whole(eh1)[:, 0:NT].bitcast(I32)
        mask_lo = [whole(b).bitcast(BF16).rearrange("p (t f) -> p t f", t=TILES) for b in (eh2, esq)]
        mask_hi = [whole(msg)[:, s * GROUP // 2:(s + 1) * GROUP // 2].bitcast(BF16)[:, 0:TILES * P].rearrange("p (t f) -> p t f", t=TILES) for s in range(SLOTS)]

        def edge_rows(a, shift):
            return a[shift:shift + EP, :].rearrange("(g f) o -> g (f o)", f=GROUP)

        def slot(b, u):
            return b[:, u, :, :].rearrange("p t c -> p (t c)")

        def group_of(a, g):
            return a[bass.ds(g, 1), :, :].rearrange("a p f -> p (a f)")

        @block.sync
        def _(sp):
            sp.wait_ge(s_pads, 2)
            sp.dma_start(dst_sorted[1:1 + E, :].rearrange("(a e) o -> a (e o)", a=16), dst.rearrange("(a e) -> a e", a=16)).then_inc(s_raw, DMA)
            sp.dma_start(src_sorted[1:1 + E, :].rearrange("(a e) o -> a (e o)", a=16), src.rearrange("(a e) -> a e", a=16)).then_inc(s_raw, DMA)
            raw = 2
            for a in (dst_sorted, src_sorted):
                for at in range(1 + E, 1 + EP, GROUP):
                    n = min(GROUP, 1 + EP - at)
                    sp.dma_start(a[at:at + n, :].rearrange("(a n) o -> a (n o)", a=1), pad_vals[0:1, 0:n]).then_inc(s_raw, DMA)
                    raw += 1
                for at in (0, EP + 1):
                    sp.dma_start(a[at:at + 1, :], pad_ends[0:1, 0:1]).then_inc(s_raw, DMA)
                    raw += 1
            sp.wait_ge(s_raw, DMA * raw)
            sp.dma_start(e_now[0:GE, :], edge_rows(dst_sorted, 1)).then_inc(s_check, DMA)
            sp.dma_start(e_prev[0:GE, :], edge_rows(dst_sorted, 0)).then_inc(s_check, DMA)
            sp.dma_start(out_gain[:, :], ng[L - 1:L, :].to_broadcast([P, C])).then_inc(s_gb, DMA)
            sp.dma_start(out_shift[:, :], nbt[L - 1:L, :].to_broadcast([P, C])).then_inc(s_gb, DMA)
            sp.wait_ge(s_vrow, 1)
            sp.wait_ge(s_const, POOL_CONSTS)
            for k, v in ((EB1, eb1), (EB2, eb2), (NB1, nb1), (NB2, nb2)):
                sp.dma_start(vec_rows[k:L * VECS:VECS, :], v).then_inc(s_vload, DMA)
            for k, v in ((XG, ng), (XB, nbt)):
                sp.dma_start(vec_rows[VECS + k:L * VECS:VECS, :], v[0:L - 1, :]).then_inc(s_vload, DMA)
            sp.dma_start(vec_rows[XB:XB + 1, :], zeros[0:1, :]).then_inc(s_vload, DMA)
            sp.wait_ge(s_flag, 1)
            is_unsorted = sp.value_load(unsorted[0:1, 0:1], min_val=0, max_val=1)
            with sp.If(is_unsorted != 0):
                with nc.allow_non_contiguous_dma("the sort's columns; a path seldom taken"):
                    sp.dma_start(dcol_i, dst_sorted[1:1 + EP, :].rearrange("(j p) o -> p (j o)", p=P)).then_inc(q_cols, DMA)
                    sp.dma_start(scol_i, src_sorted[1:1 + EP, :].rearrange("(j p) o -> p (j o)", p=P)).then_inc(q_cols, DMA)
                for c in range(CHUNKS):
                    if c:
                        sp.wait_ge(q_conv, c)
                    row = dst_sorted[1 + c * CW:1 + (c + 1) * CW, :].rearrange("(a n) o -> a (n o)", a=1)
                    sp.dma_start(chunk_i, row.to_broadcast([P, CW])).then_inc(q_chunk, DMA)
                sp.wait_ge(q_put, 2 * DMA * NT)
            with sp.Else():
                sp.nop()
            sp.wait_ge(s_dis, 2)
            sp.dma_start(e_now[0:GE, :], edge_rows(dst_sorted, 1)).then_inc(s_edges, DMA)
            sp.dma_start(e_prev[0:GE, :], edge_rows(dst_sorted, 0)).then_inc(s_edges, DMA)
            sp.dma_start(e_src[0:GE, :], edge_rows(src_sorted, 1)).then_inc(s_edges, DMA)
            sp.wait_ge(s_rel, 4)
            sp.dma_start(rel_dram, rel_b[0:GE, :]).then_inc(s_reld, DMA)
            sp.dma_start(base_dram, base_i[0:GE, :]).then_inc(s_based, DMA)
            sp.wait_ge(s_based, DMA)
            sp.dma_start(base_row[0:1, :], base_dram.rearrange("(a g) t -> a (g t)", a=1)).then_inc(s_baser, DMA)
            sp.wait_ge(s_reld, DMA)
            sp.dma_start(rel_all[:, :], rel_dram.rearrange("(a g) f -> a (g f)", a=1).to_broadcast([P, EP])).then_inc(s_rela, DMA)
            sp.wait_ge(s_num, 7)
            sp.dma_start(number_dram.rearrange("(g f) o -> g (f o)", f=GROUP), number_i[0:GN, :]).then_inc(s_numd, DMA)

            def x_load(i, last=False):
                for u in range(SLOTS):
                    sp.wait_ge(p_put[u], i * (TILES * DMA))
                    if last and u == SLOTS - 1:
                        sp.wait_ge(p_clear, 1)
                        sp.dma_start(x_rows[0:LAST_P, u, :, :].rearrange("p t c -> p (t c)"), x_in_last).then_inc(p_x[u], DMA)
                    else:
                        sp.dma_start(slot(x_rows, u), group_of(x_in_groups, i * SLOTS + u)).then_inc(p_x[u], DMA)

            with sp.Fori(0, PAIRS_N - 1) as i:
                x_load(i)
            x_load(PAIRS_N - 1, last=True)

            sp.wait_ge(s_rows, 3)
            sp.wait_ge(s_azero, DMA)
            with sp.Fori(0, L) as l:
                sp.wait_ge(n_h3P, l * GN + SLOTS)
                for k, w in ((EW2, eW2), (EW3, eW3), (NW2, nW2), (NW3, nW3)):
                    sp.dma_start(W[:, k, :], group_of(w, l)).then_inc(s_wload, DMA)
                for k, w in ((EW1_DST, eW1), (NW1_X, nW1)):
                    sp.dma_start(W[:, k:k + 2, :], w[bass.ds(l, 1), :, :].rearrange("a (h p) c -> p (a h) c", p=P)).then_inc(s_wload, DMA)
                for rows_of, v in ((msg_gain, eg), (msg_shift, ebt)):
                    sp.dma_start(rows_of[:, :], v[bass.ds(l, 1), :].to_broadcast([P, C])).then_inc(s_wload, DMA)
                for u in range(SLOTS):
                    sp.wait_ge(p_put[u], PAIRS_N * TILES * DMA)
                for u in range(SLOTS):
                    sp.wait_ge(s_st[u], l * (PAIRS_N * DMA))
                sp.sem_inc(passed["sp"], 1)

                def load_windows(i, u):
                    g = i * SLOTS + u
                    sp.wait_ge(e_dstP, free(l * GE + g))
                    sp.sem_inc(passed["sp"], 1)
                    for t in range(TILES):
                        base = sp.value_load(base_row[0:1, bass.ds(g * TILES + t, 1)], min_val=0, max_val=EP - P)
                        sp.dma_start(win_rows[:, u, t, :], x_state[bass.ds(base, P), :]).then_inc(s_win[u], DMA)

                def store_sums(i, u):
                    g = i * SLOTS + u
                    k = l * GE + g
                    sp.wait_ge(e_sum, done(k))
                    sp.sem_inc(passed["sp"], 1)
                    sp.wait_ge(s_agg, k * DMA)
                    sp.sem_inc(passed["sp"], 1)
                    base = sp.value_load(base_row[0:1, bass.ds(g * TILES, 1)], min_val=0, max_val=EP - GROUP)
                    sp.dma_start(aggT[:, bass.ds(base, GROUP)], sums[:, u, 0:GROUP]).then_inc(s_agg, DMA)

                skewed(sp, GE, [(0, load_windows), (5, store_sums)])
                sp.wait_ge(s_agg, (l + 1) * (GE * DMA))
                sp.sem_inc(passed["sp"], 1)

                def load_nodes(i, u):
                    g = i * SLOTS + u
                    k = l * GN + g
                    sp.wait_ge(n_xP, free(k))
                    sp.dma_start(slot(x_rows, u), group_of(x_groups, g)).then_inc(s_x[u], DMA)
                    sp.wait_ge(n_h1P, free(k))
                    sp.dma_start(aT[:, u, :], aggT[:, bass.ds(g * GROUP, GROUP)]).then_inc(s_a[u], DMA)

                def store_nodes(i, u):
                    g = i * SLOTS + u
                    sp.wait_ge(n_new, done(l * GN + g))
                    sp.dma_start(group_of(x_groups, g), slot(new_rows, u)).then_inc(s_st[u], DMA)

                skewed(sp, GN, [(0, load_nodes), (5, store_nodes)])

            def load_residual(i, u):
                g = i * SLOTS + u
                sp.wait_ge(f_y, free(g))
                if isinstance(g, int) and g == GN - 1:
                    sp.dma_start(win_rows[0:LAST_P, u, :, :].rearrange("p t c -> p (t c)"), x_in_last).then_inc(f_r[u], DMA)
                else:
                    sp.dma_start(slot(win_rows, u), group_of(x_in_groups, g)).then_inc(f_r[u], DMA)

            def store_out(i, u):
                g = i * SLOTS + u
                sp.wait_ge(f_new, done(g))
                if isinstance(g, int) and g == GN - 1:
                    sp.dma_start(out_last, new_rows[0:LAST_P, u, :, :].rearrange("p t c -> p (t c)")).then_inc(f_st[u], DMA)
                else:
                    sp.dma_start(group_of(out_groups, g), slot(new_rows, u)).then_inc(f_st[u], DMA)

            skewed(sp, GN, [(0, load_residual), (3, store_out)], last_apart=True)
            for u in range(SLOTS):
                sp.wait_ge(f_st[u], PAIRS_N * DMA)

        @block.gpsimd
        def _(pool):
            nc.gpsimd.memset(pad_vals[:, :], NP - 1).then_inc(s_pads, 1)
            nc.gpsimd.memset(pad_ends[:, :], -1).then_inc(s_pads, 1)
            nc.gpsimd.memset(ident[:, :], 0.0).then_inc(s_const, 1)
            nc.gpsimd.memset(below[:, :], 1.0).then_inc(s_const, 1)
            nc.gpsimd.memset(after[:, :], 1.0).then_inc(s_const, 1)
            nc.gpsimd.memset(zeros[:, :], 0.0).then_inc(s_const, 1)
            nc.gpsimd.iota(count_i[:, :], [[1, GROUP]], base=0, channel_multiplier=0).then_inc(s_const, 1)
            nc.gpsimd.iota(part_i[:, :], [[0, 1]], base=0, channel_multiplier=1).then_inc(s_const, 1)
            pool.wait_ge(s_const, 6)
            nc.gpsimd.affine_select(out=ident[:, :], in_=ident[:, :], compare_op=ALU.not_equal, fill=1.0, base=0,
                                    pattern=[[-1, P]], channel_multiplier=1).then_inc(s_const, 1)
            nc.gpsimd.affine_select(out=below[:, :], in_=below[:, :], compare_op=ALU.is_gt, fill=0.0, base=0,
                                    pattern=[[-1, P]], channel_multiplier=1).then_inc(s_const, 1)
            nc.gpsimd.affine_select(out=after[:, :], in_=after[:, :], compare_op=ALU.is_gt, fill=0.0, base=0,
                                    pattern=[[1, P]], channel_multiplier=-1).then_inc(s_const, 1)
            nc.gpsimd.memset(gather_idx[:, :, :], 0).then_inc(s_const, 1)
            pool.wait_ge(s_const, POOL_CONSTS)
            pool.wait_ge(s_flag, 1)
            is_unsorted = pool.value_load(unsorted[0:1, 0:1], min_val=0, max_val=1)
            with pool.If(is_unsorted != 0):
                pool.wait_ge(q_rank, 1)
                with pool.Fori(0, NT) as j:
                    pool.wait_ge(q_put, j * (2 * DMA))
                    pool.sem_inc(passed["pool"], 1)
                    nc.gpsimd.tensor_copy(st_rank, rank_i[:, bass.ds(j, 1)]).then_inc(q_copy, 1)
                    nc.gpsimd.tensor_copy(st_dst, dcol_i[:, bass.ds(j, 1)]).then_inc(q_copy, 1)
                    nc.gpsimd.tensor_copy(st_src, scol_i[:, bass.ds(j, 1)]).then_inc(q_copy, 1)
                    pool.wait_ge(q_copy, j * 3 + 3)
                    pool.sem_inc(passed["pool"], 1)
                    nc.gpsimd.indirect_dma_start(dst_sorted, bass.IndirectOffsetOnAxis(st_rank, 0), st_dst, None).then_inc(q_put, DMA)
                    nc.gpsimd.indirect_dma_start(src_sorted, bass.IndirectOffsetOnAxis(st_rank, 0), st_src, None).then_inc(q_put, DMA)
            with pool.Else():
                pool.nop()

            pool.wait_ge(s_numi, 1)

            def renumber_rows(i, u):
                g = i * SLOTS + u
                pool.wait_ge(p_put[u], i * (TILES * DMA))
                pool.sem_inc(passed["pool"], 1)
                nc.gpsimd.tensor_copy(gather_idx[:, u, :], num_idx[:, bass.ds(g, 1), :].rearrange("p a t -> p (a t)")).then_inc(p_stage, 1)
                pool.wait_ge(p_x[u], (i + 1) * DMA)
                pool.wait_ge(p_stage, g + 1)
                pool.sem_inc(passed["pool"], 1)
                for t in range(TILES):
                    nc.gpsimd.indirect_dma_start(x_state, bass.IndirectOffsetOnAxis(gather_idx[:, u, t:t + 1], 0), x_rows[:, u, t, :], None).then_inc(p_put[u], DMA)

            with pool.Fori(0, PAIRS_N) as i:
                for u in range(SLOTS):
                    renumber_rows(i, u)
            pool.wait_ge(s_numd, DMA)
            for u in range(SLOTS):
                pool.wait_ge(p_put[u], PAIRS_N * TILES * DMA)

            def fetch_numbers(i, u):
                g = i * SLOTS + u
                pool.wait_ge(m_put, free(g) - 1)
                pool.sem_inc(passed["pool"], 1)
                nc.gpsimd.tensor_copy(gather_idx[:, u, :], src_cols[:, bass.ds(g * TILES, TILES)]).then_inc(m_stage, 1)
                pool.wait_ge(m_stage, g + 1)
                pool.sem_inc(passed["pool"], 1)
                for t in range(TILES):
                    nc.gpsimd.indirect_dma_start(new_idx[:, u, t:t + 1], None, number_dram, bass.IndirectOffsetOnAxis(gather_idx[:, u, t:t + 1], 0)).then_inc(m_got[u], DMA)

            def keep_numbers(i, u):
                g = i * SLOTS + u
                pool.wait_ge(m_got[u], (i + 1) * (TILES * DMA))
                pool.sem_inc(passed["pool"], 1)
                nc.gpsimd.tensor_copy(src_idx[:, bass.ds(g, 1), :].rearrange("p a t -> p (a t)"), new_idx[:, u, :]).then_inc(m_put, 1)

            pool.sem_inc(m_put, 1)
            skewed(pool, GE, [(1, keep_numbers), (0, fetch_numbers)])
            pool.wait_ge(m_put, GE + 1)

            with pool.Fori(0, L) as l:
                for u in range(SLOTS):
                    pool.wait_ge(s_st[u], l * (PAIRS_N * DMA))
                pool.sem_inc(passed["pool"], 1)

                def gather(i, u):
                    pair = l * PAIRS_E + i
                    k = pair * SLOTS + u
                    pool.wait_ge(s_src[u], pair * (TILES * DMA))
                    pool.sem_inc(passed["pool"], 1)
                    nc.gpsimd.tensor_copy(gather_idx[:, u, :], src_idx[:, bass.ds(i * SLOTS + u, 1), :].rearrange("p a t -> p (a t)")).then_inc(s_gidx, 1)
                    pool.wait_ge(s_gidx, k + 1)
                    pool.wait_ge(e_srcP, free(k))
                    pool.sem_inc(passed["pool"], 1)
                    for t in range(TILES):
                        nc.gpsimd.indirect_dma_start(src_rows[:, u, t, :], None, x_state, bass.IndirectOffsetOnAxis(gather_idx[:, u, t:t + 1], 0)).then_inc(s_src[u], DMA)

                with pool.Fori(0, PAIRS_E) as i:
                    for u in range(SLOTS):
                        gather(i, u)

            for u in range(SLOTS):
                pool.wait_ge(s_st[u], L * PAIRS_N * DMA)

            def gather_out(i, u):
                g = i * SLOTS + u
                pool.wait_ge(f_x[u], i * (TILES * DMA))
                pool.sem_inc(passed["pool"], 1)
                nc.gpsimd.tensor_copy(gather_idx[:, u, :], num_idx[:, bass.ds(g, 1), :].rearrange("p a t -> p (a t)")).then_inc(f_idx, 1)
                pool.wait_ge(f_idx, g + 1)
                pool.wait_ge(f_new, free(g))
                pool.sem_inc(passed["pool"], 1)
                for t in range(TILES):
                    nc.gpsimd.indirect_dma_start(x_rows[:, u, t, :], None, x_state, bass.IndirectOffsetOnAxis(gather_idx[:, u, t:t + 1], 0)).then_inc(f_x[u], DMA)

            with pool.Fori(0, PAIRS_N) as i:
                for u in range(SLOTS):
                    gather_out(i, u)

        @block.tensor
        def _(pe):
            for s in (e_srcP, e_dstP, e_h1P, e_h2P, e_h3P, e_sumP, n_xP, n_h1P, n_h2P, n_h3P):
                pe.sem_inc(s, SLOTS)
            pe.wait_ge(s_const, POOL_CONSTS)
            pe.wait_ge(s_cst2, DVE_CONSTS)
            pe.wait_ge(s_dis, 2)
            nc.tensor.matmul(bank[0][0:1, 0:1], disorder[0:GE, :], ones[0:GE, 0:1], start=True, stop=True).then_inc(s_dsum, 1)
            pe.wait_ge(s_vload, 7 * DMA)
            nc.tensor.transpose(bank[1][:, 0:L * VECS], vec_rows[:, :], ident[0:L * VECS, 0:L * VECS]).then_inc(s_vT, 1)

            def columns(b, rows_of, n, signal, step):
                for t in range(TILES):
                    part = rows_of[0:n, t * P:(t + 1) * P] if step == 1 else rows_of[0:n, t:GROUP:TILES]
                    mm = nc.tensor.transpose(bank[b][:, t * n:(t + 1) * n], part, ident[0:n, 0:n])
                mm.then_inc(signal, 1)

            for n, (b, r) in enumerate(((2, g_hi), (3, g_lo), (4, g_src))):
                pe.wait_ge(s_colr, n + 1)
                columns(b, r, GE, s_colP, 1)
            pe.wait_ge(s_run, 3)
            nc.tensor.matmul(bank[5][0:GE, 0:1], after[0:GE, 0:GE], row_sum[0:GE, 0:1], start=True, stop=True).then_inc(s_offP, 1)
            nc.tensor.matmul(bank[6][:, :], zeros_b[:, 0:P], zeros_b[:, :], start=True, stop=False, skip_group_check=True)
            pe.sem_inc(h_P, 1)
            with pe.Fori(0, PAIRS_E) as i:
                for u in range(SLOTS):
                    pe.wait_ge(h_lo, i * SLOTS + u + 1)
                    for t in range(TILES):
                        mm = nc.tensor.matmul(bank[6][:, :], mask_hi[u][:, t, :], mask_lo[u][:, t, :], start=False, stop=False, skip_group_check=True)
                    mm.then_inc(h_P, 1)
            nc.tensor.matmul(bank[6][:, :], zeros_b[:, 0:P], zeros_b[:, :], start=False, stop=True, skip_group_check=True).then_inc(h_all, 1)
            pe.wait_ge(s_rel, 2)
            columns(7, g_rel, GE, s_relP, 1)
            pe.wait_ge(s_node, 3)
            nc.tensor.matmul(bank[0][0:GN, 1:2], after[0:GN, 0:GN], row_sum[0:GN, 1:2], start=True, stop=True)
            nc.tensor.matmul(bank[0][0:GN, 2:3], ones[0:GN, 0:GN], row_sum[0:GN, 1:2], start=True, stop=True).then_inc(s_noffP, 1)
            pe.wait_ge(s_vall, 1)
            pe.wait_ge(s_num, 6)
            columns(1, n_number, GN, s_numP, TILES)
            pe.wait_ge(s_numi, 1)
            pe.wait_ge(s_relc, 1)

            def turn(b, rows_of, u, signal):
                for t in range(TILES):
                    mm = nc.tensor.transpose(b[:, t * P:(t + 1) * P], rows_of[:, u, t, :], ident[:, :])
                mm.then_inc(signal, 1)

            with pe.Fori(0, L) as l:
                pe.wait_ge(s_wts, l + 1)
                pe.sem_inc(passed["pe"], 1)

                def edge(i, u):
                    return (l * PAIRS_E + i) * SLOTS + u

                def src_turn(i, u):
                    k = edge(i, u)
                    pe.wait_ge(s_src[u], (l * PAIRS_E + i + 1) * (TILES * DMA))
                    pe.wait_ge(e_srcT, prev(k))
                    turn(bank[B_SRC], src_rows, u, e_srcP)

                def dst_spread(i, u):
                    k = edge(i, u)
                    pe.wait_ge(s_win[u], (l * PAIRS_E + i + 1) * (TILES * DMA))
                    pe.wait_ge(e_spread, done(k))
                    pe.wait_ge(e_dstT, prev(k))
                    for t in range(TILES):
                        mm = nc.tensor.matmul(bank[B_DST][:, t * P:(t + 1) * P], win_rows[:, u, t, :], spread[:, u, t * P:(t + 1) * P], start=True, stop=True)
                    mm.then_inc(e_dstP, 1)

                def eh1_product(i, u):
                    k = edge(i, u)
                    pe.wait_ge(e_h1b, prev(k))
                    pe.wait_ge(e_srcT, done(k))
                    nc.tensor.matmul(bank[B_H1][:, :], W[:, EW1_SRC, :], srcT[:, u, :], start=True, stop=False)
                    pe.wait_ge(e_dstT, done(k))
                    nc.tensor.matmul(bank[B_H1][:, :], W[:, EW1_DST, :], dstT[:, u, :], start=False, stop=True).then_inc(e_h1P, 1)

                def eh2_product(i, u):
                    k = edge(i, u)
                    pe.wait_ge(e_h1, done(k))
                    pe.wait_ge(e_h2b, prev(k))
                    nc.tensor.matmul(bank[B_H2][:, :], W[:, EW2, :], eh1[:, u, :], start=True, stop=True).then_inc(e_h2P, 1)

                def eh3_product(i, u):
                    k = edge(i, u)
                    pe.wait_ge(e_h2, done(k))
                    pe.wait_ge(e_gain, free(k))
                    for t in range(TILES):
                        mm = nc.tensor.matmul(bank[B_H3 + u][:, t * P:(t + 1) * P], eh2[:, u, t * P:(t + 1) * P], W3c[:, 0, :], start=True, stop=True)
                    mm.then_inc(e_h3P, 1)

                def sum_product(i, u):
                    k = edge(i, u)
                    g = i * SLOTS + u
                    pe.wait_ge(e_sumc, prev(k))
                    nc.tensor.matmul(bank[B_SUM][:, :], zeros_b[:, 0:P], zeros_b[:, :], start=True, stop=False, skip_group_check=True)
                    pe.wait_ge(e_coll, done(k))
                    pe.wait_ge(e_msg, done(k))
                    for t in range(TILES):
                        off = pe.value_load(off_row[0:1, bass.ds(g * TILES + t, 1)], min_val=0, max_val=GROUP - P) if t else 0
                        mm = nc.tensor.matmul(bank[B_SUM][:, bass.ds(off, P)], msg[:, u, t, :], collect[:, u, t, :], start=False, stop=t == TILES - 1, skip_group_check=True)
                    mm.then_inc(e_sumP, 1)

                skewed(pe, GE, [(2, eh1_product), (3, eh2_product), (4, eh3_product), (5, sum_product), (1, dst_spread), (1, src_turn)])
                pe.wait_ge(e_sumc, (l + 1) * GE + SLOTS)
                pe.sem_inc(passed["pe"], 1)

                def node(i, u):
                    return (l * PAIRS_N + i) * SLOTS + u

                def x_turn(i, u):
                    k = node(i, u)
                    pe.wait_ge(s_x[u], (l * PAIRS_N + i + 1) * DMA)
                    pe.wait_ge(n_xT, prev(k))
                    turn(bank[B_SRC], x_rows, u, n_xP)

                def nh1_product(i, u):
                    k = node(i, u)
                    pe.wait_ge(n_h1b, prev(k))
                    pe.wait_ge(n_xT, done(k))
                    nc.tensor.matmul(bank[B_H1][:, :], W[:, NW1_X, :], xT[:, u, :], start=True, stop=False)
                    pe.wait_ge(s_a[u], (l * PAIRS_N + i + 1) * DMA)
                    nc.tensor.matmul(bank[B_H1][:, :].rearrange("c (t p) -> c t p", t=TILES), W[:, NW1_AGG, :], aT[:, u, :].rearrange("c (p t) -> c t p", t=TILES), start=False, stop=True).then_inc(n_h1P, 1)

                def nh2_product(i, u):
                    k = node(i, u)
                    pe.wait_ge(n_h1, done(k))
                    pe.wait_ge(n_h2b, prev(k))
                    nc.tensor.matmul(bank[B_H2][:, :], W[:, NW2, :], nh1[:, u, :], start=True, stop=True).then_inc(n_h2P, 1)

                def nh3_product(i, u):
                    k = node(i, u)
                    pe.wait_ge(n_h2, done(k))
                    pe.wait_ge(n_new, free(k))
                    for t in range(TILES):
                        mm = nc.tensor.matmul(bank[B_H3 + u][:, t * P:(t + 1) * P], nh2[:, u, t * P:(t + 1) * P], W3c[:, 1, :], start=True, stop=True)
                    mm.then_inc(n_h3P, 1)

                skewed(pe, GN, [(2, nh1_product), (3, nh2_product), (4, nh3_product), (1, x_turn)])

        @block.scalar
        def _(act):
            for s in (e_srcT, e_dstT, e_h1b, e_h2b, e_sq, e_sd, e_sumc, n_xT, n_h1b, n_h2b, n_sq, n_sd, f_sd, f_new):
                act.sem_inc(s, SLOTS)
            act.wait_ge(s_const, POOL_CONSTS)
            nc.scalar.dma_start(aggT.rearrange("p (r c) -> p r c", c=C), zeros[:, None, :].to_broadcast([P, NP // C, C])).then_inc(s_azero, DMA)
            act.wait_ge(s_cst2, DVE_CONSTS)
            with act.Fori(0, L) as l:
                act.wait_ge(s_wts, l + 1)
                act.sem_inc(passed["act"], 1)

                def edge(i, u):
                    return (l * PAIRS_E + i) * SLOTS + u

                def src_scale(i, u):
                    k = edge(i, u)
                    act.wait_ge(e_srcP, done(k))
                    act.wait_ge(e_h1P, free(k))
                    nc.scalar.activation(srcT[:, u, :], bank[B_SRC][:, :], ACT.Identity, bias=vecs[:, XB:XB + 1], scale=vecs[:, XG:XG + 1]).then_inc(e_srcT, 1)

                def dst_scale(i, u):
                    k = edge(i, u)
                    act.wait_ge(e_dstP, done(k))
                    act.wait_ge(e_h1P, free(k))
                    nc.scalar.activation(dstT[:, u, :], bank[B_DST][:, :], ACT.Identity, bias=vecs[:, XB:XB + 1], scale=vecs[:, XG:XG + 1]).then_inc(e_dstT, 1)

                def eh1_bias(i, u):
                    k = edge(i, u)
                    act.wait_ge(e_h1P, done(k))
                    act.wait_ge(e_h2P, free(k))
                    nc.scalar.activation(eh1[:, u, :], bank[B_H1][:, :], ACT.Identity, bias=vecs[:, EB1:EB1 + 1]).then_inc(e_h1b, 1)

                def eh2_bias(i, u):
                    k = edge(i, u)
                    act.wait_ge(e_h2P, done(k))
                    act.wait_ge(e_h3P, free(k))
                    nc.scalar.activation(eh2[:, u, :], bank[B_H2][:, :], ACT.Identity, bias=vecs[:, EB2:EB2 + 1]).then_inc(e_h2b, 1)

                def e_square(i, u):
                    k = edge(i, u)
                    act.wait_ge(e_h3P, done(k))
                    act.wait_ge(e_ss, free(k))
                    nc.scalar.activation(slot(esq, u), bank[B_H3 + u][:, :], ACT.Square).then_inc(e_sq, 1)

                def e_deviate(i, u):
                    k = edge(i, u)
                    act.wait_ge(e_ss, done(k))
                    act.wait_ge(e_msg, free(k))
                    nc.scalar.activation(ers[:, u, :], ess[:, u, :], ACT.Sqrt, bias=eps_col[:, :], scale=1.0 / C).then_inc(e_sd, 1)

                def sum_copy(i, u):
                    k = edge(i, u)
                    first = isinstance(i, int) and i == 0 and u == 0
                    act.wait_ge(e_sumP, done(k))
                    act.wait_ge(s_agg, l * (GE * DMA) if first else (k - 1) * DMA)
                    act.wait_ge(e_sum, prev(k))
                    nc.scalar.activation(sums[:, u, 0:GROUP], bank[B_SUM][:, :], ACT.Identity).then_inc(e_sumc, 1)

                skewed(act, GE, [(2, eh1_bias), (3, eh2_bias), (4, e_square), (5, sum_copy), (1, dst_scale), (1, src_scale), (4, e_deviate)])

                def node(i, u):
                    return (l * PAIRS_N + i) * SLOTS + u

                def x_scale(i, u):
                    k = node(i, u)
                    act.wait_ge(n_xP, done(k))
                    act.wait_ge(n_h1P, free(k))
                    nc.scalar.activation(xT[:, u, :], bank[B_SRC][:, :], ACT.Identity, bias=vecs[:, XB:XB + 1], scale=vecs[:, XG:XG + 1]).then_inc(n_xT, 1)

                def nh1_bias(i, u):
                    k = node(i, u)
                    act.wait_ge(n_h1P, done(k))
                    act.wait_ge(n_h2P, free(k))
                    nc.scalar.activation(nh1[:, u, :], bank[B_H1][:, :], ACT.Identity, bias=vecs[:, NB1:NB1 + 1]).then_inc(n_h1b, 1)

                def nh2_bias(i, u):
                    k = node(i, u)
                    act.wait_ge(n_h2P, done(k))
                    act.wait_ge(n_h3P, free(k))
                    nc.scalar.activation(nh2[:, u, :], bank[B_H2][:, :], ACT.Identity, bias=vecs[:, NB2:NB2 + 1]).then_inc(n_h2b, 1)

                def n_square(i, u):
                    k = node(i, u)
                    act.wait_ge(n_h3P, done(k))
                    act.wait_ge(n_ss, free(k))
                    nc.scalar.activation(slot(nsq, u), bank[B_H3 + u][:, :], ACT.Square).then_inc(n_sq, 1)

                def n_deviate(i, u):
                    k = node(i, u)
                    act.wait_ge(n_ss, done(k))
                    act.wait_ge(n_new, free(k))
                    nc.scalar.activation(nrs[:, u, :], nss[:, u, :], ACT.Sqrt, bias=eps_col[:, :], scale=1.0 / C).then_inc(n_sd, 1)

                skewed(act, GN, [(2, nh1_bias), (3, nh2_bias), (4, n_square), (1, x_scale), (4, n_deviate)])

            def f_deviate(i, u):
                g = i * SLOTS + u
                act.wait_ge(f_mv, done(g))
                act.wait_ge(f_new, free(g))
                nc.scalar.activation(nrs[:, u, :], fmv[:, u, :, 1], ACT.Sqrt, bias=eps_col[:, :]).then_inc(f_sd, 1)

            def f_norm(i, u):
                g = i * SLOTS + u
                act.wait_ge(f_ms, done(g))
                act.wait_ge(f_st[u], i * DMA)
                for t in range(TILES):
                    op = nc.scalar.activation(new_rows[:, u, t, :], x_rows[:, u, t, :], ACT.Identity, bias=fshift[:, u, t:t + 1], scale=nrs[:, u, t:t + 1])
                op.then_inc(f_new, 1)

            skewed(act, GN, [(2, f_norm), (1, f_deviate)])

        def rank_edges(dve):
            dve.wait_ge(q_cols, 2 * DMA)
            nc.vector.tensor_copy(dcol_f, dcol_i).then_inc(q_step, 1)
            dve.wait_ge(q_step, 1)
            steps = 1

            def count(c, j):
                dve.wait_ge(q_count, j + c * NT)
                nc.vector.tensor_scalar(chunk_junk, chunk_f, dcol_f[:, bass.ds(j, 1)], None, ALU.is_lt, ALU.add,
                                        accum_out=less(c)[:, bass.ds(j, 1)]).then_inc(q_count, 1)

            for c in range(CHUNKS):
                lo, hi = c * CT, (c + 1) * CT
                dve.wait_ge(q_chunk, (c + 1) * DMA)
                dve.wait_ge(q_used, c)
                nc.vector.tensor_copy(chunk_f, chunk_i).then_inc(q_conv, 1)
                dve.wait_ge(q_conv, c + 1)
                if c:
                    with dve.Fori(0, lo) as j:
                        count(c, j)
                with dve.Fori(lo, hi) as j:
                    at = bass.ds((j - lo) * P, P)
                    count(c, j)
                    nc.vector.tensor_scalar(equal, chunk_f[:, at], dcol_f[:, bass.ds(j, 1)], None, ALU.is_equal).then_inc(q_step, 1)
                    dve.wait_ge(q_step, (j - lo) * 3 + (steps + 1))
                    nc.vector.tensor_tensor(equal_junk, equal, below[:, :], ALU.mult).then_inc(q_step, 1)
                    dve.wait_ge(q_step, (j - lo) * 3 + (steps + 2))
                    nc.vector.reduce_sum(tie[:, bass.ds(j, 1)], equal_junk, AX.X)
                    nc.vector.tensor_scalar(chunk_f[:, at], chunk_f[:, at], -0.5, None, ALU.add).then_inc(q_step, 1)
                    dve.wait_ge(q_step, (j - lo) * 3 + (steps + 3))
                    dve.sem_inc(passed["dve"], 1)
                steps += 3 * CT
                if hi < NT:
                    with dve.Fori(hi, NT) as j:
                        count(c, j)
                dve.wait_ge(q_count, (c + 1) * NT)
                nc.vector.memset(equal, 0.0).then_inc(q_used, 1)
            dve.wait_ge(q_used, CHUNKS)
            nc.vector.tensor_scalar(rank_f, tie, 1.0, None, ALU.add).then_inc(q_step, 1)
            for c in range(CHUNKS):
                dve.wait_ge(q_step, steps + 1 + c)
                nc.vector.tensor_tensor(rank_f, rank_f, less(c), ALU.add).then_inc(q_step, 1)
            dve.wait_ge(q_step, steps + 1 + CHUNKS)
            nc.vector.tensor_copy(rank_i, rank_f).then_inc(q_rank, 1)

        @block.vector
        def _(dve):
            for s in (e_spread, e_h1, e_h2, e_ss, e_rs, e_gain, e_msg, e_coll, e_sum, n_h1, n_h2, n_ss, n_rs, n_new,
                      f_ga, f_sh, f_y, f_bn, f_mv, f_rs, f_ms):
                dve.sem_inc(s, SLOTS)
            nc.vector.memset(vec_rows[:, :], 1.0).then_inc(s_vrow, 1)
            nc.vector.memset(ones[:, :], 1.0).then_inc(s_cst2, 1)
            nc.vector.memset(zeros_b[:, :], 0.0).then_inc(s_cst2, 1)
            nc.vector.memset(eps_col[:, :], EPS).then_inc(s_cst2, 1)
            nc.vector.memset(sums[:, :, :], 0.0).then_inc(s_cst2, 1)
            dve.wait_ge(s_const, POOL_CONSTS)
            nc.vector.tensor_copy(count_h[:, :], count_i[:, :]).then_inc(s_cst2, 1)
            nc.vector.tensor_copy(count_f[:, :], count_i[:, 0:P]).then_inc(s_cst2, 1)
            nc.vector.tensor_copy(part_col[:, :], part_i[:, :]).then_inc(s_cst2, 1)
            nc.vector.tensor_scalar(group_col[:, :], part_i[:, :], float(GROUP), None, ALU.mult).then_inc(s_cst2, 1)
            dve.wait_ge(s_check, 2 * DMA)
            nc.vector.tensor_tensor(g_start[0:GE, :], e_now[0:GE, :], e_prev[0:GE, :], ALU.is_lt).then_inc(s_dis, 1)
            dve.wait_ge(s_dis, 1)
            nc.vector.reduce_max(disorder[0:GE, :], g_start[0:GE, :], AX.X).then_inc(s_dis, 1)
            dve.wait_ge(s_dsum, 1)
            nc.vector.tensor_scalar(unsorted[0:1, 0:1], bank[0][0:1, 0:1], 1.0, None, ALU.min).then_inc(s_flag, 1)
            dve.wait_ge(s_flag, 1)
            is_unsorted = dve.value_load(unsorted[0:1, 0:1], min_val=0, max_val=1)
            with dve.If(is_unsorted != 0):
                rank_edges(dve)
            with dve.Else():
                dve.nop()

            dve.wait_ge(s_edges, 3 * DMA)
            nc.vector.tensor_scalar(g_hi_i[0:GE, :], e_now[0:GE, :], GROUP_BITS, None, ALU.arith_shift_right).then_inc(s_run, 1)
            nc.vector.tensor_scalar(g_lo_i[0:GE, :], e_now[0:GE, :], GROUP - 1, None, ALU.bitwise_and).then_inc(s_run, 1)
            dve.wait_ge(s_run, 2)
            nc.vector.tensor_copy(g_hi[0:GE, :], g_hi_i[0:GE, :]).then_inc(s_colr, 1)
            nc.vector.tensor_copy(g_lo[0:GE, :], g_lo_i[0:GE, :]).then_inc(s_colr, 1)
            nc.vector.tensor_copy(g_src[0:GE, :], e_src[0:GE, :]).then_inc(s_colr, 1)
            nc.vector.tensor_tensor(g_start[0:GE, :], e_now[0:GE, :], e_prev[0:GE, :], ALU.not_equal).then_inc(s_node, 1)
            dve.wait_ge(s_node, 1)
            nc.vector.tensor_tensor_scan(g_run[0:GE, :], ones[0:GE, 0:1].to_broadcast([GE, GROUP]), g_start[0:GE, :], 0.0, ALU.mult, ALU.add).then_inc(s_rel, 1)
            dve.wait_ge(s_rel, 1)
            nc.vector.tensor_copy(row_sum[0:GE, 0:1], g_run[0:GE, GROUP - 1:GROUP]).then_inc(s_run, 1)
            for n, (b, c) in enumerate(((2, hi_cols), (3, lo_cols), (4, src_cols))):
                dve.wait_ge(s_colP, n + 1)
                nc.vector.tensor_copy(c.rearrange("p (g t) -> p t g", t=TILES), bank[b][:, 0:NT].rearrange("p (t g) -> p t g", t=TILES)).then_inc(s_col, 1)
            dve.wait_ge(s_offP, 1)
            nc.vector.tensor_scalar(g_num[0:GE, :], g_run[0:GE, :], bank[5][0:GE, 0:1], -1.0, ALU.add, ALU.add).then_inc(s_tmp, 1)
            dve.wait_ge(s_tmp, 1)
            num_t = g_num[0:GE, :].rearrange("g (t f) -> g t f", t=TILES)
            nc.vector.tensor_tensor(g_rel[0:GE, :].rearrange("g (t f) -> g t f", t=TILES), num_t, num_t[:, :, 0:1].to_broadcast([GE, TILES, P]), ALU.subtract).then_inc(s_rel, 1)
            nc.vector.tensor_copy(base_i[0:GE, :], g_num[0:GE, 0:GROUP:P]).then_inc(s_rel, 1)
            dve.wait_ge(s_rel, 3)
            nc.vector.tensor_copy(rel_b[0:GE, :], g_rel[0:GE, :]).then_inc(s_rel, 1)

            dve.wait_ge(s_col, 3)
            with dve.Fori(0, PAIRS_E) as i:
                for u in range(SLOTS):
                    g = i * SLOTS + u
                    dve.wait_ge(h_P, free(g) - 1)
                    for t in range(TILES):
                        at = bass.ds(g * TILES + t, 1)
                        nc.vector.tensor_scalar(mask_lo[u][:, t, :], count_h[:, :], lo_cols[:, at], None, ALU.is_equal)
                        op = nc.vector.tensor_scalar(mask_hi[u][:, t, :], count_h[:, 0:P], hi_cols[:, at], None, ALU.is_equal)
                    op.then_inc(h_lo, 1)
            dve.wait_ge(h_all, 1)
            nc.vector.tensor_scalar(n_has[0:GN, :], bank[6][0:GN, :], 1.0, None, ALU.min).then_inc(s_tmp, 1)
            dve.wait_ge(s_tmp, 2)
            nc.vector.tensor_tensor_scan(n_run[0:GN, :], ones[0:GN, 0:1].to_broadcast([GN, GROUP]), n_has[0:GN, :], 0.0, ALU.mult, ALU.add).then_inc(s_node, 1)
            dve.wait_ge(s_node, 2)
            nc.vector.tensor_copy(row_sum[0:GN, 1:2], n_run[0:GN, GROUP - 1:GROUP]).then_inc(s_node, 1)
            dve.wait_ge(s_noffP, 1)
            nc.vector.scalar_tensor_tensor(n_b[0:GN, :], n_run[0:GN, :], bank[0][0:GN, 1:2], n_has[0:GN, :], ALU.add, ALU.subtract).then_inc(s_num, 1)
            nc.vector.tensor_scalar(n_a[0:GN, :], count_i[0:GN, :], bank[0][0:GN, 2:3], group_col[0:GN, :], ALU.add, ALU.add).then_inc(s_num, 1)
            dve.wait_ge(s_num, 2)
            nc.vector.tensor_tensor(n_a[0:GN, :], n_a[0:GN, :], n_b[0:GN, :], ALU.subtract).then_inc(s_num, 1)
            dve.wait_ge(s_num, 3)
            nc.vector.tensor_tensor(n_b[0:GN, :], n_b[0:GN, :], n_a[0:GN, :], ALU.subtract).then_inc(s_num, 1)
            dve.wait_ge(s_num, 4)
            nc.vector.tensor_tensor(n_b[0:GN, :], n_b[0:GN, :], n_has[0:GN, :], ALU.mult).then_inc(s_num, 1)
            dve.wait_ge(s_num, 5)
            nc.vector.tensor_tensor(n_number[0:GN, :], n_a[0:GN, :], n_b[0:GN, :], ALU.add).then_inc(s_num, 1)
            dve.wait_ge(s_num, 6)
            nc.vector.tensor_copy(number_i[0:GN, :], n_number[0:GN, :]).then_inc(s_num, 1)
            dve.wait_ge(s_baser, DMA)
            nc.vector.tensor_copy(base_f, base_row[0:1, :]).then_inc(s_tmp, 1)
            dve.wait_ge(s_tmp, 3)
            base_g = base_f.rearrange("a (g t) -> a g t", t=TILES)
            nc.vector.tensor_tensor(off_row[0:1, :].rearrange("a (g t) -> a g t", t=TILES), base_g, base_g[:, :, 0:1].to_broadcast([1, GE, TILES]), ALU.subtract).then_inc(s_rows, 1)
            nc.vector.memset(step_row[0:1, 0:1], 0).then_inc(s_rows, 1)
            nc.vector.tensor_tensor(step_row[0:1, 1:GE], base_g[:, 1:GE, 0], base_g[:, 0:GE - 1, 0], ALU.subtract).then_inc(s_rows, 1)
            dve.wait_ge(s_rows, 3)
            nc.vector.memset(base_f, 0.0).then_inc(s_tmp, 1)
            dve.wait_ge(s_vT, 1)
            nc.vector.tensor_copy(vecs_all[:, :], bank[1][:, 0:L * VECS]).then_inc(s_vall, 1)
            dve.wait_ge(s_relP, 1)
            nc.vector.tensor_copy(rel_cols[:, :].rearrange("p (g t) -> p t g", t=TILES), bank[7][:, 0:NT].rearrange("p (t g) -> p t g", t=TILES)).then_inc(s_relc, 1)
            dve.wait_ge(s_numP, 1)
            nc.vector.tensor_copy(num_idx[:, :, :].rearrange("p g t -> p t g"), bank[1][:, 0:TILES * GN].rearrange("p (t g) -> p t g", t=TILES)).then_inc(s_numi, 1)
            dve.wait_ge(p_put[SLOTS - 1], (PAIRS_N - 1) * TILES * DMA)
            nc.vector.memset(x_rows[:, SLOTS - 1, :, :], 0.0).then_inc(p_clear, 1)
            dve.wait_ge(s_rela, DMA)
            dve.wait_ge(s_relc, 1)
            dve.wait_ge(m_put, GE + 1)

            with dve.Fori(0, L) as l:
                dve.wait_ge(s_wload, (l + 1) * (8 * DMA))
                dve.sem_inc(passed["dve"], 1)
                nc.vector.tensor_copy(vecs[:, :], vecs_all[:, bass.ds(l * VECS, VECS)]).then_inc(s_wmean, 1)
                for n, k in enumerate((EW3, NW3)):
                    nc.vector.reduce_sum(w3_mean[:, n:n + 1], W[:, k, :], AX.X).then_inc(s_wmean, 1)
                dve.wait_ge(s_wmean, l * 4 + 3)
                nc.vector.tensor_scalar(w3_mean[:, :], w3_mean[:, :], 1.0 / C, None, ALU.mult).then_inc(s_wmean, 1)
                dve.wait_ge(s_wmean, l * 4 + 4)
                nc.vector.tensor_scalar(W3c[:, 0, :], W[:, EW3, :], w3_mean[:, 0:1], None, ALU.subtract)
                nc.vector.tensor_scalar(W3c[:, 1, :], W[:, NW3, :], w3_mean[:, 1:2], None, ALU.subtract).then_inc(s_wts, 1)
                dve.wait_ge(s_wts, l + 1)
                dve.sem_inc(passed["dve"], 1)

                def edge(i, u):
                    return (l * PAIRS_E + i) * SLOTS + u

                def make_spread(i, u):
                    k = edge(i, u)
                    dve.wait_ge(e_dstP, free(k))
                    nc.vector.tensor_scalar(spread[:, u, :], rel_all[:, bass.ds((i * SLOTS + u) * GROUP, GROUP)], part_col[:, :], None, ALU.is_equal).then_inc(e_spread, 1)

                def make_collect(i, u):
                    k = edge(i, u)
                    dve.wait_ge(e_sumP, free(k))
                    at = rel_cols[:, bass.ds((i * SLOTS + u) * TILES, TILES)]
                    nc.vector.tensor_tensor(collect[:, u, :, :], count_f[:, None, :].to_broadcast([P, TILES, P]), at[:, :, None].to_broadcast([P, TILES, P]), ALU.is_equal).then_inc(e_coll, 1)

                def eh1_slope(i, u):
                    k = edge(i, u)
                    dve.wait_ge(e_h1b, done(k))
                    nc.vector.scalar_tensor_tensor(eh1[:, u, :], eh1[:, u, :], SLOPE, eh1[:, u, :], ALU.mult, ALU.max).then_inc(e_h1, 1)

                def eh2_slope(i, u):
                    k = edge(i, u)
                    dve.wait_ge(e_h2b, done(k))
                    nc.vector.scalar_tensor_tensor(eh2[:, u, :], eh2[:, u, :], SLOPE, eh2[:, u, :], ALU.mult, ALU.max).then_inc(e_h2, 1)

                def e_square_sum(i, u):
                    k = edge(i, u)
                    dve.wait_ge(e_sq, done(k))
                    dve.wait_ge(e_sd, free(k))
                    nc.vector.reduce_sum(ess[:, u, :], esq[:, u, :, :], AX.X).then_inc(e_ss, 1)

                def e_gained(i, u):
                    k = edge(i, u)
                    dve.wait_ge(e_sumP, free(k))
                    dve.wait_ge(e_sq, done(k))
                    nc.vector.tensor_tensor(msg[:, u, :, :], bank[B_H3 + u][:, :].rearrange("p (t c) -> p t c", t=TILES), msg_gain[:, None, :].to_broadcast([P, TILES, C]), ALU.mult).then_inc(e_gain, 1)

                def e_message(i, u):
                    k = edge(i, u)
                    dve.wait_ge(e_sd, done(k))
                    nc.vector.reciprocal(ers[:, u, :], ers[:, u, :]).then_inc(e_rs, 1)
                    dve.wait_ge(e_rs, done(k))
                    dve.wait_ge(e_gain, done(k))
                    for t in range(TILES):
                        op = nc.vector.scalar_tensor_tensor(msg[:, u, t, :], msg[:, u, t, :], ers[:, u, t:t + 1], msg_shift[:, :], ALU.mult, ALU.add)
                    op.then_inc(e_msg, 1)

                def carry(i, u):
                    k = edge(i, u)
                    step = dve.value_load(step_row[0:1, bass.ds(i * SLOTS + u, 1)], min_val=0, max_val=GROUP)
                    dve.wait_ge(e_sumc, done(k))
                    dve.wait_ge(e_sum, prev(k))
                    if isinstance(i, int) and i == 0 and u == 0:
                        nc.vector.tensor_scalar(sums[:, u, 0:1], sums[:, u, 0:1], 0.0, None, ALU.add).then_inc(e_sum, 1)
                    else:
                        nc.vector.tensor_tensor(sums[:, u, 0:1], sums[:, u, 0:1], sums[:, 1 - u, bass.ds(step, 1)], ALU.add).then_inc(e_sum, 1)

                skewed(dve, GE, [(2, eh1_slope), (3, eh2_slope), (0, make_spread), (4, make_collect), (4, e_square_sum),
                                 (4, e_gained), (5, carry), (4, e_message)])

                def node(i, u):
                    return (l * PAIRS_N + i) * SLOTS + u

                def nh1_slope(i, u):
                    k = node(i, u)
                    dve.wait_ge(n_h1b, done(k))
                    nc.vector.scalar_tensor_tensor(nh1[:, u, :], nh1[:, u, :], SLOPE, nh1[:, u, :], ALU.mult, ALU.max).then_inc(n_h1, 1)

                def nh2_slope(i, u):
                    k = node(i, u)
                    dve.wait_ge(n_h2b, done(k))
                    nc.vector.scalar_tensor_tensor(nh2[:, u, :], nh2[:, u, :], SLOPE, nh2[:, u, :], ALU.mult, ALU.max).then_inc(n_h2, 1)

                def n_square_sum(i, u):
                    k = node(i, u)
                    dve.wait_ge(n_sq, done(k))
                    dve.wait_ge(n_sd, free(k))
                    nc.vector.reduce_sum(nss[:, u, :], nsq[:, u, :, :], AX.X).then_inc(n_ss, 1)

                def n_rows(i, u):
                    k = node(i, u)
                    dve.wait_ge(n_sd, done(k))
                    nc.vector.reciprocal(nrs[:, u, :], nrs[:, u, :]).then_inc(n_rs, 1)
                    dve.wait_ge(n_rs, done(k))
                    dve.wait_ge(s_st[u], (l * PAIRS_N + i) * DMA)
                    nc.vector.tensor_tensor(new_rows[:, u, :, :], bank[B_H3 + u][:, :].rearrange("p (t c) -> p t c", t=TILES),
                                            nrs[:, u, :, None].to_broadcast([P, TILES, C]), ALU.mult).then_inc(n_new, 1)

                skewed(dve, GN, [(2, nh1_slope), (3, nh2_slope), (4, n_square_sum), (4, n_rows)])

            dve.wait_ge(s_gb, 2 * DMA)

            def f_sum(i, u):
                g = i * SLOTS + u
                dve.wait_ge(f_x[u], (i + 1) * (TILES * DMA))
                nc.vector.tensor_tensor(x_rows[:, u, :, :], x_rows[:, u, :, :], out_gain[:, None, :].to_broadcast([P, TILES, C]), ALU.mult).then_inc(f_ga, 1)
                dve.wait_ge(f_r[u], (i + 1) * DMA)
                nc.vector.tensor_tensor(win_rows[:, u, :, :], win_rows[:, u, :, :], out_shift[:, None, :].to_broadcast([P, TILES, C]), ALU.add).then_inc(f_sh, 1)
                dve.wait_ge(f_ga, done(g))
                dve.wait_ge(f_sh, done(g))
                nc.vector.tensor_tensor(x_rows[:, u, :, :], x_rows[:, u, :, :], win_rows[:, u, :, :], ALU.add).then_inc(f_y, 1)
                dve.wait_ge(f_y, done(g))
                for t in range(TILES):
                    op = nc.vector.bn_stats(fstat[:, u, t, :], x_rows[:, u, t, :])
                op.then_inc(f_bn, 1)
                dve.wait_ge(f_bn, done(g))
                dve.wait_ge(f_sd, free(g))
                dve.sem_inc(passed["dve"], 1)
                for t in range(TILES):
                    op = nc.vector.bn_aggr(fmv[:, u, t, :], fstat[:, u, t, :])
                op.then_inc(f_mv, 1)

            def f_shifts(i, u):
                g = i * SLOTS + u
                dve.wait_ge(f_sd, done(g))
                nc.vector.reciprocal(nrs[:, u, :], nrs[:, u, :]).then_inc(f_rs, 1)
                dve.wait_ge(f_rs, done(g))
                nc.vector.scalar_tensor_tensor(fshift[:, u, :], fmv[:, u, :, 0], -1.0, nrs[:, u, :], ALU.mult, ALU.mult).then_inc(f_ms, 1)

            skewed(dve, GN, [(1, f_sum), (2, f_shifts)])


_INS = ["x", "src", "dst"] + [f"L0_gnn_{n}" for n in ("eW1", "eb1", "eW2", "eb2", "eW3", "eg", "ebt", "nW1", "nb1", "nW2", "nb2", "nW3", "ng", "nbt")]


def kernel(**inputs):
    import numpy as np
    import concourse.bacc as bacc
    from concourse.bass_utils import run_bass_kernel_spmd

    nc = bacc.Bacc("TRN2", target_bir_lowering=False, num_devices=1)
    arrays, args = {}, []
    for name in _INS:
        a = np.ascontiguousarray(inputs[name])
        arrays[f"in_{name}"] = a
        args.append(nc.dram_tensor(f"in_{name}", a.shape, mybir.dt.from_np(a.dtype), kind="ExternalInput").ap())
    out = nc.dram_tensor("out_0", inputs["x"].shape, F32, kind="ExternalOutput").ap()
    gnn_kernel(nc, *args, out)
    r = run_bass_kernel_spmd(nc, [arrays], core_ids=[0])
    return r.results[0]["out_0"]
```

```python
from contextlib import ExitStack

import concourse.bass as bass
from concourse import mybir
from concourse.alu_op_type import AluOpType as ALU

ACT = mybir.ActivationFunctionType
F32 = mybir.dt.float32
BF16 = mybir.dt.bfloat16
F16 = mybir.dt.float16
I32 = mybir.dt.int32
AX = mybir.AxisListType

P = 128
TILES = 4
GROUP = P * TILES
GROUP_BITS = 9
SLOTS = 2
EPS = 1e-5
SLOPE = 0.2
DMA = 16
EB1, EB2, NB1, NB2, XG, XB = range(6)
VECS = 8
POOL_CONSTS, DVE_CONSTS = 11, 8
EW1_DST, EW1_SRC, EW2, EW3, NW1_X, NW1_AGG, NW2, NW3 = range(8)


def done(k):
    return k + 1 + SLOTS


def prev(k):
    return k + SLOTS


def free(k):
    return k + 1


def over(rounds, size=DMA):
    return (rounds + 1) * size


def skewed(eng, groups, stages, apart=0):
    deepest = max(lag for lag, _ in stages)
    pairs = groups // SLOTS

    def steps(i, always):
        for u in range(SLOTS):
            for lag, fn in stages:
                if always or 0 <= i * SLOTS + u - lag < groups:
                    fn(i + (u - lag) // SLOTS, (u - lag) % SLOTS)

    first = max(-(-deepest // SLOTS), apart)
    assert first < pairs
    for i in range(first):
        steps(i, False)
    with eng.Fori(first, pairs) as i:
        steps(i, True)
    for i in range(pairs, pairs - (-deepest // SLOTS)):
        steps(i, False)


def gnn_kernel(nc, x, src, dst, eW1, eb1, eW2, eb2, eW3, eg, ebt, nW1, nb1, nW2, nb2, nW3, ng, nbt, out):
    N, C = x.shape
    E = src.shape[0]
    L = eW2.shape[0]
    assert L >= 3
    assert C == P and GROUP == 1 << GROUP_BITS
    GE = -(-E // (SLOTS * GROUP)) * SLOTS
    GN = -(-N // (SLOTS * GROUP)) * SLOTS
    EP, NP = GE * GROUP, GN * GROUP
    PAIRS_E, PAIRS_N = GE // SLOTS, GN // SLOTS
    NT = GE * TILES
    PADS = max(EP - E, 1)
    assert GE <= P and GN <= P and EP <= NP and NP > N
    LAST_ROWS = N - (GN - 1) * GROUP
    assert 0 < LAST_ROWS and LAST_ROWS % TILES == 0
    LAST_P = LAST_ROWS // TILES
    CHUNKS = next(c for c in range(6, NT + 1) if NT % c == 0)
    CW, CT = EP // CHUNKS, NT // CHUNKS

    def scratch(name, shape, dt):
        return nc.dram_tensor(name, shape, dt, kind="Internal").ap()

    x_perm = scratch("x_perm", [NP, C], F32)
    x_state = scratch("x_state", [NP, C], F32)
    aggT = scratch("aggT", [P, NP], F32)
    dst_sorted = scratch("dst_sorted", [EP + 2, 1], I32)
    src_sorted = scratch("src_sorted", [EP + 2, 1], I32)
    rel_dram = scratch("rel_dram", [GE, GROUP], BF16)
    base_dram = scratch("base_dram", [GE, TILES], I32)
    number_dram = scratch("number_dram", [NP, 1], I32)
    old_dram = scratch("old_dram", [NP, 1], I32)

    x_in_groups = x[0:(GN - 1) * GROUP, :].rearrange("(g p t) c -> g p (t c)", p=P, t=TILES)
    x_in_last = x[(GN - 1) * GROUP:N, :].rearrange("(p t) c -> p (t c)", t=TILES)

    with ExitStack() as ctx:
        def sb(name, shape, dt=F32):
            return ctx.enter_context(nc.sbuf_tensor(name, shape, dt))

        def sem(name):
            return ctx.enter_context(nc.semaphore(name))

        def sems(name):
            return [sem(f"{name}{u}") for u in range(SLOTS)]

        ident = sb("ident", [P, P])
        below = sb("below", [P, P])
        after = sb("after", [P, P])
        ones = sb("ones", [P, P])
        group_col = sb("group_col", [P, 1])
        zeros = sb("zeros", [P, C])
        zeros_b = sb("zeros_b", [P, GROUP], BF16)
        eps_col = sb("eps_col", [P, 1])
        part_col = sb("part_col", [P, 1])
        part_i = sb("part_i", [P, 1], I32)
        count_i = sb("count_i", [P, GROUP], I32)
        count_h = sb("count_h", [P, GROUP], F16)
        count_f = sb("count_f", [P, P])
        pad_dst = sb("pad_dst", [1, PADS], I32)
        pad_src = sb("pad_src", [1, PADS], I32)
        pad_ends = sb("pad_ends", [1, 1], I32)
        vec_rows = sb("vec_rows", [L * VECS, C])
        vecs_all = sb("vecs_all", [P, L * VECS])
        vecs = sb("vecs", [P, VECS])
        W = sb("W", [P, 8, C])
        W3c = sb("W3c", [P, 2, C])
        w3_mean = sb("w3_mean", [P, 2])
        msg_gain = sb("msg_gain", [P, C])
        msg_shift = sb("msg_shift", [P, C])
        out_gain = sb("out_gain", [P, C])
        out_shift = sb("out_shift", [P, C])
        e_now = sb("e_now", [P, GROUP], I32)
        e_prev = sb("e_prev", [P, GROUP], I32)
        e_src = sb("e_src", [P, GROUP], I32)
        disorder = sb("disorder", [P, 1])
        unsorted = sb("unsorted", [1, 1], I32)
        row_sum = sb("row_sum", [P, 2])
        base_i = sb("base_i", [P, TILES], I32)
        base_row = sb("base_row", [1, NT], I32)
        off_row = sb("off_row", [1, NT], I32)
        step_row = sb("step_row", [1, GE], I32)
        src_idx = sb("src_idx", [P, GE, TILES], I32)
        num_idx = sb("num_idx", [P, GN, TILES], I32)
        rel_cols = sb("rel_cols", [P, NT])
        rel_all = sb("rel_all", [P, EP], BF16)
        gather_idx = sb("gather_idx", [P, SLOTS, TILES], I32)
        new_idx = sb("new_idx", [P, SLOTS, TILES], I32)
        src_rows = sb("src_rows", [P, SLOTS, TILES, C])
        win_rows = sb("win_rows", [P, SLOTS, TILES, C])
        spread = sb("spread", [P, SLOTS, GROUP])
        collect = sb("collect", [P, SLOTS, TILES, P])
        srcT = sb("srcT", [P, SLOTS, GROUP])
        dstT = sb("dstT", [P, SLOTS, GROUP])
        eh1 = sb("eh1", [P, SLOTS, GROUP])
        eh2 = sb("eh2", [P, SLOTS, GROUP])
        esq = sb("esq", [P, SLOTS, TILES, C])
        msg = sb("msg", [P, SLOTS, TILES, C])
        ess = sb("ess", [P, SLOTS, TILES])
        ers = sb("ers", [P, SLOTS, TILES])
        sums = sb("sums", [P, SLOTS, GROUP + 1])
        x_rows = sb("x_rows", [P, SLOTS, TILES, C])
        aT = sb("aT", [P, SLOTS, GROUP])
        xT = sb("xT", [P, SLOTS, GROUP])
        nh1 = sb("nh1", [P, SLOTS, GROUP])
        nh2 = sb("nh2", [P, SLOTS, GROUP])
        nsq = sb("nsq", [P, SLOTS, TILES, C])
        new_rows = sb("new_rows", [P, SLOTS, TILES, C])
        nss = sb("nss", [P, SLOTS, TILES])
        nrs = sb("nrs", [P, SLOTS, TILES])
        fstat = sb("fstat", [P, SLOTS, TILES, 6])
        fmv = sb("fmv", [P, SLOTS, TILES, 2])
        fshift = sb("fshift", [P, SLOTS, TILES])
        frs = sb("frs", [P, SLOTS, TILES])
        node_ids = sb("node_ids", [P, SLOTS, TILES], I32)

        bank = [ctx.enter_context(nc.psum_tensor(f"bank{b}", [P, GROUP], F32)) for b in range(8)]
        B_SRC, B_DST, B_H1, B_H2, B_H3, B_SUM = 0, 1, 2, 3, 4, 6

        s_const = sem("pool_constants")
        s_cst2 = sem("dve_constants")
        passed = {e: sem(f"{e}_passed") for e in ("sp", "pool", "pe", "act", "dve")}
        s_pads = sem("pads_made")
        s_raw = sem("edges_copied")
        s_check = sem("check_loaded")
        s_dis = sem("disorder_counted")
        s_dsum = sem("disorder_summed")
        s_flag = sem("flag_made")
        s_edges = sem("edges_loaded")
        s_colr = sem("columns_rows_ready")
        s_colP = sem("columns_turned")
        s_col = sem("columns_made")
        s_run = sem("edge_scan")
        s_tmp = sem("numbering_step")
        s_offP = sem("edge_offsets")
        s_rel = sem("edge_numbers")
        s_reld = sem("rel_in_dram")
        s_rela = sem("rel_spread")
        s_based = sem("base_in_dram")
        s_baser = sem("base_row_loaded")
        s_rows = sem("row_tables")
        s_relP = sem("rel_turned")
        s_relc = sem("rel_columns")
        h_lo = sem("histogram_masks")
        h_P = sem("histogram_tiles")
        h_all = sem("histogram_over")
        s_node = sem("node_scan")
        s_noffP = sem("node_offsets")
        s_num = sem("node_numbers")
        s_numd = sem("numbers_in_dram")
        s_numP = sem("numbers_turned")
        s_numi = sem("number_table")
        s_vrow = sem("vec_rows_set")
        s_vload = sem("vec_rows_loaded")
        s_vT = sem("vecs_turned")
        s_vall = sem("vecs_all_made")
        s_azero = sem("aggT_zeroed")
        s_gb = sem("out_gain_shift_loaded")
        m_stage = sem("remap_staged")
        m_got = sems("remap_gathered")
        m_put = sem("remap_kept")
        p_x = sems("perm_x_loaded")
        p_clear = sem("perm_pads_cleared")
        p_stage = sem("perm_staged")
        p_put = sems("perm_scattered")
        q_cols = sem("sort_columns_loaded")
        q_chunk = sem("sort_chunk_loaded")
        q_conv = sem("sort_chunk_converted")
        q_used = sem("sort_chunk_used")
        q_step = sem("sort_step")
        q_count = sem("sort_tiles_counted")
        q_rank = sem("sort_ranks_made")
        q_copy = sem("sort_staged")
        q_put = sem("sort_scattered")
        s_wload = sem("weights_loaded")
        s_wmean = sem("w3_means")
        s_wts = sem("weights_ready")
        s_gidx = sem("gather_idx_staged")
        s_src = sems("src_rows_gathered")
        s_win = sems("win_rows_loaded")
        s_agg = sem("sums_stored")
        e_srcP, e_srcT = sem("e_src_turned"), sem("e_src_scaled")
        e_spread, e_dstP, e_dstT = sem("e_spread"), sem("e_dst_spread"), sem("e_dst_scaled")
        e_h1P, e_h1b, e_h1 = sem("e_h1_product"), sem("e_h1_biased"), sem("e_h1_ready")
        e_h2P, e_h2b, e_h2 = sem("e_h2_product"), sem("e_h2_biased"), sem("e_h2_ready")
        e_h3P, e_sq, e_ss, e_sd = sem("e_h3_product"), sem("e_squares"), sem("e_square_sums"), sem("e_deviation")
        e_rs, e_gain, e_msg, e_coll = sem("e_rsd"), sem("e_gained"), sem("e_message"), sem("e_collect")
        e_sumP, e_sumc, e_sum = sem("e_sum_product"), sem("e_sum_copied"), sem("e_sum_carried")
        s_x, s_a, s_st = sems("x_rows_loaded"), sems("aT_loaded"), sems("new_rows_stored")
        n_xP, n_xT = sem("n_x_turned"), sem("n_x_scaled")
        n_h1P, n_h1b, n_h1 = sem("n_h1_product"), sem("n_h1_biased"), sem("n_h1_ready")
        n_h2P, n_h2b, n_h2 = sem("n_h2_product"), sem("n_h2_biased"), sem("n_h2_ready")
        n_h3P, n_sq, n_ss, n_sd = sem("n_h3_product"), sem("n_squares"), sem("n_square_sums"), sem("n_deviation")
        n_rs, n_new = sem("n_rsd"), sem("n_new_rows")
        v_stage, v_put, v_ids, v_table = sem("old_staged"), sems("old_scattered"), sem("node_ids_stepped"), sem("old_table_loaded")
        f_r, f_sh, f_y, f_bn, f_mv = sems("f_residual_loaded"), sem("f_shifted"), sem("f_summed"), sem("f_stats"), sem("f_mean_var")
        f_sd, f_rs, f_ms, f_new = sem("f_deviation"), sem("f_rsd"), sem("f_mean_shift"), sem("f_rows")
        f_idx, f_put, f_out = sem("f_idx_staged"), sems("f_out_scattered"), sem("f_out_over")

        block = ctx.enter_context(nc.Block())

        def whole(b):
            return b[:, :, :].rearrange("p s f -> p (s f)") if len(b.shape) == 3 else b[:, :, :, :].rearrange("p s t c -> p (s t c)")

        sort_room = rel_all[:, :].bitcast(F32)
        chunk_f = sort_room[:, 0:CW]
        chunk_i = sort_room[:, CW:2 * CW].bitcast(I32)
        chunk_junk = sort_room[:, 2 * CW:3 * CW]
        dcol_f, dcol_i, scol_i = whole(srcT)[:, 0:NT], whole(dstT)[:, 0:NT].bitcast(I32), whole(eh1)[:, 0:NT].bitcast(I32)
        tie, rank_f, rank_i = whole(eh2)[:, 0:NT], whole(esq)[:, 0:NT], whole(spread)[:, 0:NT].bitcast(I32)
        equal, equal_junk = whole(msg)[:, 0:P], whole(msg)[:, P:2 * P]
        PER = SLOTS * GROUP // NT
        sort_counts = [whole(x_rows), whole(aT), whole(xT), whole(nh1), whole(nh2)]
        assert CHUNKS <= PER * len(sort_counts)

        def less(c):
            return sort_counts[c // PER][:, (c % PER) * NT:(c % PER + 1) * NT]

        st_rank, st_dst, st_src = gather_idx[:, 0, 0:1], gather_idx[:, 0, 1:2], gather_idx[:, 0, 2:3]

        rows = [whole(b)[:, s * GROUP:(s + 1) * GROUP] for b in (nh1, nh2, nsq, new_rows, aT, xT) for s in range(SLOTS)]
        g_start, g_run, g_num, g_rel, g_hi, g_lo, g_src, n_has, n_run, n_a, n_b, n_number = rows
        g_hi_i, g_lo_i = whole(collect)[:, 0:GROUP].bitcast(I32), whole(collect)[:, GROUP:2 * GROUP].bitcast(I32)
        number_i = whole(spread)[:, 0:GROUP].bitcast(I32)
        rel_b = whole(spread)[:, GROUP:GROUP + GROUP // 2].bitcast(BF16)
        base_f = whole(sums)[0:1, 0:NT]
        row_f = whole(sums)[0:1, NT:2 * NT]
        hi_cols, lo_cols = whole(srcT)[:, 0:NT], whole(dstT)[:, 0:NT]
        mask_lo = [whole(b).bitcast(BF16).rearrange("p (t f) -> p t f", t=TILES) for b in (eh2, esq)]
        mask_hi = [whole(msg)[:, s * GROUP // 2:(s + 1) * GROUP // 2].bitcast(BF16)[:, 0:TILES * P].rearrange("p (t f) -> p t f", t=TILES) for s in range(SLOTS)]

        def edge_rows(a, shift):
            return a[shift:shift + EP, :].rearrange("(g f) o -> g (f o)", f=GROUP)

        def slot(b, u):
            return b[:, u, :, :].rearrange("p t c -> p (t c)")

        def group_of(a, g):
            return a[bass.ds(g, 1), :, :].rearrange("a p f -> p (a f)")

        @block.sync
        def _(sp):
            sp.sem_inc(s_agg, 2 * DMA)
            for s in s_st:
                sp.sem_inc(s, DMA)
            sp.wait_ge(s_pads, 3)
            sp.dma_start(dst_sorted[1:1 + E, :].rearrange("(a e) o -> a (e o)", a=16), dst.rearrange("(a e) -> a e", a=16)).then_inc(s_raw, DMA)
            sp.dma_start(src_sorted[1:1 + E, :].rearrange("(a e) o -> a (e o)", a=16), src.rearrange("(a e) -> a e", a=16)).then_inc(s_raw, DMA)
            raw = 2
            for a, pads in ((dst_sorted, pad_dst), (src_sorted, pad_src)):
                if EP > E:
                    sp.dma_start(a[1 + E:1 + EP, :].rearrange("(a n) o -> a (n o)", a=1), pads[:, :]).then_inc(s_raw, DMA)
                    raw += 1
                for at in (0, EP + 1):
                    sp.dma_start(a[at:at + 1, :], pad_ends[0:1, 0:1]).then_inc(s_raw, DMA)
                    raw += 1
            sp.wait_ge(s_raw, DMA * raw)
            sp.dma_start(e_now[0:GE, :], edge_rows(dst_sorted, 1)).then_inc(s_check, DMA)
            sp.dma_start(e_prev[0:GE, :], edge_rows(dst_sorted, 0)).then_inc(s_check, DMA)
            sp.dma_start(out_gain[:, :], ng[L - 1:L, :].to_broadcast([P, C])).then_inc(s_gb, DMA)
            sp.dma_start(out_shift[:, :], nbt[L - 1:L, :].to_broadcast([P, C])).then_inc(s_gb, DMA)
            sp.wait_ge(s_vrow, 1)
            sp.wait_ge(s_const, POOL_CONSTS)
            for k, v in ((EB1, eb1), (EB2, eb2), (NB1, nb1), (NB2, nb2)):
                sp.dma_start(vec_rows[k:L * VECS:VECS, :], v).then_inc(s_vload, DMA)
            for k, v in ((XG, ng), (XB, nbt)):
                sp.dma_start(vec_rows[VECS + k:L * VECS:VECS, :], v[0:L - 1, :]).then_inc(s_vload, DMA)
            sp.dma_start(vec_rows[XB:XB + 1, :], zeros[0:1, :]).then_inc(s_vload, DMA)
            sp.wait_ge(s_flag, 1)
            is_unsorted = sp.value_load(unsorted[0:1, 0:1], min_val=0, max_val=1)
            with sp.If(is_unsorted != 0):
                with nc.allow_non_contiguous_dma("the sort's columns; a path seldom taken"):
                    sp.dma_start(dcol_i, dst_sorted[1:1 + EP, :].rearrange("(j p) o -> p (j o)", p=P)).then_inc(q_cols, DMA)
                    sp.dma_start(scol_i, src_sorted[1:1 + EP, :].rearrange("(j p) o -> p (j o)", p=P)).then_inc(q_cols, DMA)
                for c in range(CHUNKS):
                    if c:
                        sp.wait_ge(q_conv, c)
                    row = dst_sorted[1 + c * CW:1 + (c + 1) * CW, :].rearrange("(a n) o -> a (n o)", a=1)
                    sp.dma_start(chunk_i, row.to_broadcast([P, CW])).then_inc(q_chunk, DMA)
                sp.wait_ge(q_put, NT * (2 * DMA))
            with sp.Else():
                sp.nop()
            sp.wait_ge(s_dis, 2)
            sp.dma_start(e_now[0:GE, :], edge_rows(dst_sorted, 1)).then_inc(s_edges, DMA)
            sp.dma_start(e_prev[0:GE, :], edge_rows(dst_sorted, 0)).then_inc(s_edges, DMA)
            sp.dma_start(e_src[0:GE, :], edge_rows(src_sorted, 1)).then_inc(s_edges, DMA)
            sp.wait_ge(s_rel, 4)
            sp.dma_start(rel_dram, rel_b[0:GE, :]).then_inc(s_reld, DMA)
            sp.dma_start(base_dram, base_i[0:GE, :]).then_inc(s_based, DMA)
            sp.wait_ge(s_based, DMA)
            sp.dma_start(base_row[0:1, :], base_dram.rearrange("(a g) t -> a (g t)", a=1)).then_inc(s_baser, DMA)
            sp.wait_ge(s_reld, DMA)
            sp.dma_start(rel_all[:, :], rel_dram.rearrange("(a g) f -> a (g f)", a=1).to_broadcast([P, EP])).then_inc(s_rela, DMA)
            sp.wait_ge(s_num, 7)
            sp.dma_start(number_dram.rearrange("(g f) o -> g (f o)", f=GROUP), number_i[0:GN, :]).then_inc(s_numd, DMA)

            def x_load(i, first=False, last=False):
                for u in range(SLOTS):
                    if not first:
                        sp.wait_ge(p_put[u], i * (TILES * DMA))
                    if last and u == SLOTS - 1:
                        sp.wait_ge(p_clear, 1)
                        sp.dma_start(x_rows[0:LAST_P, u, :, :].rearrange("p t c -> p (t c)"), x_in_last).then_inc(p_x[u], DMA)
                    else:
                        sp.dma_start(slot(x_rows, u), group_of(x_in_groups, i * SLOTS + u)).then_inc(p_x[u], DMA)

            x_load(0, first=True)
            with sp.Fori(1, PAIRS_N - 1) as i:
                x_load(i)
            x_load(PAIRS_N - 1, last=True)

            sp.wait_ge(s_rows, 3)
            sp.wait_ge(s_azero, DMA)
            def layer(l, state, last=False):
                sp.wait_ge(n_h3P, l * GN + SLOTS)
                for k, w in ((EW2, eW2), (EW3, eW3), (NW2, nW2), (NW3, nW3)):
                    sp.dma_start(W[:, k, :], group_of(w, l)).then_inc(s_wload, DMA)
                for k, w in ((EW1_DST, eW1), (NW1_X, nW1)):
                    sp.dma_start(W[:, k:k + 2, :], w[bass.ds(l, 1), :, :].rearrange("a (h p) c -> p (a h) c", p=P)).then_inc(s_wload, DMA)
                for rows_of, v in ((msg_gain, eg), (msg_shift, ebt)):
                    sp.dma_start(rows_of[:, :], v[bass.ds(l, 1), :].to_broadcast([P, C])).then_inc(s_wload, DMA)
                for u in range(SLOTS):
                    sp.wait_ge(p_put[u], PAIRS_N * (TILES * DMA))
                for u in range(SLOTS):
                    sp.wait_ge(s_st[u], over(l * PAIRS_N))
                sp.sem_inc(passed["sp"], 1)

                def load_windows(i, u):
                    g = i * SLOTS + u
                    sp.wait_ge(e_dstP, free(l * GE + g))
                    sp.sem_inc(passed["sp"], 1)
                    for t in range(TILES):
                        base = sp.value_load(base_row[0:1, bass.ds(g * TILES + t, 1)], min_val=0, max_val=EP - P)
                        sp.dma_start(win_rows[:, u, t, :], state[bass.ds(base, P), :]).then_inc(s_win[u], DMA)

                skewed(sp, GE, [(0, load_windows)])
                sp.wait_ge(s_agg, over((l + 1) * GE + 1))
                sp.sem_inc(passed["sp"], 1)

                state_groups = state.rearrange("(g p t) c -> g p (t c)", p=P, t=TILES)

                def load_nodes(i, u):
                    g = i * SLOTS + u
                    k = l * GN + g
                    sp.wait_ge(n_xP, free(k))
                    sp.dma_start(slot(x_rows, u), group_of(state_groups, g)).then_inc(s_x[u], DMA)

                def load_sums(i, u):
                    g = i * SLOTS + u
                    sp.wait_ge(n_h1P, free(l * GN + g))
                    sp.dma_start(aT[:, u, :], aggT[:, bass.ds(g * GROUP, GROUP)]).then_inc(s_a[u], DMA)

                def store_nodes(i, u):
                    g = i * SLOTS + u
                    sp.wait_ge(n_new, done(l * GN + g))
                    sp.dma_start(group_of(new_groups, g), slot(new_rows, u)).then_inc(s_st[u], DMA)

                def load_residual(i, u):
                    g = i * SLOTS + u
                    sp.wait_ge(f_y, free(g))
                    sp.dma_start(slot(win_rows, u), group_of(perm_groups, g)).then_inc(f_r[u], DMA)

                skewed(sp, GN, [(0, load_nodes), (1, load_sums), (4, load_residual) if last else (6, store_nodes)])

            new_groups = x_state.rearrange("(g p t) c -> g p (t c)", p=P, t=TILES)
            perm_groups = x_perm.rearrange("(g p t) c -> g p (t c)", p=P, t=TILES)
            layer(0, x_perm)
            with sp.Fori(1, L - 1) as l:
                layer(l, x_state)
            for u in range(SLOTS):
                sp.wait_ge(v_put[u], PAIRS_N * (TILES * DMA))
            sp.dma_start(num_idx[:, :, :], old_dram.rearrange("(g p t) o -> p g (t o)", p=P, t=TILES)).then_inc(v_table, DMA)
            layer(L - 1, x_state, last=True)

        @block.gpsimd
        def _(pool):
            nc.gpsimd.memset(pad_dst[:, :], NP - 1).then_inc(s_pads, 1)
            nc.gpsimd.memset(pad_src[:, :], 0).then_inc(s_pads, 1)
            nc.gpsimd.memset(pad_ends[:, :], -1).then_inc(s_pads, 1)
            nc.gpsimd.memset(ident[:, :], 0.0).then_inc(s_const, 1)
            nc.gpsimd.memset(below[:, :], 1.0).then_inc(s_const, 1)
            nc.gpsimd.memset(after[:, :], 1.0).then_inc(s_const, 1)
            nc.gpsimd.memset(zeros[:, :], 0.0).then_inc(s_const, 1)
            nc.gpsimd.iota(count_i[:, :], [[1, GROUP]], base=0, channel_multiplier=0).then_inc(s_const, 1)
            nc.gpsimd.iota(part_i[:, :], [[0, 1]], base=0, channel_multiplier=1).then_inc(s_const, 1)
            nc.gpsimd.iota(node_ids[:, :, :], [[GROUP, SLOTS], [1, TILES]], base=0, channel_multiplier=TILES).then_inc(s_const, 1)
            pool.wait_ge(s_const, 7)
            nc.gpsimd.affine_select(out=ident[:, :], in_=ident[:, :], compare_op=ALU.not_equal, fill=1.0, base=0,
                                    pattern=[[-1, P]], channel_multiplier=1).then_inc(s_const, 1)
            nc.gpsimd.affine_select(out=below[:, :], in_=below[:, :], compare_op=ALU.is_gt, fill=0.0, base=0,
                                    pattern=[[-1, P]], channel_multiplier=1).then_inc(s_const, 1)
            nc.gpsimd.affine_select(out=after[:, :], in_=after[:, :], compare_op=ALU.is_gt, fill=0.0, base=0,
                                    pattern=[[1, P]], channel_multiplier=-1).then_inc(s_const, 1)
            nc.gpsimd.memset(gather_idx[:, :, :], 0).then_inc(s_const, 1)
            pool.wait_ge(s_const, POOL_CONSTS)
            pool.wait_ge(s_flag, 1)
            is_unsorted = pool.value_load(unsorted[0:1, 0:1], min_val=0, max_val=1)
            with pool.If(is_unsorted != 0):
                pool.wait_ge(q_rank, 1)
                with pool.Fori(0, NT) as j:
                    nc.gpsimd.tensor_copy(st_rank, rank_i[:, bass.ds(j, 1)]).then_inc(q_copy, 1)
                    nc.gpsimd.tensor_copy(st_dst, dcol_i[:, bass.ds(j, 1)]).then_inc(q_copy, 1)
                    nc.gpsimd.tensor_copy(st_src, scol_i[:, bass.ds(j, 1)]).then_inc(q_copy, 1)
                    pool.wait_ge(q_copy, j * 3 + 3)
                    pool.sem_inc(passed["pool"], 1)
                    nc.gpsimd.indirect_dma_start(dst_sorted, bass.IndirectOffsetOnAxis(st_rank, 0), st_dst, None).then_inc(q_put, DMA)
                    nc.gpsimd.indirect_dma_start(src_sorted, bass.IndirectOffsetOnAxis(st_rank, 0), st_src, None).then_inc(q_put, DMA)
                    pool.wait_ge(q_put, (j + 1) * (2 * DMA))
                    pool.sem_inc(passed["pool"], 1)
            with pool.Else():
                pool.nop()

            pool.wait_ge(s_numi, 1)

            def renumber_rows(i, u, first=False):
                g = i * SLOTS + u
                if not first:
                    pool.wait_ge(p_put[u], i * (TILES * DMA))
                    pool.sem_inc(passed["pool"], 1)
                nc.gpsimd.tensor_copy(gather_idx[:, u, :], num_idx[:, bass.ds(g, 1), :].rearrange("p a t -> p (a t)")).then_inc(p_stage, 1)
                pool.wait_ge(p_x[u], (i + 1) * DMA)
                pool.wait_ge(p_stage, g + 1)
                pool.sem_inc(passed["pool"], 1)
                for t in range(TILES):
                    nc.gpsimd.indirect_dma_start(x_perm, bass.IndirectOffsetOnAxis(gather_idx[:, u, t:t + 1], 0), x_rows[:, u, t, :], None).then_inc(p_put[u], DMA)

            for u in range(SLOTS):
                renumber_rows(0, u, first=True)
            with pool.Fori(1, PAIRS_N) as i:
                for u in range(SLOTS):
                    renumber_rows(i, u)
            for u in range(SLOTS):
                pool.wait_ge(p_put[u], PAIRS_N * (TILES * DMA))

            def gather_sources(layer, state):
                def gather(i, u):
                    pair = layer * PAIRS_E + i
                    k = pair * SLOTS + u
                    pool.wait_ge(e_srcP, free(k))
                    pool.sem_inc(passed["pool"], 1)
                    nc.gpsimd.tensor_copy(gather_idx[:, u, :], src_idx[:, bass.ds(i * SLOTS + u, 1), :].rearrange("p a t -> p (a t)")).then_inc(s_gidx, 1)
                    pool.wait_ge(s_gidx, k + 1)
                    pool.sem_inc(passed["pool"], 1)
                    for t in range(TILES):
                        nc.gpsimd.indirect_dma_start(src_rows[:, u, t, :], None, state, bass.IndirectOffsetOnAxis(gather_idx[:, u, t:t + 1], 0)).then_inc(s_src[u], DMA)

                with pool.Fori(0, PAIRS_E) as i:
                    for u in range(SLOTS):
                        gather(i, u)

            gather_sources(0, x)
            pool.wait_ge(s_numd, DMA)
            for u in range(SLOTS):
                pool.wait_ge(s_src[u], PAIRS_E * (TILES * DMA))

            def fetch_numbers(i, u):
                g = i * SLOTS + u
                pool.wait_ge(m_put, free(g))
                pool.sem_inc(passed["pool"], 1)
                nc.gpsimd.tensor_copy(gather_idx[:, u, :], src_idx[:, bass.ds(g, 1), :].rearrange("p a t -> p (a t)")).then_inc(m_stage, 1)
                pool.wait_ge(m_stage, g + 1)
                pool.sem_inc(passed["pool"], 1)
                for t in range(TILES):
                    nc.gpsimd.indirect_dma_start(new_idx[:, u, t:t + 1], None, number_dram, bass.IndirectOffsetOnAxis(gather_idx[:, u, t:t + 1], 0)).then_inc(m_got[u], DMA)

            def keep_numbers(i, u):
                g = i * SLOTS + u
                pool.wait_ge(m_got[u], (i + 1) * (TILES * DMA))
                pool.sem_inc(passed["pool"], 1)
                nc.gpsimd.tensor_copy(src_idx[:, bass.ds(g, 1), :].rearrange("p a t -> p (a t)"), new_idx[:, u, :]).then_inc(m_put, 1)

            pool.sem_inc(m_put, SLOTS)
            skewed(pool, GE, [(0, fetch_numbers), (1, keep_numbers)])
            pool.wait_ge(m_put, done(GE - 1))

            def later_layer(l):
                for u in range(SLOTS):
                    pool.wait_ge(s_st[u], over(l * PAIRS_N))
                pool.sem_inc(passed["pool"], 1)
                gather_sources(l, x_state)

            later_layer(1)
            for u in range(SLOTS):
                pool.wait_ge(s_src[u], 2 * PAIRS_E * (TILES * DMA))

            def scatter_ids(i, u, first=False):
                g = i * SLOTS + u
                if not first:
                    pool.wait_ge(v_put[u], i * (TILES * DMA))
                    pool.sem_inc(passed["pool"], 1)
                    nc.gpsimd.tensor_scalar(node_ids[:, u, :], node_ids[:, u, :], float(SLOTS * GROUP), None, ALU.add).then_inc(v_ids, 1)
                nc.gpsimd.tensor_copy(gather_idx[:, u, :], num_idx[:, bass.ds(g, 1), :].rearrange("p a t -> p (a t)")).then_inc(v_stage, 1)
                pool.wait_ge(v_stage, g + 1)
                if not first:
                    pool.wait_ge(v_ids, g + (1 - SLOTS))
                pool.sem_inc(passed["pool"], 1)
                for t in range(TILES):
                    nc.gpsimd.indirect_dma_start(old_dram, bass.IndirectOffsetOnAxis(gather_idx[:, u, t:t + 1], 0), node_ids[:, u, t:t + 1], None).then_inc(v_put[u], DMA)

            for u in range(SLOTS):
                scatter_ids(0, u, first=True)
            with pool.Fori(1, PAIRS_N) as i:
                for u in range(SLOTS):
                    scatter_ids(i, u)
            for u in range(SLOTS):
                pool.wait_ge(v_put[u], PAIRS_N * (TILES * DMA))

            with pool.Fori(2, L) as l:
                later_layer(l)

            pool.wait_ge(v_table, DMA)
            for u in range(SLOTS):
                pool.wait_ge(s_src[u], L * PAIRS_E * (TILES * DMA))

            def shift_residual(i, u):
                pool.wait_ge(f_r[u], (i + 1) * DMA)
                pool.sem_inc(passed["pool"], 1)
                nc.gpsimd.tensor_tensor(win_rows[:, u, :, :], win_rows[:, u, :, :], out_shift[:, None, :].to_broadcast([P, TILES, C]), ALU.add).then_inc(f_sh, 1)

            def scatter_out(i, u):
                g = i * SLOTS + u
                if not (isinstance(i, int) and i == 0):
                    pool.wait_ge(f_put[u], i * (TILES * DMA))
                    pool.sem_inc(f_out, 1)
                nc.gpsimd.tensor_copy(gather_idx[:, u, :], num_idx[:, bass.ds(g, 1), :].rearrange("p a t -> p (a t)")).then_inc(f_idx, 1)
                pool.wait_ge(f_idx, g + 1)
                pool.wait_ge(f_new, done(g))
                pool.sem_inc(passed["pool"], 1)
                for t in range(TILES):
                    nc.gpsimd.indirect_dma_start(out, bass.IndirectOffsetOnAxis(gather_idx[:, u, t:t + 1], 0), new_rows[:, u, t, :], None,
                                                 bounds_check=N - 1, oob_is_err=False).then_inc(f_put[u], DMA)

            pool.sem_inc(f_out, SLOTS)
            pool.sem_inc(f_sh, SLOTS)
            pool.wait_ge(s_gb, 2 * DMA)
            skewed(pool, GN, [(2, scatter_out), (0, shift_residual)], apart=2)
            for u in range(SLOTS):
                pool.wait_ge(f_put[u], PAIRS_N * (TILES * DMA))

        @block.tensor
        def _(pe):
            for s in (e_srcP, e_dstP, e_h1P, e_h2P, e_h3P, e_sumP, n_xP, n_h1P, n_h2P, n_h3P):
                pe.sem_inc(s, SLOTS)
            pe.wait_ge(s_const, POOL_CONSTS)
            pe.wait_ge(s_cst2, DVE_CONSTS)
            pe.wait_ge(s_dis, 2)
            nc.tensor.matmul(bank[0][0:1, 0:1], disorder[0:GE, :], ones[0:GE, 0:1], start=True, stop=True).then_inc(s_dsum, 1)
            pe.wait_ge(s_vload, 7 * DMA)
            nc.tensor.transpose(bank[1][:, 0:L * VECS], vec_rows[:, :], ident[0:L * VECS, 0:L * VECS]).then_inc(s_vT, 1)

            def columns(b, rows_of, n, signal, step):
                for t in range(TILES):
                    part = rows_of[0:n, t * P:(t + 1) * P] if step == 1 else rows_of[0:n, t:GROUP:TILES]
                    mm = nc.tensor.transpose(bank[b][:, t * n:(t + 1) * n], part, ident[0:n, 0:n])
                mm.then_inc(signal, 1)

            for n, (b, r) in enumerate(((2, g_hi), (3, g_lo), (4, g_src))):
                pe.wait_ge(s_colr, n + 1)
                columns(b, r, GE, s_colP, 1)
            pe.wait_ge(s_run, 3)
            nc.tensor.matmul(bank[5][0:GE, 0:1], after[0:GE, 0:GE], row_sum[0:GE, 0:1], start=True, stop=True).then_inc(s_offP, 1)
            nc.tensor.matmul(bank[6][:, :], zeros_b[:, 0:P], zeros_b[:, :], start=True, stop=False, skip_group_check=True)
            pe.sem_inc(h_P, SLOTS)
            with pe.Fori(0, PAIRS_E) as i:
                for u in range(SLOTS):
                    pe.wait_ge(h_lo, i * SLOTS + u + 1)
                    for t in range(TILES):
                        mm = nc.tensor.matmul(bank[6][:, :], mask_hi[u][:, t, :], mask_lo[u][:, t, :], start=False, stop=False, skip_group_check=True)
                    mm.then_inc(h_P, 1)
            nc.tensor.matmul(bank[6][:, :], zeros_b[:, 0:P], zeros_b[:, :], start=False, stop=True, skip_group_check=True).then_inc(h_all, 1)
            pe.wait_ge(s_rel, 2)
            columns(7, g_rel, GE, s_relP, 1)
            pe.wait_ge(s_node, 3)
            nc.tensor.matmul(bank[0][0:GN, 1:2], after[0:GN, 0:GN], row_sum[0:GN, 1:2], start=True, stop=True)
            nc.tensor.matmul(bank[0][0:GN, 2:3], ones[0:GN, 0:GN], row_sum[0:GN, 1:2], start=True, stop=True).then_inc(s_noffP, 1)
            pe.wait_ge(s_vall, 1)
            pe.wait_ge(s_num, 6)
            columns(1, n_number, GN, s_numP, TILES)
            pe.wait_ge(s_numi, 1)
            pe.wait_ge(s_relc, 1)

            def turn(b, rows_of, u, signal):
                for t in range(TILES):
                    mm = nc.tensor.transpose(b[:, t * P:(t + 1) * P], rows_of[:, u, t, :], ident[:, :])
                mm.then_inc(signal, 1)

            with pe.Fori(0, L) as l:
                pe.wait_ge(s_wts, l + 1)
                pe.sem_inc(passed["pe"], 1)

                def edge(i, u):
                    return (l * PAIRS_E + i) * SLOTS + u

                def src_turn(i, u):
                    k = edge(i, u)
                    pe.wait_ge(s_src[u], (l * PAIRS_E + i + 1) * (TILES * DMA))
                    pe.wait_ge(e_srcT, prev(k))
                    turn(bank[B_SRC], src_rows, u, e_srcP)

                def dst_spread(i, u):
                    k = edge(i, u)
                    pe.wait_ge(s_win[u], (l * PAIRS_E + i + 1) * (TILES * DMA))
                    pe.wait_ge(e_spread, done(k))
                    pe.wait_ge(e_dstT, prev(k))
                    for t in range(TILES):
                        mm = nc.tensor.matmul(bank[B_DST][:, t * P:(t + 1) * P], win_rows[:, u, t, :], spread[:, u, t * P:(t + 1) * P], start=True, stop=True)
                    mm.then_inc(e_dstP, 1)

                def eh1_product(i, u):
                    k = edge(i, u)
                    pe.wait_ge(e_h1b, prev(k))
                    pe.wait_ge(e_srcT, done(k))
                    nc.tensor.matmul(bank[B_H1][:, :], W[:, EW1_SRC, :], srcT[:, u, :], start=True, stop=False)
                    pe.wait_ge(e_dstT, done(k))
                    nc.tensor.matmul(bank[B_H1][:, :], W[:, EW1_DST, :], dstT[:, u, :], start=False, stop=True).then_inc(e_h1P, 1)

                def eh2_product(i, u):
                    k = edge(i, u)
                    pe.wait_ge(e_h1, done(k))
                    pe.wait_ge(e_h2b, prev(k))
                    nc.tensor.matmul(bank[B_H2][:, :], W[:, EW2, :], eh1[:, u, :], start=True, stop=True).then_inc(e_h2P, 1)

                def eh3_product(i, u):
                    k = edge(i, u)
                    pe.wait_ge(e_h2, done(k))
                    pe.wait_ge(e_gain, free(k))
                    for t in range(TILES):
                        mm = nc.tensor.matmul(bank[B_H3 + u][:, t * P:(t + 1) * P], eh2[:, u, t * P:(t + 1) * P], W3c[:, 0, :], start=True, stop=True)
                    mm.then_inc(e_h3P, 1)

                def sum_product(i, u):
                    k = edge(i, u)
                    g = i * SLOTS + u
                    pe.wait_ge(e_sumc, prev(k))
                    nc.tensor.matmul(bank[B_SUM][:, :], zeros_b[:, 0:P], zeros_b[:, :], start=True, stop=False, skip_group_check=True)
                    pe.wait_ge(e_coll, done(k))
                    pe.wait_ge(e_msg, done(k))
                    for t in range(TILES):
                        off = pe.value_load(off_row[0:1, bass.ds(g * TILES + t, 1)], min_val=0, max_val=GROUP - P) if t else 0
                        mm = nc.tensor.matmul(bank[B_SUM][:, bass.ds(off, P)], msg[:, u, t, :], collect[:, u, t, :], start=False, stop=t == TILES - 1, skip_group_check=True)
                    mm.then_inc(e_sumP, 1)

                skewed(pe, GE, [(3, eh1_product), (4, eh2_product), (5, eh3_product), (6, sum_product), (1, dst_spread), (1, src_turn)])
                pe.wait_ge(e_sumc, (l + 1) * GE + SLOTS)
                pe.sem_inc(passed["pe"], 1)

                def node(i, u):
                    return (l * PAIRS_N + i) * SLOTS + u

                def x_turn(i, u):
                    k = node(i, u)
                    pe.wait_ge(s_x[u], (l * PAIRS_N + i + 1) * DMA)
                    pe.wait_ge(n_xT, prev(k))
                    turn(bank[B_SRC], x_rows, u, n_xP)

                def nh1_product(i, u):
                    k = node(i, u)
                    pe.wait_ge(n_h1b, prev(k))
                    pe.wait_ge(n_xT, done(k))
                    nc.tensor.matmul(bank[B_H1][:, :], W[:, NW1_X, :], xT[:, u, :], start=True, stop=False)
                    pe.wait_ge(s_a[u], (l * PAIRS_N + i + 1) * DMA)
                    nc.tensor.matmul(bank[B_H1][:, :].rearrange("c (t p) -> c t p", t=TILES), W[:, NW1_AGG, :], aT[:, u, :].rearrange("c (p t) -> c t p", t=TILES), start=False, stop=True).then_inc(n_h1P, 1)

                def nh2_product(i, u):
                    k = node(i, u)
                    pe.wait_ge(n_h1, done(k))
                    pe.wait_ge(n_h2b, prev(k))
                    nc.tensor.matmul(bank[B_H2][:, :], W[:, NW2, :], nh1[:, u, :], start=True, stop=True).then_inc(n_h2P, 1)

                def nh3_product(i, u):
                    k = node(i, u)
                    pe.wait_ge(n_h2, done(k))
                    pe.wait_ge(n_new, free(k))
                    for t in range(TILES):
                        mm = nc.tensor.matmul(bank[B_H3 + u][:, t * P:(t + 1) * P], nh2[:, u, t * P:(t + 1) * P], W3c[:, 1, :], start=True, stop=True)
                    mm.then_inc(n_h3P, 1)

                skewed(pe, GN, [(3, nh1_product), (4, nh2_product), (5, nh3_product), (1, x_turn)])

        @block.scalar
        def _(act):
            for s in (e_srcT, e_dstT, e_h1b, e_h2b, e_sq, e_sd, e_sumc, n_xT, n_h1b, n_h2b, n_sq, n_sd, f_sd, f_new):
                act.sem_inc(s, SLOTS)
            act.wait_ge(s_const, POOL_CONSTS)
            act.wait_ge(s_rela, DMA)
            nc.scalar.dma_start(aggT.rearrange("p (r c) -> p r c", c=C), zeros[:, None, :].to_broadcast([P, NP // C, C])).then_inc(s_azero, DMA)
            act.wait_ge(s_cst2, DVE_CONSTS)
            act.wait_ge(s_azero, DMA)
            act.wait_ge(s_rows, 3)

            def layer(l, last=False):
                act.wait_ge(s_wts, l + 1)
                act.sem_inc(passed["act"], 1)

                def edge(i, u):
                    return (l * PAIRS_E + i) * SLOTS + u

                def src_scale(i, u):
                    k = edge(i, u)
                    act.wait_ge(e_srcP, done(k))
                    act.wait_ge(e_h1P, free(k))
                    nc.scalar.activation(srcT[:, u, :], bank[B_SRC][:, :], ACT.Identity, bias=vecs[:, XB:XB + 1], scale=vecs[:, XG:XG + 1]).then_inc(e_srcT, 1)

                def dst_scale(i, u):
                    k = edge(i, u)
                    act.wait_ge(e_dstP, done(k))
                    act.wait_ge(e_h1P, free(k))
                    nc.scalar.activation(dstT[:, u, :], bank[B_DST][:, :], ACT.Identity, bias=vecs[:, XB:XB + 1], scale=vecs[:, XG:XG + 1]).then_inc(e_dstT, 1)

                def eh1_bias(i, u):
                    k = edge(i, u)
                    act.wait_ge(e_h1P, done(k))
                    act.wait_ge(e_h2P, free(k))
                    nc.scalar.activation(eh1[:, u, :], bank[B_H1][:, :], ACT.Identity, bias=vecs[:, EB1:EB1 + 1]).then_inc(e_h1b, 1)

                def eh2_bias(i, u):
                    k = edge(i, u)
                    act.wait_ge(e_h2P, done(k))
                    act.wait_ge(e_h3P, free(k))
                    nc.scalar.activation(eh2[:, u, :], bank[B_H2][:, :], ACT.Identity, bias=vecs[:, EB2:EB2 + 1]).then_inc(e_h2b, 1)

                def e_square(i, u):
                    k = edge(i, u)
                    act.wait_ge(e_h3P, done(k))
                    act.wait_ge(e_ss, free(k))
                    nc.scalar.activation(slot(esq, u), bank[B_H3 + u][:, :], ACT.Square).then_inc(e_sq, 1)

                def e_deviate(i, u):
                    k = edge(i, u)
                    act.wait_ge(e_ss, done(k))
                    act.wait_ge(e_msg, free(k))
                    nc.scalar.activation(ers[:, u, :], ess[:, u, :], ACT.Sqrt, bias=eps_col[:, :], scale=1.0 / C).then_inc(e_sd, 1)

                def sum_copy(i, u):
                    k = edge(i, u)
                    act.wait_ge(e_sumP, done(k))
                    act.wait_ge(s_agg, over(k))
                    act.wait_ge(e_sum, prev(k))
                    nc.scalar.activation(sums[:, u, 0:GROUP], bank[B_SUM][:, :], ACT.Identity).then_inc(e_sumc, 1)

                def store_sums(i, u):
                    g = i * SLOTS + u
                    k = edge(i, u)
                    act.wait_ge(e_sum, done(k))
                    act.sem_inc(passed["act"], 1)
                    act.wait_ge(s_agg, over(k + 1))
                    act.sem_inc(passed["act"], 1)
                    base = act.value_load(base_row[0:1, bass.ds(g * TILES, 1)], min_val=0, max_val=EP - GROUP)
                    nc.scalar.dma_start(aggT[:, bass.ds(base, GROUP)], sums[:, u, 0:GROUP]).then_inc(s_agg, DMA)

                skewed(act, GE, [(7, store_sums), (3, eh1_bias), (4, eh2_bias), (5, e_square), (6, sum_copy), (5, e_deviate), (1, dst_scale), (1, src_scale)])

                def node(i, u):
                    return (l * PAIRS_N + i) * SLOTS + u

                def x_scale(i, u):
                    k = node(i, u)
                    act.wait_ge(n_xP, done(k))
                    act.wait_ge(n_h1P, free(k))
                    nc.scalar.activation(xT[:, u, :], bank[B_SRC][:, :], ACT.Identity, bias=vecs[:, XB:XB + 1], scale=vecs[:, XG:XG + 1]).then_inc(n_xT, 1)

                def nh1_bias(i, u):
                    k = node(i, u)
                    act.wait_ge(n_h1P, done(k))
                    act.wait_ge(n_h2P, free(k))
                    nc.scalar.activation(nh1[:, u, :], bank[B_H1][:, :], ACT.Identity, bias=vecs[:, NB1:NB1 + 1]).then_inc(n_h1b, 1)

                def nh2_bias(i, u):
                    k = node(i, u)
                    act.wait_ge(n_h2P, done(k))
                    act.wait_ge(n_h3P, free(k))
                    nc.scalar.activation(nh2[:, u, :], bank[B_H2][:, :], ACT.Identity, bias=vecs[:, NB2:NB2 + 1]).then_inc(n_h2b, 1)

                def n_square(i, u):
                    k = node(i, u)
                    act.wait_ge(n_h3P, done(k))
                    act.wait_ge(n_ss, free(k))
                    nc.scalar.activation(slot(nsq, u), bank[B_H3 + u][:, :], ACT.Square).then_inc(n_sq, 1)

                def n_deviate(i, u):
                    k = node(i, u)
                    act.wait_ge(n_ss, done(k))
                    act.wait_ge(n_new, free(k))
                    nc.scalar.activation(nrs[:, u, :], nss[:, u, :], ACT.Sqrt, bias=eps_col[:, :], scale=1.0 / C).then_inc(n_sd, 1)

                def f_deviate(i, u):
                    g = i * SLOTS + u
                    act.wait_ge(f_mv, done(g))
                    act.wait_ge(f_new, free(g))
                    nc.scalar.activation(frs[:, u, :], fmv[:, u, :, 1], ACT.Sqrt, bias=eps_col[:, :]).then_inc(f_sd, 1)

                def f_norm(i, u):
                    g = i * SLOTS + u
                    act.wait_ge(f_ms, done(g))
                    act.wait_ge(f_out, free(g))
                    for t in range(TILES):
                        op = nc.scalar.activation(new_rows[:, u, t, :], src_rows[:, u, t, :], ACT.Identity, bias=fshift[:, u, t:t + 1], scale=frs[:, u, t:t + 1])
                    op.then_inc(f_new, 1)

                if last:
                    skewed(act, GN, [(3, nh1_bias), (4, nh2_bias), (6, f_deviate), (5, n_square), (5, n_deviate), (1, x_scale), (6, f_norm)])
                else:
                    skewed(act, GN, [(3, nh1_bias), (4, nh2_bias), (5, n_square), (1, x_scale), (5, n_deviate)])

            with act.Fori(0, L - 1) as l:
                layer(l)
            layer(L - 1, last=True)

        def rank_edges(dve):
            dve.wait_ge(q_cols, 2 * DMA)
            dve.sem_inc(q_count, 1)
            nc.vector.tensor_copy(dcol_f, dcol_i).then_inc(q_step, 1)
            dve.wait_ge(q_step, 1)
            steps = 1

            def count(c, j):
                dve.wait_ge(q_count, j + (c * NT + 1))
                nc.vector.tensor_scalar(chunk_junk, chunk_f, dcol_f[:, bass.ds(j, 1)], None, ALU.is_lt, ALU.add,
                                        accum_out=less(c)[:, bass.ds(j, 1)]).then_inc(q_count, 1)

            for c in range(CHUNKS):
                lo, hi = c * CT, (c + 1) * CT
                dve.wait_ge(q_chunk, (c + 1) * DMA)
                dve.wait_ge(q_used, c)
                nc.vector.tensor_copy(chunk_f, chunk_i).then_inc(q_conv, 1)
                dve.wait_ge(q_conv, c + 1)
                if c:
                    with dve.Fori(0, lo) as j:
                        count(c, j)
                with dve.Fori(lo, hi) as j:
                    at = bass.ds((j - lo) * P, P)
                    count(c, j)
                    nc.vector.tensor_scalar(equal, chunk_f[:, at], dcol_f[:, bass.ds(j, 1)], None, ALU.is_equal).then_inc(q_step, 1)
                    dve.wait_ge(q_step, (j - lo) * 3 + (steps + 1))
                    nc.vector.tensor_tensor(equal_junk, equal, below[:, :], ALU.mult).then_inc(q_step, 1)
                    dve.wait_ge(q_step, (j - lo) * 3 + (steps + 2))
                    nc.vector.reduce_sum(tie[:, bass.ds(j, 1)], equal_junk, AX.X)
                    nc.vector.tensor_scalar(chunk_f[:, at], chunk_f[:, at], -0.5, None, ALU.add).then_inc(q_step, 1)
                    dve.wait_ge(q_step, (j - lo) * 3 + (steps + 3))
                    dve.sem_inc(passed["dve"], 1)
                steps += 3 * CT
                if hi < NT:
                    with dve.Fori(hi, NT) as j:
                        count(c, j)
                dve.wait_ge(q_count, (c + 1) * NT + 1)
                nc.vector.memset(equal, 0.0).then_inc(q_used, 1)
            dve.wait_ge(q_used, CHUNKS)
            nc.vector.tensor_scalar(rank_f, tie, 1.0, None, ALU.add).then_inc(q_step, 1)
            for c in range(CHUNKS):
                dve.wait_ge(q_step, steps + 1 + c)
                nc.vector.tensor_tensor(rank_f, rank_f, less(c), ALU.add).then_inc(q_step, 1)
            dve.wait_ge(q_step, steps + 1 + CHUNKS)
            nc.vector.tensor_copy(rank_i, rank_f).then_inc(q_rank, 1)

        @block.vector
        def _(dve):
            for s in (e_spread, e_h1, e_h2, e_ss, e_rs, e_gain, e_msg, e_coll, e_sum, n_h1, n_h2, n_ss, n_rs, n_new,
                      f_y, f_bn, f_mv, f_rs, f_ms):
                dve.sem_inc(s, SLOTS)
            nc.vector.memset(vec_rows[:, :], 1.0).then_inc(s_vrow, 1)
            nc.vector.memset(ones[:, :], 1.0).then_inc(s_cst2, 1)
            nc.vector.memset(zeros_b[:, :], 0.0).then_inc(s_cst2, 1)
            nc.vector.memset(eps_col[:, :], EPS).then_inc(s_cst2, 1)
            nc.vector.memset(sums[:, :, :], 0.0).then_inc(s_cst2, 1)
            dve.wait_ge(s_const, POOL_CONSTS)
            nc.vector.tensor_copy(count_h[:, :], count_i[:, :]).then_inc(s_cst2, 1)
            nc.vector.tensor_copy(count_f[:, :], count_i[:, 0:P]).then_inc(s_cst2, 1)
            nc.vector.tensor_copy(part_col[:, :], part_i[:, :]).then_inc(s_cst2, 1)
            nc.vector.tensor_scalar(group_col[:, :], part_i[:, :], float(GROUP), None, ALU.mult).then_inc(s_cst2, 1)
            dve.wait_ge(s_check, 2 * DMA)
            nc.vector.tensor_tensor(g_start[0:GE, :], e_now[0:GE, :], e_prev[0:GE, :], ALU.is_lt).then_inc(s_dis, 1)
            dve.wait_ge(s_dis, 1)
            nc.vector.reduce_max(disorder[0:GE, :], g_start[0:GE, :], AX.X).then_inc(s_dis, 1)
            dve.wait_ge(s_dsum, 1)
            nc.vector.tensor_scalar(unsorted[0:1, 0:1], bank[0][0:1, 0:1], 1.0, None, ALU.min).then_inc(s_flag, 1)
            dve.wait_ge(s_flag, 1)
            is_unsorted = dve.value_load(unsorted[0:1, 0:1], min_val=0, max_val=1)
            with dve.If(is_unsorted != 0):
                rank_edges(dve)
            with dve.Else():
                dve.nop()

            dve.wait_ge(s_edges, 3 * DMA)
            nc.vector.tensor_scalar(g_hi_i[0:GE, :], e_now[0:GE, :], GROUP_BITS, None, ALU.arith_shift_right).then_inc(s_run, 1)
            nc.vector.tensor_scalar(g_lo_i[0:GE, :], e_now[0:GE, :], GROUP - 1, None, ALU.bitwise_and).then_inc(s_run, 1)
            dve.wait_ge(s_run, 2)
            nc.vector.tensor_copy(g_hi[0:GE, :], g_hi_i[0:GE, :]).then_inc(s_colr, 1)
            nc.vector.tensor_copy(g_lo[0:GE, :], g_lo_i[0:GE, :]).then_inc(s_colr, 1)
            nc.vector.tensor_copy(g_src[0:GE, :], e_src[0:GE, :]).then_inc(s_colr, 1)
            nc.vector.tensor_tensor(g_start[0:GE, :], e_now[0:GE, :], e_prev[0:GE, :], ALU.not_equal).then_inc(s_node, 1)
            dve.wait_ge(s_node, 1)
            nc.vector.tensor_tensor_scan(g_run[0:GE, :], ones[0:GE, 0:1].to_broadcast([GE, GROUP]), g_start[0:GE, :], 0.0, ALU.mult, ALU.add).then_inc(s_rel, 1)
            dve.wait_ge(s_rel, 1)
            nc.vector.tensor_copy(row_sum[0:GE, 0:1], g_run[0:GE, GROUP - 1:GROUP]).then_inc(s_run, 1)
            src_cols = src_idx[:, :, :].rearrange("p g t -> p (g t)")
            for n, (b, c) in enumerate(((2, hi_cols), (3, lo_cols), (4, src_cols))):
                dve.wait_ge(s_colP, n + 1)
                nc.vector.tensor_copy(c.rearrange("p (g t) -> p t g", t=TILES), bank[b][:, 0:NT].rearrange("p (t g) -> p t g", t=TILES)).then_inc(s_col, 1)
            dve.wait_ge(s_offP, 1)
            nc.vector.tensor_scalar(g_num[0:GE, :], g_run[0:GE, :], bank[5][0:GE, 0:1], -1.0, ALU.add, ALU.add).then_inc(s_tmp, 1)
            dve.wait_ge(s_tmp, 1)
            num_t = g_num[0:GE, :].rearrange("g (t f) -> g t f", t=TILES)
            nc.vector.tensor_tensor(g_rel[0:GE, :].rearrange("g (t f) -> g t f", t=TILES), num_t, num_t[:, :, 0:1].to_broadcast([GE, TILES, P]), ALU.subtract).then_inc(s_rel, 1)
            nc.vector.tensor_copy(base_i[0:GE, :], g_num[0:GE, 0:GROUP:P]).then_inc(s_rel, 1)
            dve.wait_ge(s_rel, 3)
            nc.vector.tensor_copy(rel_b[0:GE, :], g_rel[0:GE, :]).then_inc(s_rel, 1)

            dve.wait_ge(s_col, 3)
            with dve.Fori(0, PAIRS_E) as i:
                for u in range(SLOTS):
                    g = i * SLOTS + u
                    dve.wait_ge(h_P, free(g))
                    for t in range(TILES):
                        at = bass.ds(g * TILES + t, 1)
                        nc.vector.tensor_scalar(mask_lo[u][:, t, :], count_h[:, :], lo_cols[:, at], None, ALU.is_equal)
                        op = nc.vector.tensor_scalar(mask_hi[u][:, t, :], count_h[:, 0:P], hi_cols[:, at], None, ALU.is_equal)
                    op.then_inc(h_lo, 1)
            dve.wait_ge(h_all, 1)
            nc.vector.tensor_scalar(n_has[0:GN, :], bank[6][0:GN, :], 1.0, None, ALU.min).then_inc(s_tmp, 1)
            dve.wait_ge(s_tmp, 2)
            nc.vector.tensor_tensor_scan(n_run[0:GN, :], ones[0:GN, 0:1].to_broadcast([GN, GROUP]), n_has[0:GN, :], 0.0, ALU.mult, ALU.add).then_inc(s_node, 1)
            dve.wait_ge(s_node, 2)
            nc.vector.tensor_copy(row_sum[0:GN, 1:2], n_run[0:GN, GROUP - 1:GROUP]).then_inc(s_node, 1)
            dve.wait_ge(s_noffP, 1)
            nc.vector.scalar_tensor_tensor(n_b[0:GN, :], n_run[0:GN, :], bank[0][0:GN, 1:2], n_has[0:GN, :], ALU.add, ALU.subtract).then_inc(s_num, 1)
            nc.vector.tensor_scalar(n_a[0:GN, :], count_i[0:GN, :], bank[0][0:GN, 2:3], group_col[0:GN, :], ALU.add, ALU.add).then_inc(s_num, 1)
            dve.wait_ge(s_num, 2)
            nc.vector.tensor_tensor(n_a[0:GN, :], n_a[0:GN, :], n_b[0:GN, :], ALU.subtract).then_inc(s_num, 1)
            dve.wait_ge(s_num, 3)
            nc.vector.tensor_tensor(n_b[0:GN, :], n_b[0:GN, :], n_a[0:GN, :], ALU.subtract).then_inc(s_num, 1)
            dve.wait_ge(s_num, 4)
            nc.vector.tensor_tensor(n_b[0:GN, :], n_b[0:GN, :], n_has[0:GN, :], ALU.mult).then_inc(s_num, 1)
            dve.wait_ge(s_num, 5)
            nc.vector.tensor_tensor(n_number[0:GN, :], n_a[0:GN, :], n_b[0:GN, :], ALU.add).then_inc(s_num, 1)
            dve.wait_ge(s_num, 6)
            nc.vector.tensor_copy(number_i[0:GN, :], n_number[0:GN, :]).then_inc(s_num, 1)
            dve.wait_ge(s_baser, DMA)
            nc.vector.tensor_copy(base_f, base_row[0:1, :]).then_inc(s_tmp, 1)
            dve.wait_ge(s_tmp, 3)
            base_g = base_f.rearrange("a (g t) -> a g t", t=TILES)
            nc.vector.tensor_tensor(off_row[0:1, :].rearrange("a (g t) -> a g t", t=TILES), base_g, base_g[:, :, 0:1].to_broadcast([1, GE, TILES]), ALU.subtract).then_inc(s_rows, 1)
            nc.vector.memset(step_row[0:1, 0:1], GROUP).then_inc(s_rows, 1)
            nc.vector.tensor_tensor(step_row[0:1, 1:GE], base_g[:, 1:GE, 0], base_g[:, 0:GE - 1, 0], ALU.subtract).then_inc(s_rows, 1)
            dve.wait_ge(s_rows, 3)
            nc.vector.memset(base_f, 0.0).then_inc(s_tmp, 1)
            dve.wait_ge(s_vT, 1)
            nc.vector.tensor_copy(vecs_all[:, :], bank[1][:, 0:L * VECS]).then_inc(s_vall, 1)
            dve.wait_ge(s_relP, 1)
            nc.vector.tensor_copy(rel_cols[:, :].rearrange("p (g t) -> p t g", t=TILES), bank[7][:, 0:NT].rearrange("p (t g) -> p t g", t=TILES)).then_inc(s_relc, 1)
            dve.wait_ge(s_numP, 1)
            nc.vector.tensor_copy(num_idx[:, :, :].rearrange("p g t -> p t g"), bank[1][:, 0:TILES * GN].rearrange("p (t g) -> p t g", t=TILES)).then_inc(s_numi, 1)
            dve.wait_ge(p_put[SLOTS - 1], (PAIRS_N - 1) * TILES * DMA)
            nc.vector.memset(x_rows[:, SLOTS - 1, :, :], 0.0).then_inc(p_clear, 1)
            dve.wait_ge(s_rela, DMA)
            dve.wait_ge(s_relc, 1)

            dve.wait_ge(s_gb, 2 * DMA)

            def layer(l, last=False):
                dve.wait_ge(s_wload, (l + 1) * (8 * DMA))
                dve.sem_inc(passed["dve"], 1)
                nc.vector.tensor_copy(vecs[:, :], vecs_all[:, bass.ds(l * VECS, VECS)]).then_inc(s_wmean, 1)
                for n, k in enumerate((EW3, NW3)):
                    nc.vector.reduce_sum(w3_mean[:, n:n + 1], W[:, k, :], AX.X).then_inc(s_wmean, 1)
                dve.wait_ge(s_wmean, l * 4 + 3)
                nc.vector.tensor_scalar(w3_mean[:, :], w3_mean[:, :], 1.0 / C, None, ALU.mult).then_inc(s_wmean, 1)
                dve.wait_ge(s_wmean, l * 4 + 4)
                nc.vector.tensor_scalar(W3c[:, 0, :], W[:, EW3, :], w3_mean[:, 0:1], None, ALU.subtract)
                nc.vector.tensor_scalar(W3c[:, 1, :], W[:, NW3, :], w3_mean[:, 1:2], None, ALU.subtract).then_inc(s_wts, 1)
                dve.wait_ge(s_wts, l + 1)
                dve.sem_inc(passed["dve"], 1)

                def edge(i, u):
                    return (l * PAIRS_E + i) * SLOTS + u

                def make_spread(i, u):
                    k = edge(i, u)
                    dve.wait_ge(e_dstP, free(k))
                    nc.vector.tensor_scalar(spread[:, u, :], rel_all[:, bass.ds((i * SLOTS + u) * GROUP, GROUP)], part_col[:, :], None, ALU.is_equal).then_inc(e_spread, 1)

                def make_collect(i, u):
                    k = edge(i, u)
                    dve.wait_ge(e_sumP, free(k))
                    at = rel_cols[:, bass.ds((i * SLOTS + u) * TILES, TILES)]
                    nc.vector.tensor_tensor(collect[:, u, :, :], count_f[:, None, :].to_broadcast([P, TILES, P]), at[:, :, None].to_broadcast([P, TILES, P]), ALU.is_equal).then_inc(e_coll, 1)

                def eh1_slope(i, u):
                    k = edge(i, u)
                    dve.wait_ge(e_h1b, done(k))
                    nc.vector.scalar_tensor_tensor(eh1[:, u, :], eh1[:, u, :], SLOPE, eh1[:, u, :], ALU.mult, ALU.max).then_inc(e_h1, 1)

                def eh2_slope(i, u):
                    k = edge(i, u)
                    dve.wait_ge(e_h2b, done(k))
                    nc.vector.scalar_tensor_tensor(eh2[:, u, :], eh2[:, u, :], SLOPE, eh2[:, u, :], ALU.mult, ALU.max).then_inc(e_h2, 1)

                def e_square_sum(i, u):
                    k = edge(i, u)
                    dve.wait_ge(e_sq, done(k))
                    dve.wait_ge(e_sd, free(k))
                    nc.vector.reduce_sum(ess[:, u, :], esq[:, u, :, :], AX.X).then_inc(e_ss, 1)

                def e_gained(i, u):
                    k = edge(i, u)
                    dve.wait_ge(e_sumP, free(k))
                    dve.wait_ge(e_sq, done(k))
                    nc.vector.tensor_tensor(msg[:, u, :, :], bank[B_H3 + u][:, :].rearrange("p (t c) -> p t c", t=TILES), msg_gain[:, None, :].to_broadcast([P, TILES, C]), ALU.mult).then_inc(e_gain, 1)

                def e_message(i, u):
                    k = edge(i, u)
                    dve.wait_ge(e_sd, done(k))
                    nc.vector.reciprocal(ers[:, u, :], ers[:, u, :]).then_inc(e_rs, 1)
                    dve.wait_ge(e_rs, done(k))
                    dve.wait_ge(e_gain, done(k))
                    for t in range(TILES):
                        op = nc.vector.scalar_tensor_tensor(msg[:, u, t, :], msg[:, u, t, :], ers[:, u, t:t + 1], msg_shift[:, :], ALU.mult, ALU.add)
                    op.then_inc(e_msg, 1)

                def carry(i, u):
                    k = edge(i, u)
                    step = dve.value_load(step_row[0:1, bass.ds(i * SLOTS + u, 1)], min_val=0, max_val=GROUP)
                    dve.wait_ge(e_sumc, done(k))
                    dve.wait_ge(e_sum, prev(k))
                    nc.vector.tensor_tensor(sums[:, u, 0:1], sums[:, u, 0:1], sums[:, 1 - u, bass.ds(step, 1)], ALU.add).then_inc(e_sum, 1)

                skewed(dve, GE, [(0, make_spread), (5, make_collect), (3, eh1_slope), (4, eh2_slope), (5, e_square_sum),
                                 (5, e_gained), (6, carry), (5, e_message)])

                def node(i, u):
                    return (l * PAIRS_N + i) * SLOTS + u

                def nh1_slope(i, u):
                    k = node(i, u)
                    dve.wait_ge(n_h1b, done(k))
                    nc.vector.scalar_tensor_tensor(nh1[:, u, :], nh1[:, u, :], SLOPE, nh1[:, u, :], ALU.mult, ALU.max).then_inc(n_h1, 1)

                def nh2_slope(i, u):
                    k = node(i, u)
                    dve.wait_ge(n_h2b, done(k))
                    nc.vector.scalar_tensor_tensor(nh2[:, u, :], nh2[:, u, :], SLOPE, nh2[:, u, :], ALU.mult, ALU.max).then_inc(n_h2, 1)

                def n_square_sum(i, u):
                    k = node(i, u)
                    dve.wait_ge(n_sq, done(k))
                    dve.wait_ge(n_sd, free(k))
                    nc.vector.reduce_sum(nss[:, u, :], nsq[:, u, :, :], AX.X).then_inc(n_ss, 1)

                def n_rows(i, u):
                    k = node(i, u)
                    dve.wait_ge(n_sd, done(k))
                    nc.vector.reciprocal(nrs[:, u, :], nrs[:, u, :]).then_inc(n_rs, 1)
                    dve.wait_ge(n_rs, done(k))
                    dve.wait_ge(s_st[u], over(l * PAIRS_N + i))
                    nc.vector.tensor_tensor(new_rows[:, u, :, :], bank[B_H3 + u][:, :].rearrange("p (t c) -> p t c", t=TILES),
                                            nrs[:, u, :, None].to_broadcast([P, TILES, C]), ALU.mult).then_inc(n_new, 1)

                def gained_rows(i, u):
                    k = node(i, u)
                    g = i * SLOTS + u
                    dve.wait_ge(n_sd, done(k))
                    nc.vector.reciprocal(nrs[:, u, :], nrs[:, u, :]).then_inc(n_rs, 1)
                    dve.wait_ge(n_rs, done(k))
                    dve.wait_ge(f_new, free(g))
                    for t in range(TILES):
                        op = nc.vector.scalar_tensor_tensor(src_rows[:, u, t, :], bank[B_H3 + u][:, t * P:(t + 1) * P], nrs[:, u, t:t + 1], out_gain[:, :], ALU.mult, ALU.mult)
                    op.then_inc(n_new, 1)

                def f_sum(i, u):
                    k = node(i, u)
                    g = i * SLOTS + u
                    dve.wait_ge(n_new, done(k))
                    dve.wait_ge(f_sh, done(g))
                    nc.vector.tensor_tensor(src_rows[:, u, :, :], src_rows[:, u, :, :], win_rows[:, u, :, :], ALU.add).then_inc(f_y, 1)
                    dve.wait_ge(f_y, done(g))
                    for t in range(TILES):
                        op = nc.vector.bn_stats(fstat[:, u, t, :], src_rows[:, u, t, :])
                    op.then_inc(f_bn, 1)
                    dve.wait_ge(f_bn, done(g))
                    dve.wait_ge(f_sd, free(g))
                    dve.sem_inc(passed["dve"], 1)
                    for t in range(TILES):
                        op = nc.vector.bn_aggr(fmv[:, u, t, :], fstat[:, u, t, :])
                    op.then_inc(f_mv, 1)

                def f_shifts(i, u):
                    g = i * SLOTS + u
                    dve.wait_ge(f_sd, done(g))
                    nc.vector.reciprocal(frs[:, u, :], frs[:, u, :]).then_inc(f_rs, 1)
                    dve.wait_ge(f_rs, done(g))
                    nc.vector.scalar_tensor_tensor(fshift[:, u, :], fmv[:, u, :, 0], -1.0, frs[:, u, :], ALU.mult, ALU.mult).then_inc(f_ms, 1)

                if last:
                    skewed(dve, GN, [(3, nh1_slope), (4, nh2_slope), (5, n_square_sum), (6, f_shifts), (5, gained_rows), (5, f_sum)])
                else:
                    skewed(dve, GN, [(3, nh1_slope), (4, nh2_slope), (5, n_square_sum), (5, n_rows)])

            with dve.Fori(0, L - 1) as l:
                layer(l)
            layer(L - 1, last=True)


_INS = ["x", "src", "dst"] + [f"L0_gnn_{n}" for n in ("eW1", "eb1", "eW2", "eb2", "eW3", "eg", "ebt", "nW1", "nb1", "nW2", "nb2", "nW3", "ng", "nbt")]


def kernel(**inputs):
    import numpy as np
    import concourse.bacc as bacc
    from concourse.bass_utils import run_bass_kernel_spmd

    nc = bacc.Bacc("TRN2", target_bir_lowering=False, num_devices=1)
    arrays, args = {}, []
    for name in _INS:
        a = np.ascontiguousarray(inputs[name])
        arrays[f"in_{name}"] = a
        args.append(nc.dram_tensor(f"in_{name}", a.shape, mybir.dt.from_np(a.dtype), kind="ExternalInput").ap())
    out = nc.dram_tensor("out_0", inputs["x"].shape, F32, kind="ExternalOutput").ap()
    gnn_kernel(nc, *args, out)
    r = run_bass_kernel_spmd(nc, [arrays], core_ids=[0])
    return r.results[0]["out_0"]
```
